# Optimizing a Trainium2 kernel written in Bass

```python
import numpy as np
import jax
import jax.numpy as jnp

def _softmax(x, axis=-1):
    return jax.nn.softmax(x, axis=axis)

def _gelu(x):
    return jax.nn.gelu(x, approximate=True)

def _silu(x):
    return jax.nn.silu(x)

def _sigmoid(x):
    return jax.nn.sigmoid(x)

def _layernorm(x, axis=-1, eps=1e-05):
    m = jnp.mean(x, axis=axis, keepdims=True)
    v = jnp.var(x, axis=axis, keepdims=True)
    return (x - m) / jnp.sqrt(v + eps)

def _scatter_add(tgt, idx, src, axis=0):
    return tgt.at[idx].add(src)

def _segment_sum(src, seg, n):
    return jax.ops.segment_sum(src, seg, n)
kernel_name = 'mk_flamingo_gated_d1_seqx_r4_1186a5'

def setup_inputs(seed: int=0):
    np.random.seed(seed)
    _w = jnp.asarray

    def _rec_inputs():
        import jax
        import jax.numpy as jnp
        _rk = jax.random.key(seed)
        x = -0.000125 + 0.9999 * jax.random.normal(jax.random.fold_in(_rk, 1), (32, 256, 256), jnp.float32)
        _lenS = 256 - jax.random.randint(jax.random.fold_in(_rk, 7), (32,), 0, max(1, 256 // 4) + 1, jnp.int32)
        _lenS2 = 77 - jax.random.randint(jax.random.fold_in(_rk, 8), (32,), 0, max(1, 77 // 4) + 1, jnp.int32)
        _ctx_2048P = jax.random.normal(jax.random.fold_in(_rk, 11), (32, 16, 512), jnp.float32)
        _ctx_2048c = jax.random.dirichlet(jax.random.fold_in(_rk, 511), 0.3 * jnp.ones((16,), jnp.float32), (32, 77))
        _ctx_2048t = jnp.einsum('bsk,bkd->bsd', _ctx_2048c, _ctx_2048P)
        _ctx_2048t = _ctx_2048t * jax.lax.rsqrt(jnp.mean(jnp.square(_ctx_2048t)) + 1e-12) * 0.953939
        ctx_2048 = -1.39393e-06 + 0.999914 * (_ctx_2048t + 0.3 * jax.random.normal(jax.random.fold_in(_rk, 611), (32, 77, 512), jnp.float32))
        _g = jax.random.normal(jax.random.fold_in(_rk, 9001), (2, 1), jnp.float32)
        _g = jnp.sign(_g) * jnp.maximum(jnp.abs(_g), 1.0) + (_g == 0) * 1.0
        g_xattn = _g[0]
        g_ffn = _g[1]
        return (x, ctx_2048, g_xattn, g_ffn)
    x, ctx_2048, g_xattn, g_ffn = _rec_inputs()

    def _L0_xattn_setup():
        import jax, jax.numpy as jnp
        import numpy as np
        B, N, DIM = (8, 1024, 256)
        M, CTX = (64, 512)
        HEADS, DH = (16, 64)
        INNER = HEADS * DH
        EPS = 1e-06

        def _split_heads(t):
            b, n, _ = t.shape
            return t.reshape(b, n, HEADS, DH).transpose(0, 2, 1, 3)
        key = jax.random.key(seed)
        ks = jax.random.split(key, 6)
        x = jax.random.normal(ks[0], (B, N, DIM), dtype=jnp.float32)
        context = jax.random.normal(ks[1], (B, M, CTX), dtype=jnp.float32)
        Wq = jax.random.normal(ks[2], (DIM, INNER), dtype=jnp.float32) / np.sqrt(DIM)
        Wkv = jax.random.normal(ks[3], (CTX, 2 * INNER), dtype=jnp.float32) / np.sqrt(CTX)
        null_kv = jax.random.normal(ks[4], (2, DH), dtype=jnp.float32) / np.sqrt(2.0)
        Wout = jax.random.normal(ks[5], (INNER, DIM), dtype=jnp.float32) / np.sqrt(INNER)
        ln_scale = jnp.ones((DIM,), dtype=jnp.float32)
        ln_bias = jnp.zeros((DIM,), dtype=jnp.float32)
        return {'x': x, 'context': context, 'Wq': Wq, 'Wkv': Wkv, 'null_kv': null_kv, 'Wout': Wout, 'ln_scale': ln_scale, 'ln_bias': ln_bias}
    _L0_xattn_all = _L0_xattn_setup()
    _L0_xattn_in = {k: v for k, v in _L0_xattn_all.items() if k in ('Wq', 'Wkv', 'null_kv', 'Wout', 'ln_scale', 'ln_bias')}
    del _L0_xattn_all

    def _L0_ffn_setup():
        import jax, jax.numpy as jnp
        import numpy as np
        H, I, E, K = (256, 128, 32, 8)
        B, S = (4, 256)

        def silu(x):
            return x * jax.nn.sigmoid(x)
        key = jax.random.key(seed)
        ks = jax.random.split(key, 14)

        def w(k, shape, fan_in):
            return jax.random.normal(k, shape, jnp.float32) / np.float32(np.sqrt(fan_in))
        return {'hidden_states': jax.random.normal(ks[0], (B, S, H), jnp.float32), 'Wr': w(ks[1], (H, E), H), 'br': jnp.zeros((E,), jnp.float32), 'Wg_s': w(ks[2], (H, I), H), 'bg_s': jnp.zeros((I,), jnp.float32), 'Wu_s': w(ks[3], (H, I), H), 'bu_s': jnp.zeros((I,), jnp.float32), 'Wd_s': w(ks[4], (I, H), I), 'bd_s': jnp.zeros((H,), jnp.float32), 'Wg': w(ks[5], (E, H, I), H), 'bg': jnp.zeros((E, I), jnp.float32), 'Wu': w(ks[6], (E, H, I), H), 'bu': jnp.zeros((E, I), jnp.float32), 'Wd': w(ks[7], (E, I, H), I), 'bd': jnp.zeros((E, H), jnp.float32)}
    _L0_ffn_all = _L0_ffn_setup()
    _L0_ffn_in = {k: v for k, v in _L0_ffn_all.items() if k in ('Wr', 'br', 'Wg_s', 'bg_s', 'Wu_s', 'bu_s', 'Wd_s', 'bd_s', 'Wg', 'bg', 'Wu', 'bu', 'Wd', 'bd')}
    del _L0_ffn_all
    return {'x': x, 'ctx_2048': ctx_2048, 'g_xattn': g_xattn, 'g_ffn': g_ffn, 'L0_xattn_Wq': _L0_xattn_in['Wq'], 'L0_xattn_Wkv': _L0_xattn_in['Wkv'], 'L0_xattn_null_kv': _L0_xattn_in['null_kv'], 'L0_xattn_Wout': _L0_xattn_in['Wout'], 'L0_xattn_ln_scale': _L0_xattn_in['ln_scale'], 'L0_xattn_ln_bias': _L0_xattn_in['ln_bias'], 'L0_ffn_Wr': _L0_ffn_in['Wr'], 'L0_ffn_br': _L0_ffn_in['br'], 'L0_ffn_Wg_s': _L0_ffn_in['Wg_s'], 'L0_ffn_bg_s': _L0_ffn_in['bg_s'], 'L0_ffn_Wu_s': _L0_ffn_in['Wu_s'], 'L0_ffn_bu_s': _L0_ffn_in['bu_s'], 'L0_ffn_Wd_s': _L0_ffn_in['Wd_s'], 'L0_ffn_bd_s': _L0_ffn_in['bd_s'], 'L0_ffn_Wg': _L0_ffn_in['Wg'], 'L0_ffn_bg': _L0_ffn_in['bg'], 'L0_ffn_Wu': _L0_ffn_in['Wu'], 'L0_ffn_bu': _L0_ffn_in['bu'], 'L0_ffn_Wd': _L0_ffn_in['Wd'], 'L0_ffn_bd': _L0_ffn_in['bd']}

def reference(x, ctx_2048, g_xattn, g_ffn, L0_xattn_Wq, L0_xattn_Wkv, L0_xattn_null_kv, L0_xattn_Wout, L0_xattn_ln_scale, L0_xattn_ln_bias, L0_ffn_Wr, L0_ffn_br, L0_ffn_Wg_s, L0_ffn_bg_s, L0_ffn_Wu_s, L0_ffn_bu_s, L0_ffn_Wd_s, L0_ffn_bd_s, L0_ffn_Wg, L0_ffn_bg, L0_ffn_Wu, L0_ffn_bu, L0_ffn_Wd, L0_ffn_bd):
    import jax
    import jax.numpy as jnp

    def _L0_xattn_ref(x, context, Wq, Wkv, null_kv, Wout, ln_scale, ln_bias):
        import jax, jax.numpy as jnp
        import numpy as np
        B, N, DIM = (8, 1024, 256)
        M, CTX = (64, 512)
        HEADS, DH = (16, 64)
        INNER = HEADS * DH
        EPS = 1e-06

        def _split_heads(t):
            b, n, _ = t.shape
            return t.reshape(b, n, HEADS, DH).transpose(0, 2, 1, 3)
        scale = DH ** (-0.5)
        b = x.shape[0]
        q = _split_heads(jnp.einsum('bnd,df->bnf', x, Wq))
        kv = jnp.einsum('bmc,cf->bmf', context, Wkv)
        k, v = jnp.split(kv, 2, axis=-1)
        k, v = (_split_heads(k), _split_heads(v))
        nk = jnp.broadcast_to(null_kv[0], (b, HEADS, 1, DH))
        nv = jnp.broadcast_to(null_kv[1], (b, HEADS, 1, DH))
        k = jnp.concatenate((nk, k), axis=-2)
        v = jnp.concatenate((nv, v), axis=-2)
        q = q * scale
        sim = jnp.einsum('bhid,bhjd->bhij', q, k)
        attn = jax.nn.softmax(sim, axis=-1)
        out = jnp.einsum('bhij,bhjd->bhid', attn, v)
        out = out.transpose(0, 2, 1, 3).reshape(b, -1, INNER)
        out = jnp.einsum('bnf,fd->bnd', out, Wout)
        mu = jnp.mean(out, axis=-1, keepdims=True)
        var = jnp.var(out, axis=-1, keepdims=True)
        out = (out - mu) * jax.lax.rsqrt(var + EPS) * ln_scale + ln_bias
        return out

    def _L0_ffn_ref(hidden_states, Wr, br, Wg_s, bg_s, Wu_s, bu_s, Wd_s, bd_s, Wg, bg, Wu, bu, Wd, bd):
        import jax, jax.numpy as jnp
        import numpy as np
        H, I, E, K = (256, 128, 32, 8)
        B, S = (4, 256)

        def silu(x):
            return x * jax.nn.sigmoid(x)
        b, s, h = hidden_states.shape
        T = b * s
        x = hidden_states.reshape(T, h)
        logits = jnp.dot(x.astype(jnp.float32), Wr) + br
        aff = jax.nn.sigmoid(logits)
        top_v, top_i = jax.lax.top_k(aff, K)
        top_w = top_v / (jnp.sum(top_v, axis=-1, keepdims=True) + 1e-09)
        top_w = top_w.astype(hidden_states.dtype)
        e_total = Wr.shape[1]
        w_full = jnp.zeros((T, e_total), hidden_states.dtype)
        w_full = w_full.at[jnp.arange(T)[:, None], top_i].set(top_w)
        shared = jnp.dot(silu(jnp.dot(x, Wg_s) + bg_s) * (jnp.dot(x, Wu_s) + bu_s), Wd_s) + bd_s
        gate = silu(jnp.einsum('th,ehi->eti', x, Wg) + bg[:, None, :])
        up = jnp.einsum('th,ehi->eti', x, Wu) + bu[:, None, :]
        down = jnp.einsum('eti,eih->eth', gate * up, Wd) + bd[:, None, :]
        routed = jnp.einsum('te,eth->th', w_full, down)
        return (shared + routed).reshape(b, s, h)
    x = x + jnp.tanh(g_xattn[0]) * _L0_xattn_ref(_layernorm(x, axis=-1), ctx_2048, L0_xattn_Wq, L0_xattn_Wkv, L0_xattn_null_kv, L0_xattn_Wout, L0_xattn_ln_scale, L0_xattn_ln_bias)
    x = x + jnp.tanh(g_ffn[0]) * _L0_ffn_ref(_layernorm(x, axis=-1), L0_ffn_Wr, L0_ffn_br, L0_ffn_Wg_s, L0_ffn_bg_s, L0_ffn_Wu_s, L0_ffn_bu_s, L0_ffn_Wd_s, L0_ffn_bd_s, L0_ffn_Wg, L0_ffn_bg, L0_ffn_Wu, L0_ffn_bu, L0_ffn_Wd, L0_ffn_bd)
    return x

_drawn_inputs = setup_inputs


def setup_inputs(seed=0):
    import zlib

    import numpy as np

    out = dict(_drawn_inputs(seed))
    spreads = {'L0_xattn_ln_scale': (1.0, 0.2),
     'L0_xattn_ln_bias': (0.0, 0.1),
     'L0_ffn_br': (0.0, 0.1),
     'L0_ffn_bg_s': (0.0, 0.1),
     'L0_ffn_bu_s': (0.0, 0.1),
     'L0_ffn_bd_s': (0.0, 0.1),
     'L0_ffn_bg': (0.0, 0.555),
     'L0_ffn_bu': (0.0, 0.566),
     'L0_ffn_bd': (0.0, 0.338)}
    factors = {}
    for name, (base, spread) in spreads.items():
        noise = np.random.default_rng([zlib.crc32(name.encode()), seed]).standard_normal(out[name].shape)
        drawn = base * np.exp(spread * noise) if base else spread * noise
        out[name] = jnp.asarray(drawn.astype(out[name].dtype))
    for name, factor in factors.items():
        out[name] = (out[name] * factor).astype(out[name].dtype)
    return out
```

```python
from contextlib import ExitStack

import concourse.bass as bass
from concourse import mybir

F32 = mybir.dt.float32
F32R = mybir.dt.float32r
ACT = mybir.ActivationFunctionType
ALU = mybir.AluOpType
AX = mybir.AxisListType

P = 128
B, N, D = 32, 256, 256
M, CTX = 77, 512
J = M + 1
HEADS, DH = 16, 64
INNER = HEADS * DH
PAIRS = HEADS // 2
HP = PAIRS // 2
TT = N // P
DC, CC = D // P, CTX // P
T = B * N
SCALE = DH ** -0.5
LN_EPS, OUT_EPS = 1e-5, 1e-6
ROUTED, TOPK = 32, 8
I = 128
GT = 1024
BLK = 512
NB = GT // BLK
GTILES = GT // P
SLOTS = 4
EW = 2 * DC * I + D
STEPS = NB * (ROUTED + 1)
SPLIT_AHEAD = 2
LOWEST = -3.0e38

RING = ["O", "X", "C", "T0a", "T0b", "K0", "T1a", "T1b", "Q0", "Q1", "PV0a", "PV0b", "K1",
        "T2a", "T2b", "Q2", "T3a", "T3b", "Q3", "N2", "V0", "PV1a", "PV1b", "V1"]
NBANK = 4
HI = [n for n in RING if n != "O"]
LO = [n for n in RING if n not in ("O", "N2")]


def runs(name, b):
    if not isinstance(b, int):
        return True
    if name in ("O", "N2"):
        return 1 <= b <= B
    return 0 <= b < B if name[0] in "TP" else -1 <= b < B - 1


def nth(names, name, b):
    return (b + 1) * len(names) + (names.index(name) + 1)


def split_product(eng, out, left, right, start=True, stop=True):
    eng.matmul(out, left[0], right[0], start=start, stop=False)
    eng.matmul(out, left[1], right[0], start=False, stop=False)
    return eng.matmul(out, left[0], right[1], start=False, stop=stop)


def iterations(eng, step):
    for b in (-2, -1, 0, 1):
        step(b)
    with eng.Fori(2, B - 2) as b:
        step(b)
    for b in (B - 2, B - 1, B):
        step(b)


def within(b, first, last):
    return first <= b <= last if isinstance(b, int) else True


def attention_phase(nc, ctx, dram):
    def sb(name, shape, dt=F32, where=ctx):
        return where.enter_context(nc.sbuf_tensor(name, shape, dt))

    def sem(name):
        return ctx.enter_context(nc.semaphore(name))

    wq = [sb(f"wq_{s}", [P, DC, INNER], F32R) for s in "hl"]
    wkv = [sb(f"wkv_{s}", [P, CC, 2 * INNER], F32R) for s in "hl"]
    wo = [sb(f"wo_{s}", [P, PAIRS, D], F32R) for s in "hl"]
    ident = sb("ident", [P, P])
    scale_row = sb("scale_row", [P, D])
    bias_row = sb("bias_row", [P, D])
    gate = sb("gate", [P, 2])
    minus_half = sb("minus_half", [P, TT])
    eps_col = [sb(f"eps_col{i}", [P, TT]) for i in range(3)]
    null_k = sb("null_k", [P, 1])
    null_v = sb("null_v", [1, DH])
    null_v8 = [sb(f"null_v8_{s}", [1, PAIRS, DH], F32R) for s in "hl"]
    x_in = sb("x_in", [P, TT, D])
    x_res = sb("x_res", [P, TT, D])
    ctx_in = sb("ctx_in", [M, CTX])
    xn = sb("xn", [P, TT, D])
    xnT = [sb(f"xnT_{s}", [P, DC, N], F32R) for s in "hl"]
    ctxT = [sb(f"ctxT_{s}", [P, CC, J], F32R) for s in "hl"]
    kT = [sb(f"kT_{s}", [P, PAIRS, 2 * J], F32R) for s in "hl"]
    vv = [sb(f"v_{s}", [J, PAIRS, 3 * DH], F32R) for s in "hl"]
    qT = [sb(f"qT_{s}", [P, PAIRS, N], F32R) for s in "hl"]
    outT = [sb(f"outT_{s}", [P, PAIRS, N], F32R) for s in "hl"]
    probs = [sb(f"probs{i}", [P, PAIRS, J]) for i in range(2)]
    row_max = [sb(f"row_max{i}", [P, PAIRS]) for i in range(2)]
    row_sum = [sb(f"row_sum{i}", [P, PAIRS]) for i in range(2)]
    row_inv = [sb(f"row_inv{i}", [P, PAIRS]) for i in range(2)]
    stats = [sb(f"stats{i}", [P, TT, 6]) for i in range(3)]
    mean_var = [sb(f"mean_var{i}", [P, TT, 2]) for i in range(3)]
    var_eps = [sb(f"var_eps{i}", [P, TT]) for i in range(3)]
    rstd = [sb(f"rstd{i}", [P, TT]) for i in range(3)]
    z = sb("z", [P, TT, D])
    x1 = sb("x1", [P, TT, D])
    xn2 = sb("xn2", [P, TT, D])
    x2T = sb("x2T", [P, DC, N])
    with ExitStack() as early:
        stage = [sb(f"stage{i}", [P, 2048], where=early) for i in range(2)]
    pT = [sb(f"pT_{s}", [J, PAIRS, N], F32R) for s in "hl"]

    sim = [ctx.enter_context(nc.psum_tensor(f"sim{i}", [P, 2, 512], F32)) for i in range(2)]
    ring = [ctx.enter_context(nc.psum_tensor(f"ring{i}", [P, 512], F32)) for i in range(NBANK)]

    w_loaded = [sem(f"w_loaded{i}") for i in range(2)]
    w_hi, w_lo = sem("w_hi"), sem("w_lo")
    const_loaded, zeroed, made = sem("const_loaded"), sem("zeroed"), sem("made")
    null_hi, null_lo, null_placed = sem("null_hi"), sem("null_lo"), sem("null_placed")
    gate_ready, rows_ready = sem("gate_ready"), sem("rows_ready")
    x_loaded, ctx_loaded, res_loaded = sem("x_loaded"), sem("ctx_loaded"), sem("res_loaded")
    x1_stored, x2_stored = sem("x1_stored"), sem("x2_stored")
    ring_full, ring_hi, ring_lo = sem("ring_full"), sem("ring_hi"), sem("ring_lo")
    sim_full, max_done, centred, exp_done = sem("sim_full"), sem("max_done"), sem("centred"), sem("exp_done")
    sum_done, inv_done, probs_ready = sem("sum_done"), sem("inv_done"), sem("probs_ready")
    stats_done = [sem(f"stats_done{i}") for i in range(3)]
    var_done = [sem(f"var_done{i}") for i in range(3)]
    eps_done = [sem(f"eps_done{i}") for i in range(3)]
    rstd_done = [sem(f"rstd_done{i}") for i in range(3)]
    applied = [sem(f"applied{i}") for i in range(3)]
    scaled, shifted, summed = sem("scaled"), sem("shifted"), sem("summed")

    pieces = [(dram["Wq"].rearrange("(c p) n -> p c n", p=P), [w[:, :, :] for w in wq], SCALE)]
    for c in range(CC):
        pieces.append((dram["Wkv"][c * P:(c + 1) * P, :], [w[:, c, :] for w in wkv], 1.0))
    pieces.append((dram["Wout"].rearrange("(c p) n -> p c n", p=P), [w[:, :, :] for w in wo], 1.0))

    def staged(i):
        shape = pieces[i][1][0].shape
        s = stage[i % 2][:, :]
        return s.rearrange("p (c n) -> p c n", c=shape[1]) if len(shape) == 3 else s

    x_tiles = dram["x"].rearrange("b (t p) d -> b p t d", p=P)
    x1_tiles = dram["x1"].rearrange("(b t p) d -> b p t d", t=TT, p=P)
    x2_cols = dram["x2T"].rearrange("c p n -> p c n")

    def bank(name):
        return ring[RING.index(name) % NBANK]

    def scores(u):
        return sim[u % 2][:, :, 0:4 * J].rearrange("p a (h j) -> p a h j", j=J)

    def by_bank(ap):
        return ap.rearrange("p (a h) j -> p a h j", a=2)

    def destinations(name):
        ps, half = bank(name), int(name[-1]) if name[-1] in "01" else 0
        if name == "X":
            return [(ps[:, :].rearrange("p (c n) -> p c n", c=DC), [t[:, :, :] for t in xnT])]
        if name == "C":
            return [(ps[:, 0:CC * J].rearrange("p (c j) -> p c j", c=CC)[:, :, 0:M], [t[:, :, 0:M] for t in ctxT])]
        if name[0] == "T":
            tt, first = int(name[1]) % 2, 4 * "ab".index(name[2])
            return [(ps[0:J, :].rearrange("p (h n) -> p h n", h=4),
                     [t[:, first:first + 4, tt * P:(tt + 1) * P] for t in pT])]
        if name[0] == "K":
            src = ps[:, 0:HP * J].rearrange("p (h j) -> p h j", h=HP)[:, :, 0:M]
            pairs = slice(half * HP, (half + 1) * HP)
            return [(src[0:DH], [t[0:DH, pairs, 0:M] for t in kT]),
                    (src[DH:P], [t[DH:P, pairs, J:J + M] for t in kT])]
        if name[0] == "Q":
            q = 2 * int(name[1])
            return [(ps[:, :].rearrange("p (h n) -> p h n", h=2), [t[:, q:q + 2, :] for t in qT])]
        if name[0] == "V":
            pairs = slice(half * HP, (half + 1) * HP)
            return [(ps[0:M, :].rearrange("p (h s d) -> p h s d", s=2, d=DH),
                     [t[0:M, pairs, :].rearrange("p h (s d) -> p h s d", d=DH)[:, :, 0:3:2, :] for t in vv])]
        q = HP * int(name[2]) + 2 * "ab".index(name[3])
        return [(ps[:, :].rearrange("p (h n) -> p h n", h=2), [t[:, q:q + 2, :] for t in outT])]

    def counted(names, semaphore):
        left_out = [0]

        def skip():
            left_out[0] += 1

        def signal(instruction):
            instruction.then_inc(semaphore, 1 + left_out[0])
            left_out[0] = 0
        return skip, signal

    with nc.Block() as block:
        @block.sync
        def _(sp):
            for i in range(len(pieces)):
                if i >= 2:
                    sp.wait_ge(w_lo, i - 1)
                sp.dma_start(staged(i), pieces[i][0]).then_inc(w_loaded[i % 2], 16)
                if i == 0:
                    sp.dma_start(x_in[:, :, :], x_tiles[0]).then_inc(x_loaded, 16)
                    sp.dma_start(ctx_in[:, :], dram["ctx"][0]).then_inc(ctx_loaded, 16)
            sp.wait_ge(null_lo, 2)
            sp.wait_ge(zeroed, 1)
            for s in range(2):
                for col in (0, 2 * DH):
                    sp.dma_start(vv[s][M:J, :, col:col + DH].bitcast(F32),
                                 null_v8[s][:, :, :].bitcast(F32)).then_inc(null_placed, 16)

            def step(b):
                if within(b, -1, B - 3):
                    sp.wait_ge(applied[0], b + 2)
                    sp.dma_start(x_in[:, :, :], x_tiles[b + 2]).then_inc(x_loaded, 16)
                    sp.wait_ge(ring_full, nth(RING, "C", b))
                    sp.dma_start(ctx_in[:, :], dram["ctx"][b + 2]).then_inc(ctx_loaded, 16)
                if within(b, 1, B):
                    sp.wait_ge(summed, b)
                    sp.dma_start(x1_tiles[b - 1], x1[:, :, :]).then_inc(x1_stored, 16)
                if within(b, 0, B - 1):
                    sp.dma_start(x_res[:, :, :], x_tiles[b]).then_inc(res_loaded, 16)
                if within(b, 1, B):
                    sp.wait_ge(ring_hi, nth(HI, "N2", b))
                    sp.dma_start(x2_cols[:, :, bass.ds((b - 1) * N, N)], x2T[:, :, :]).then_inc(x2_stored, 16)

            iterations(sp, step)
            sp.wait_ge(x1_stored, 16 * B)
            sp.wait_ge(x2_stored, 16 * B)

        @block.gpsimd
        def _(pool):
            pool.memset(ident[:, :], 0.0).then_inc(made, 1)
            pool.memset(minus_half[:, :], -0.5).then_inc(made, 1)
            for i, eps in enumerate((LN_EPS, OUT_EPS, LN_EPS)):
                pool.memset(eps_col[i][:, :], eps).then_inc(made, 1)
            pool.wait_ge(made, 5)
            pool.affine_select(out=ident[:, :], in_=ident[:, :], compare_op=ALU.not_equal, fill=1.0, base=0,
                               pattern=[[-1, P]], channel_multiplier=1).then_inc(made, 1)
            with nc.allow_non_contiguous_dma(reason="one column of 64 elements"):
                for half in (slice(0, DH), slice(DH, P)):
                    pool.dma_start(null_k[half, :], dram["null_kv"][0:1, :].rearrange("a d -> d a")).then_inc(const_loaded, 16)
            pool.dma_start(null_v[:, :], dram["null_kv"][1:2, :]).then_inc(const_loaded, 16)
            pool.dma_start(gate[:, 0:1], dram["g_xattn"].unsqueeze(0).broadcast_to([P, 1])).then_inc(const_loaded, 16)
            pool.dma_start(scale_row[:, :], dram["ln_scale"].unsqueeze(0).broadcast_to([P, D])).then_inc(const_loaded, 16)
            pool.dma_start(bias_row[:, :], dram["ln_bias"].unsqueeze(0).broadcast_to([P, D])).then_inc(const_loaded, 16)

            def make_rstd(i, batch):
                pool.wait_ge(var_done[i], batch + 1)
                pool.tensor_tensor(var_eps[i][:, :], mean_var[i][:, :, 1], eps_col[i][:, :], ALU.add).then_inc(eps_done[i], 1)
                pool.wait_ge(eps_done[i], batch + 1)
                pool.tensor_tensor(rstd[i][:, :], var_eps[i][:, :], minus_half[:, :], ALU.pow).then_inc(rstd_done[i], 1)

            def normalise(u, b):
                pool.wait_ge(inv_done, 4 * b + u + 1)
                e = probs[u % 2]
                pool.tensor_tensor(e[:, :, :], e[:, :, :], row_inv[u % 2][:, :].unsqueeze(2).broadcast_to([P, PAIRS, J]),
                                   ALU.mult).then_inc(probs_ready, 1)

            def step(b):
                if within(b, 0, B - 1):
                    normalise(0, b)
                    normalise(1, b)
                if within(b, 1, B):
                    make_rstd(1, b - 1)
                    pool.wait_ge(res_loaded, 16 * b)
                    if isinstance(b, int) and b == 1:
                        pool.wait_ge(rows_ready, 2)
                    if within(b, 2, B):
                        pool.wait_ge(x1_stored, 16 * (b - 1))
                        pool.wait_ge(applied[2], b - 1)
                    pool.tensor_tensor(x1[:, :, :], x_res[:, :, :], bias_row[:, :].unsqueeze(1).broadcast_to([P, TT, D]),
                                       ALU.add).then_inc(shifted, 1)
                    pool.wait_ge(applied[1], b)
                    pool.tensor_tensor(z[:, :, :], z[:, :, :], scale_row[:, :].unsqueeze(1).broadcast_to([P, TT, D]),
                                       ALU.mult).then_inc(scaled, 1)
                    pool.wait_ge(scaled, b)
                    pool.wait_ge(shifted, b)
                    pool.tensor_tensor(x1[:, :, :], x1[:, :, :], z[:, :, :], ALU.add).then_inc(summed, 1)
                if within(b, 0, B - 1):
                    normalise(2, b)
                if within(b, 1, B):
                    make_rstd(2, b - 1)
                if within(b, 0, B - 1):
                    normalise(3, b)
                if within(b, -2, B - 3):
                    if within(b, -2, -2):
                        pool.wait_ge(made, 6)
                    make_rstd(0, b + 2)

            iterations(pool, step)

        @block.scalar
        def _(act):
            skip, signal = counted(HI, ring_hi)

            act.wait_ge(const_loaded, 96)
            act.activation(gate[:, 1:2], gate[:, 0:1], ACT.Tanh).then_inc(gate_ready, 1)
            act.wait_ge(zeroed, 1)
            act.activation(kT[0][0:DH, :, M], null_k[0:DH, 0:1].broadcast_to([DH, PAIRS]), ACT.Copy).then_inc(null_hi, 1)
            act.activation(kT[0][DH:P, :, J + M], null_k[DH:P, 0:1].broadcast_to([DH, PAIRS]), ACT.Copy).then_inc(null_hi, 1)
            act.activation(null_v8[0][:, :, :], null_v[:, :].unsqueeze(1).broadcast_to([1, PAIRS, DH]), ACT.Copy).then_inc(null_hi, 1)
            for i, (_, dst, factor) in enumerate(pieces):
                act.wait_ge(w_loaded[i % 2], 16 * (i // 2 + 1))
                act.activation(dst[0], staged(i), ACT.Copy, scale=factor).then_inc(w_hi, 1)

            def exp(u, b):
                act.wait_ge(centred, 4 * b + u + 1)
                act.activation(probs[u % 2][:, :, :], probs[u % 2][:, :, :], ACT.Exp).then_inc(exp_done, 1)

            def high(name, b):
                if not runs(name, b):
                    return skip()
                act.wait_ge(ring_full, nth(RING, name, b))
                if name == "N2":
                    if within(b, 2, B):
                        act.wait_ge(x2_stored, 16 * (b - 1))
                    last = act.activation(x2T[:, :, :], bank(name)[:, :].rearrange("p (c n) -> p c n", c=DC), ACT.Copy)
                else:
                    for src, dst in destinations(name):
                        last = act.activation(dst[0], src, ACT.Copy)
                signal(last)

            def step(b):
                if within(b, 0, B - 1):
                    exp(0, b)
                    exp(1, b)
                for name in HI:
                    if within(b, -1, B):
                        high(name, b)
                    if name == "T1b" and within(b, 0, B - 1):
                        exp(2, b)
                        exp(3, b)

            iterations(act, step)

        @block.vector
        def _(dve):
            skip, signal = counted(LO, ring_lo)

            for t in (*kT, *vv):
                dve.memset(t[:, :, :].bitcast(F32), 0.0)
            for t in ctxT:
                last = dve.memset(t[:, :, M:J].bitcast(F32), 0.0)
            last.then_inc(zeroed, 1)
            dve.wait_ge(gate_ready, 1)
            for row in (scale_row, bias_row):
                dve.tensor_scalar(row[:, :], row[:, :], gate[:, 1:2], None, ALU.mult).then_inc(rows_ready, 1)
            dve.wait_ge(null_hi, 3)
            dve.tensor_tensor(kT[1][0:DH, :, M], null_k[0:DH, 0:1].broadcast_to([DH, PAIRS]),
                              kT[0][0:DH, :, M].bitcast(F32), ALU.subtract)
            dve.tensor_tensor(kT[1][DH:P, :, J + M], null_k[DH:P, 0:1].broadcast_to([DH, PAIRS]),
                              kT[0][DH:P, :, J + M].bitcast(F32), ALU.subtract).then_inc(null_lo, 1)
            dve.tensor_tensor(null_v8[1][:, :, :], null_v[:, :].unsqueeze(1).broadcast_to([1, PAIRS, DH]),
                              null_v8[0][:, :, :].bitcast(F32), ALU.subtract).then_inc(null_lo, 1)
            for i, (_, dst, factor) in enumerate(pieces):
                dve.wait_ge(w_hi, i + 1)
                dve.scalar_tensor_tensor(out=dst[1], in0=staged(i), scalar=factor, in1=dst[0].bitcast(F32),
                                         op0=ALU.mult, op1=ALU.subtract).then_inc(w_lo, 1)

            def centre(u, b):
                n = 4 * b + u
                dve.wait_ge(sim_full, n + 1)
                if within(b, 1, B) or u >= 2:
                    dve.wait_ge(centred, n - 1)
                dve.tensor_reduce(row_max[u % 2][:, :].rearrange("p (a h) -> p a h", a=2), scores(u), AX.X,
                                  ALU.max).then_inc(max_done, 1)
                dve.wait_ge(max_done, n + 1)
                if u >= 2:
                    dve.wait_ge(ring_full, nth(RING, f"T{u - 2}b", b))
                elif within(b, 1, B):
                    dve.wait_ge(ring_full, nth(RING, f"T{u + 2}b", b - 1))
                dve.tensor_tensor(by_bank(probs[u % 2][:, :, :]), scores(u),
                                  by_bank(row_max[u % 2][:, :].unsqueeze(2).broadcast_to([P, PAIRS, J])),
                                  ALU.subtract).then_inc(centred, 1)

            def total(u, b):
                n = 4 * b + u
                dve.wait_ge(exp_done, n + 1)
                if within(b, 1, B) or u >= 2:
                    dve.wait_ge(probs_ready, n - 1)
                dve.tensor_reduce(row_sum[u % 2][:, :], probs[u % 2][:, :, :], AX.X, ALU.add).then_inc(sum_done, 1)
                dve.wait_ge(sum_done, n + 1)
                dve.reciprocal(row_inv[u % 2][:, :], row_sum[u % 2][:, :]).then_inc(inv_done, 1)

            def statistics(i, src, batch, first):
                if not first:
                    dve.wait_ge(applied[i], batch)
                for t in range(TT):
                    last = dve.bn_stats(stats[i][:, t, :], src(t))
                last.then_inc(stats_done[i], 1)
                dve.wait_ge(zeroed, 1)
                dve.wait_ge(stats_done[i], batch + 1)
                for t in range(TT):
                    last = dve.bn_aggr(mean_var[i][:, t, :], stats[i][:, t, :])
                last.then_inc(var_done[i], 1)

            def apply(i, out, src, batch):
                dve.wait_ge(rstd_done[i], batch + 1)
                for t in range(TT):
                    last = dve.tensor_scalar(out[:, t, :], src(t), mean_var[i][:, t, 0:1], rstd[i][:, t:t + 1],
                                             ALU.subtract, ALU.mult)
                return last.then_inc(applied[i], 1)

            def from_o(t):
                return bank("O")[:, t * D:(t + 1) * D]

            def low(name, b):
                if not runs(name, b):
                    return skip()
                dve.wait_ge(ring_hi, nth(HI, name, b))
                for src, dst in destinations(name):
                    last = dve.tensor_tensor(dst[1], src, dst[0].bitcast(F32), ALU.subtract)
                signal(last)

            def step(b):
                here = within(b, 0, B - 1)
                if here:
                    centre(0, b)
                    centre(1, b)
                    total(0, b)
                    total(1, b)
                if within(b, 1, B):
                    dve.wait_ge(ring_full, nth(RING, "O", b))
                    statistics(1, from_o, b - 1, isinstance(b, int) and b == 1)
                for name in LO:
                    if within(b, -1, B):
                        low(name, b)
                    if name == "C" and within(b, 1, B):
                        if within(b, 2, B):
                            dve.wait_ge(summed, b - 1)
                        apply(1, z, from_o, b - 1)
                    if name == "T1b" and here:
                        centre(2, b)
                        centre(3, b)
                    if name == "Q0" and here:
                        total(2, b)
                    if name == "Q1" and here:
                        total(3, b)
                    if name == "PV0a" and within(b, 1, B):
                        dve.wait_ge(summed, b)
                        statistics(2, lambda t: x1[:, t, :], b - 1, isinstance(b, int) and b == 1)
                    if name == "K1" and within(b, -2, B - 3):
                        dve.wait_ge(x_loaded, 16 * (b + 3))
                        statistics(0, lambda t: x_in[:, t, :], b + 2, isinstance(b, int) and b == -2)
                    if name == "T2b" and within(b, 1, B):
                        if within(b, 2, B):
                            dve.wait_ge(ring_full, nth(RING, "N2", b - 1))
                        apply(2, xn2, lambda t: x1[:, t, :], b - 1)
                if within(b, -2, B - 3):
                    if within(b, -1, B - 3):
                        dve.wait_ge(ring_full, nth(RING, "X", b))
                    apply(0, xn, lambda t: x_in[:, t, :], b + 2)

            iterations(dve, step)

        @block.tensor
        def _(pe):
            skip, signal = counted(RING, ring_full)

            def similarity(u, b):
                n = 4 * b + u
                pe.wait_ge(ring_lo, nth(LO, "Q3", b - 1))
                if within(b, 1, B) or u >= 2:
                    pe.wait_ge(centred, n - 1)
                tt, half = u % 2, u // 2
                for i in range(HP):
                    pair = half * HP + i
                    last = split_product(pe, sim[u % 2][:, i // 2, (i % 2) * 2 * J:(i % 2 + 1) * 2 * J],
                                         [t[:, pair, tt * P:(tt + 1) * P] for t in qT], [t[:, pair, :] for t in kT])
                last.then_inc(sim_full, 1)

            def accumulate(out, products):
                for k, (left, right) in enumerate(products):
                    last = split_product(pe, out, left, right, start=k == 0, stop=k == len(products) - 1)
                return last

            def output(name, b):
                if not runs(name, b):
                    return skip()
                i, at = RING.index(name) - NBANK, b
                while True:
                    if i < 0:
                        i, at = i + len(RING), at - 1
                    if runs(RING[i], at):
                        before = RING[i]
                        if before == "O":
                            pe.wait_ge(applied[1], at)
                        elif before == "N2":
                            pe.wait_ge(ring_hi, nth(HI, before, at))
                        else:
                            pe.wait_ge(ring_lo, nth(LO, before, at))
                        break
                    i -= NBANK
                    if isinstance(at, int) and at < -1:
                        break
                ps = bank(name)
                if name == "X":
                    pe.wait_ge(applied[0], b + 2)
                    for c in range(DC):
                        for t in range(TT):
                            last = pe.transpose(ps[:, c * N + t * P:c * N + (t + 1) * P], xn[:, t, c * P:(c + 1) * P], ident[:, :])
                elif name == "C":
                    pe.wait_ge(ctx_loaded, 16 * (b + 2))
                    for c in range(CC):
                        last = pe.transpose(ps[:, c * J:c * J + M], ctx_in[:, c * P:(c + 1) * P], ident[0:M, 0:M])
                elif name[0] == "T":
                    u, first = int(name[1]), 4 * "ab".index(name[2])
                    pe.wait_ge(probs_ready, 4 * b + u + 1)
                    for h in range(4):
                        last = pe.transpose(ps[0:J, h * P:(h + 1) * P], probs[u % 2][:, first + h, :], ident[:, :])
                elif name[0] == "K":
                    pe.wait_ge(ring_lo, nth(LO, "C", b))
                    for i in range(HP):
                        col = (HP * int(name[1]) + i) * P
                        last = accumulate(ps[:, i * J:(i + 1) * J],
                                          [([w[:, c, col:col + P] for w in wkv], [t[:, c, :] for t in ctxT]) for c in range(CC)])
                elif name[0] == "Q":
                    pe.wait_ge(ring_lo, nth(LO, "X", b))
                    for i in range(2):
                        col = (2 * int(name[1]) + i) * P
                        last = accumulate(ps[:, i * N:(i + 1) * N],
                                          [([w[:, c, col:col + P] for w in wq], [t[:, c, :] for t in xnT]) for c in range(DC)])
                elif name[0] == "V":
                    pe.wait_ge(ring_lo, nth(LO, "C", b))
                    col = INNER + int(name[1]) * 512
                    last = accumulate(ps[0:M, :],
                                      [([t[:, c, 0:M] for t in ctxT], [w[:, c, col:col + 512] for w in wkv]) for c in range(CC)])
                elif name[0] == "P":
                    half = int(name[2])
                    pe.wait_ge(ring_lo, nth(LO, f"T{2 * half + 1}b", b))
                    for i in range(2):
                        local = 2 * "ab".index(name[3]) + i
                        last = accumulate(ps[:, i * N:(i + 1) * N],
                                          [([t[:, half * HP + local, s * DH:s * DH + P] for t in vv],
                                            [t[:, 2 * local + s, :] for t in pT]) for s in range(2)])
                elif name == "O":
                    pe.wait_ge(ring_lo, nth(LO, "PV1b", b - 1))
                    for t in range(TT):
                        last = accumulate(ps[:, t * D:(t + 1) * D],
                                          [([o[:, q, t * P:(t + 1) * P] for o in outT], [w[:, q, :] for w in wo]) for q in range(PAIRS)])
                else:
                    pe.wait_ge(applied[2], b)
                    for c in range(DC):
                        for t in range(TT):
                            last = pe.transpose(ps[:, c * N + t * P:c * N + (t + 1) * P], xn2[:, t, c * P:(c + 1) * P], ident[:, :])
                signal(last)

            pe.wait_ge(made, 6)
            pe.wait_ge(w_lo, len(pieces))
            pe.wait_ge(null_lo, 2)
            pe.wait_ge(null_placed, 64)

            def step(b):
                here = within(b, 0, B - 1)
                if here:
                    similarity(0, b)
                    similarity(1, b)
                for name in RING:
                    if within(b, -1, B):
                        output(name, b)
                    if name == "T1b" and here:
                        similarity(2, b)
                        similarity(3, b)

            iterations(pe, step)


def expert_phase(nc, ctx, dram):
    def sb(name, shape, dt=F32):
        return ctx.enter_context(nc.sbuf_tensor(name, shape, dt))

    def sem(name):
        return ctx.enter_context(nc.semaphore(name))

    groups = T // GT
    ident = sb("ident2", [P, P])
    gate = sb("gate2", [P, 2])
    router = sb("router_raw", [P, DC, ROUTED])
    router_w = [sb(f"router_{s}", [P, DC, ROUTED], F32R) for s in "hl"]
    router_bias = sb("router_bias", [P, ROUTED])
    bias_rows = [sb(f"{n}_bias_rows", [ROUTED + 1, I]) for n in ("gate", "up")]
    bias_cols = [sb(f"{n}_bias_cols", [P, ROUTED + 1]) for n in ("gate", "up")]
    gate_bias = sb("gate_bias", [P, SLOTS])
    down_bias_raw = sb("down_bias_raw", [ROUTED + 1, D])
    down_bias = [sb(f"down_bias_{s}", [ROUTED + 1, D], F32R) for s in "hl"]
    w_raw = [sb(f"w_raw{i}", [P, EW]) for i in range(SLOTS + 1)]
    w_split = [[sb(f"w{i}_{s}", [P, EW], F32R) for s in "hl"] for i in range(SLOTS + 1)]
    xT_raw = sb("xT_raw", [P, DC, GT])
    xT = [sb(f"xT_{s}", [P, DC, GT], F32R) for s in "hl"]
    x1 = sb("x1_rows", [P, GTILES, D])
    logits = sb("logits", [P, GTILES, ROUTED])
    affinity = sb("affinity", [P, GTILES, ROUTED])
    top = sb("top", [P, GTILES, TOPK])
    without_top = sb("without_top", [P, GTILES, ROUTED])
    chosen = sb("chosen", [P, GTILES, ROUTED])
    weight = sb("weight", [P, GTILES, ROUTED])
    total = sb("total", [P, GTILES])
    total_inv = sb("total_inv", [P, GTILES])
    weightT = sb("weightT", [ROUTED, GT])
    weightT_split = [sb(f"weightT_{s}", [ROUTED + 1, GT], F32R) for s in "hl"]
    weight_rows = [sb(f"weight_rows{i}", [1, 2, GT]) for i in range(2)]
    spread = [sb(f"spread{i}", [P, GT]) for i in range(2)]
    act_gate = [sb(f"act_gate{i}", [P, BLK]) for i in range(2)]
    hidden = [sb(f"hidden{i}", [P, BLK]) for i in range(2)]
    hid = [[sb(f"hid{i}_{s}", [P, BLK], F32R) for s in "hl"] for i in range(2)]
    accT = sb("accT", [P, DC, GT])

    acc = ctx.enter_context(nc.psum_tensor("acc", [P, DC, NB, BLK], F32))
    gu = [[ctx.enter_context(nc.psum_tensor(f"{n}{i}", [P, BLK], F32)) for n in ("gate_ps", "up_ps")] for i in range(2)]
    banks = [gu[0][0], gu[0][1], gu[1][0], gu[1][1]]
    per_slot = ROUTED // SLOTS

    const_loaded, shared_loaded, made, gate_ready = sem("const2_loaded"), sem("shared_loaded"), sem("made2"), sem("gate2_ready")
    const_hi, const_lo, bias_turned, bias_ready, gate_bias_ready = sem("const_hi"), sem("const_lo"), sem("bias_turned"), sem("bias_ready"), sem("gate_bias_ready")
    w_loaded = [sem(f"w2_loaded{i}") for i in range(SLOTS)]
    w_hi, w_lo = sem("w2_hi"), sem("w2_lo")
    xT_loaded, xT_hi, xT_lo = sem("xT_loaded"), sem("xT_hi"), sem("xT_lo")
    x1_loaded = sem("x1_loaded")
    logits_full, logits_ready, affinity_ready, top_ready = sem("logits_full"), sem("logits_ready"), sem("affinity_ready"), sem("top_ready")
    removed, chosen_ready, picked, total_ready, total_safe, inv_ready, weight_ready = (
        sem(n) for n in ("removed", "chosen_ready", "picked", "total_ready", "total_safe", "inv_ready", "weight_ready"))
    weightT_full, weightT_copied, weightT_hi, weightT_lo = (sem(n) for n in ("weightT_full", "weightT_copied", "weightT_hi", "weightT_lo"))
    weightT_stored = sem("weightT_stored")
    rows_loaded = [sem(f"rows_loaded{i}") for i in range(2)]
    spread_ready = sem("spread_ready")
    gate_full, up_full, silu_done, weighted, hidden_ready, hid_hi, hid_lo, down_done = (
        sem(n) for n in ("gate_full", "up_full", "silu_done", "weighted", "hidden_ready", "hid_hi", "hid_lo", "down_done"))
    acc_full, acc_read_act, acc_read_dve = sem("acc_full"), sem("acc_read_act"), sem("acc_read_dve")
    turned, out_ready, out_stored = sem("turned"), sem("out_ready"), sem("out_stored")

    def weight_views(w):
        return (w[:, 0:DC * I].rearrange("p (c i) -> p c i", c=DC), w[:, DC * I:2 * DC * I].rearrange("p (c i) -> p c i", c=DC),
                w[:, 2 * DC * I:EW])

    def step_index(g, e, k):
        return g * STEPS + e * NB + k

    constants = [(gate[:, 0:1], dram["g_ffn"].unsqueeze(0).broadcast_to([P, 1])),
                 (router[:, :, :], dram["Wr"].rearrange("(c p) e -> p c e", p=P)),
                 (router_bias[:, :], dram["br"].unsqueeze(0).broadcast_to([P, ROUTED])),
                 (bias_rows[0][0:ROUTED, :], dram["bg"]), (bias_rows[0][ROUTED:, :], dram["bg_s"].unsqueeze(0)),
                 (bias_rows[1][0:ROUTED, :], dram["bu"]), (bias_rows[1][ROUTED:, :], dram["bu_s"].unsqueeze(0)),
                 (down_bias_raw[0:ROUTED, :], dram["bd"]), (down_bias_raw[ROUTED:, :], dram["bd_s"].unsqueeze(0))]
    x2_cols = dram["x2T"].rearrange("c p n -> p c n")
    x1_tiles = dram["x1"].rearrange("(g t p) d -> g p t d", t=GTILES, p=P)
    out_tiles = dram["out"].rearrange("b (s p) d -> p (b s) d", p=P)

    with nc.Block() as block:
        def over_groups(eng, group):
            group(0)
            with eng.Fori(1, groups - 1) as g:
                group(g)
            group(groups - 1)

        def is_first(g):
            return isinstance(g, int) and g == 0

        def is_last(g):
            return isinstance(g, int) and g == groups - 1

        @block.sync
        def _(sp):
            for dst, name in zip(weight_views(w_raw[SLOTS]), ("Wg_s", "Wu_s", "Wd_s")):
                src = dram[name] if name == "Wd_s" else dram[name].rearrange("(c p) i -> p c i", p=P)
                sp.dma_start(dst, src).then_inc(shared_loaded, 16)

            def load_expert(e, slot):
                for dst, name in zip(weight_views(w_raw[slot]), ("Wg", "Wu", "Wd")):
                    src = dram[name] if name == "Wd" else dram[name].rearrange("e (c p) i -> e p c i", p=P)
                    sp.dma_start(dst, src[e]).then_inc(w_loaded[slot], 16)

            def load_xT(g):
                sp.dma_start(xT_raw[:, :, :], x2_cols[:, :, bass.ds(g * GT, GT)]).then_inc(xT_loaded, 16)

            def group(g):
                if not is_first(g):
                    sp.wait_ge(out_stored, 64 * g)
                sp.dma_start(x1[:, :, :], x1_tiles[g]).then_inc(x1_loaded, 16)
                sp.wait_ge(weightT_copied, g + 1)
                sp.dma_start(dram["weightT"][:, bass.ds(g * GT, GT)], weightT[:, :]).then_inc(weightT_stored, 16)
                sp.wait_ge(weightT_stored, 16 * (g + 1))

                def load_rows(j):
                    for half in range(2):
                        if not (is_first(g) and isinstance(j, int)):
                            sp.wait_ge(spread_ready, g * ROUTED + SLOTS * j + 2 * half - 2)
                        sp.dma_start(weight_rows[half][:, :, :],
                                     dram["weightT"][bass.ds(SLOTS * j + 2 * half, 2), bass.ds(g * GT, GT)].unsqueeze(0)
                                     ).then_inc(rows_loaded[half], 16)

                def reload(j, e0):
                    for q in range(SLOTS):
                        sp.wait_ge(w_hi, g * ROUTED + SLOTS * j + q + 1)
                        sp.wait_ge(w_lo, g * ROUTED + SLOTS * j + q + 1)
                        load_expert(e0 + q, q)

                load_rows(0)
                with sp.Fori(1, per_slot) as j:
                    reload(j - 1, SLOTS * j)
                    load_rows(j)
                reload(per_slot - 1, 0)
                if not is_last(g):
                    load_xT(g + 1)
                for i in range(4):
                    sp.wait_ge(out_ready, 4 * g + i + 1)
                    sp.dma_start(out_tiles[:, bass.ds(g * GTILES + 2 * i, 2), :], x1[:, 2 * i:2 * i + 2, :]).then_inc(out_stored, 16)

            load_xT(0)
            for slot in range(SLOTS):
                load_expert(slot, slot)
            over_groups(sp, group)
            sp.wait_ge(out_stored, 64 * groups)
            for slot in range(SLOTS):
                sp.wait_ge(w_loaded[slot], 48 * (groups * per_slot + 1))

        @block.gpsimd
        def _(pool):
            pool.memset(ident[:, :], 0.0).then_inc(made, 1)
            pool.wait_ge(made, 1)
            pool.affine_select(out=ident[:, :], in_=ident[:, :], compare_op=ALU.not_equal, fill=1.0, base=0,
                               pattern=[[-1, P]], channel_multiplier=1).then_inc(made, 1)
            for dst, src in constants:
                pool.dma_start(dst, src).then_inc(const_loaded, 16)

            def split_low(slot, r):
                pool.wait_ge(w_hi, r + 1)
                pool.tensor_tensor(w_split[slot][1][:, :], w_raw[slot][:, :], w_split[slot][0][:, :].bitcast(F32),
                                   ALU.subtract).then_inc(w_lo, 1)

            split_low(0, 0)

            def group(g):
                def experts(j):
                    for q in range(SLOTS):
                        r = g * ROUTED + SLOTS * j + q
                        if q % 2 == 0:
                            pool.wait_ge(rows_loaded[q // 2], 16 * (g * per_slot + j + 1))
                        if not (is_first(g) and isinstance(j, int) and q < 2):
                            pool.wait_ge(weighted, NB * (r - 1))
                        split_low((q + 1) % SLOTS, r + 1)
                        pool.partition_broadcast(spread[q % 2][:, :], weight_rows[q // 2][:, q % 2, :], P).then_inc(spread_ready, 1)

                experts(0)
                with pool.Fori(1, per_slot) as j:
                    experts(j)

            over_groups(pool, group)

        @block.scalar
        def _(act):
            act.wait_ge(const_loaded, 16 * len(constants))
            act.activation(gate[:, 1:2], gate[:, 0:1], ACT.Tanh).then_inc(gate_ready, 1)
            act.activation(router_w[0][:, :, :], router[:, :, :], ACT.Copy).then_inc(const_hi, 1)
            act.activation(down_bias[0][:, :], down_bias_raw[:, :], ACT.Copy).then_inc(const_hi, 1)
            act.wait_ge(shared_loaded, 48)
            act.activation(w_split[SLOTS][0][:, :], w_raw[SLOTS][:, :], ACT.Copy).then_inc(const_hi, 1)

            def split_high(slot, r, loads, steps):
                act.wait_ge(w_loaded[slot], 48 * loads)
                if steps is not None:
                    act.wait_ge(down_done, steps)
                act.activation(w_split[slot][0][:, :], w_raw[slot][:, :], ACT.Copy).then_inc(w_hi, 1)

            for r in range(SPLIT_AHEAD):
                split_high(r, r, 1, None)
            act.wait_ge(bias_ready, 1)

            def half_step(g, e, k, bias):
                n = step_index(g, e, k)
                fresh = is_first(g) and isinstance(e, int) and e == 0
                act.wait_ge(gate_full, n + 1)
                if not fresh:
                    act.wait_ge(hidden_ready, n - 1)
                act.activation(act_gate[k][:, :], gu[k][0][:, :], ACT.Silu, bias=bias).then_inc(silu_done, 1)
                act.wait_ge(hidden_ready, n + 1)
                if not fresh:
                    act.wait_ge(down_done, n - 1)
                act.activation(hid[k][0][:, :], hidden[k][:, :], ACT.Copy).then_inc(hid_hi, 1)

            def split_xT(g):
                act.wait_ge(xT_loaded, 16 * (g + 1))
                if not is_first(g):
                    act.wait_ge(up_full, g * STEPS)
                act.activation(xT[0][:, :, :], xT_raw[:, :, :], ACT.Copy).then_inc(xT_hi, 1)

            def group(g):
                act.wait_ge(logits_ready, g + 1)
                act.activation(affinity[:, :, :], logits[:, :, :], ACT.Sigmoid).then_inc(affinity_ready, 1)
                for k in range(NB):
                    half_step(g, 0, k, bias_cols[0][:, ROUTED:])
                act.wait_ge(weightT_copied, g + 1)
                if not is_first(g):
                    act.wait_ge(acc_full, g)
                for i in range(2):
                    last = act.activation(weightT_split[0][0:ROUTED, i * 512:(i + 1) * 512], gu[0][i][0:ROUTED, :], ACT.Copy)
                last.then_inc(weightT_hi, 1)

                def experts(j):
                    act.wait_ge(silu_done, step_index(g, SLOTS * j + 1, 0))
                    act.activation(gate_bias[:, :], bias_cols[0][:, bass.ds(SLOTS * j, SLOTS)], ACT.Copy).then_inc(gate_bias_ready, 1)
                    act.wait_ge(gate_bias_ready, g * per_slot + j + 1)
                    for q in range(SLOTS):
                        e = SLOTS * j + q
                        half_step(g, e + 1, 0, gate_bias[:, q:q + 1])
                        ahead = q + SPLIT_AHEAD
                        if isinstance(j, int) and ahead < SLOTS:
                            steps = None if is_first(g) else g * STEPS
                        else:
                            steps = step_index(g, e, 0)
                        split_high(ahead % SLOTS, g * ROUTED + e + SPLIT_AHEAD, g * per_slot + j + ahead // SLOTS + 1, steps)
                        half_step(g, e + 1, 1, gate_bias[:, q:q + 1])

                experts(0)
                with act.Fori(1, per_slot) as j:
                    experts(j)
                if not is_last(g):
                    split_xT(g + 1)
                act.wait_ge(acc_full, g + 1)
                if not is_first(g):
                    act.wait_ge(turned, 4 * g)
                for c in range(DC):
                    last = act.activation(accT[:, c, 0:BLK], acc[:, c, 0, :], ACT.Copy, scale=gate[:, 1:2])
                last.then_inc(acc_read_act, 1)

            split_xT(0)
            over_groups(act, group)

        @block.vector
        def _(dve):
            dve.memset(weightT_split[0][ROUTED:, :].bitcast(F32), 1.0)
            dve.memset(weightT_split[1][ROUTED:, :].bitcast(F32), 0.0)
            dve.wait_ge(const_hi, 3)
            for dst, src in ((router_w, router), (down_bias, down_bias_raw), (w_split[SLOTS], w_raw[SLOTS])):
                whole = (slice(None),) * len(src.shape)
                last = dve.tensor_tensor(dst[1][whole], src[whole], dst[0][whole].bitcast(F32), ALU.subtract)
            last.then_inc(const_lo, 1)
            dve.wait_ge(bias_turned, 1)
            for i in range(2):
                last = dve.tensor_copy(bias_cols[i][:, :], gu[0][i][:, 0:ROUTED + 1])
            last.then_inc(bias_ready, 1)
            dve.wait_ge(bias_ready, 1)
            dve.wait_ge(gate_ready, 1)

            def half_step(g, e, k, bias, row=None, routed=None):
                n = step_index(g, e, k)
                dve.wait_ge(silu_done, n + 1)
                if row is not None:
                    if k == 0:
                        dve.wait_ge(spread_ready, routed + 1)
                    dve.tensor_tensor(act_gate[k][:, :], act_gate[k][:, :], row[:, k * BLK:(k + 1) * BLK],
                                      ALU.mult).then_inc(weighted, 1)
                    dve.wait_ge(weighted, NB * routed + k + 1)
                dve.wait_ge(up_full, n + 1)
                if not (is_first(g) and isinstance(e, int) and e == 0):
                    dve.wait_ge(hid_lo, n - 1)
                dve.scalar_tensor_tensor(out=hidden[k][:, :], in0=gu[k][1][:, :], scalar=bias, in1=act_gate[k][:, :],
                                         op0=ALU.add, op1=ALU.mult).then_inc(hidden_ready, 1)
                dve.wait_ge(hid_hi, n + 1)
                dve.tensor_tensor(hid[k][1][:, :], hidden[k][:, :], hid[k][0][:, :].bitcast(F32), ALU.subtract).then_inc(hid_lo, 1)

            def split_xT(g):
                dve.wait_ge(xT_hi, g + 1)
                dve.tensor_tensor(xT[1][:, :, :], xT_raw[:, :, :], xT[0][:, :, :].bitcast(F32), ALU.subtract).then_inc(xT_lo, 1)

            def route(g):
                dve.wait_ge(logits_full, g + 1)
                if not is_first(g):
                    dve.wait_ge(affinity_ready, g)
                dve.tensor_tensor(logits[:, :, :], gu[1][0][:, 0:GTILES * ROUTED].rearrange("p (t e) -> p t e", t=GTILES),
                                  router_bias[:, :].unsqueeze(1).broadcast_to([P, GTILES, ROUTED]), ALU.add).then_inc(logits_ready, 1)
                dve.wait_ge(gate_ready, 1)
                dve.wait_ge(logits_ready, g + 1)
                for t in range(GTILES):
                    last = dve.max(top[:, t, :], logits[:, t, :])
                last.then_inc(top_ready, 1)
                dve.wait_ge(gate_ready, 1)
                dve.wait_ge(top_ready, g + 1)
                for t in range(GTILES):
                    last = dve.match_replace(without_top[:, t, :], top[:, t, :], logits[:, t, :], LOWEST)
                last.then_inc(removed, 1)
                dve.wait_ge(removed, g + 1)
                dve.tensor_tensor(chosen[:, :, :], logits[:, :, :], without_top[:, :, :], ALU.not_equal).then_inc(chosen_ready, 1)
                dve.wait_ge(chosen_ready, g + 1)
                dve.wait_ge(affinity_ready, g + 1)
                dve.tensor_tensor(chosen[:, :, :], chosen[:, :, :], affinity[:, :, :], ALU.mult).then_inc(picked, 1)
                dve.wait_ge(picked, g + 1)
                dve.tensor_reduce(total[:, :], chosen[:, :, :], AX.X, ALU.add).then_inc(total_ready, 1)
                dve.wait_ge(total_ready, g + 1)
                dve.tensor_scalar(total[:, :], total[:, :], 1e-9, None, ALU.add).then_inc(total_safe, 1)
                dve.wait_ge(total_safe, g + 1)
                dve.reciprocal(total_inv[:, :], total[:, :]).then_inc(inv_ready, 1)
                dve.wait_ge(inv_ready, g + 1)
                if not is_first(g):
                    dve.wait_ge(weightT_full, g)
                dve.tensor_tensor(weight[:, :, :], chosen[:, :, :], total_inv[:, :].unsqueeze(2).broadcast_to([P, GTILES, ROUTED]),
                                  ALU.mult).then_inc(weight_ready, 1)

            def group(g):
                route(g)
                for k in range(NB):
                    half_step(g, 0, k, bias_cols[1][:, ROUTED:])
                dve.wait_ge(weightT_full, g + 1)
                if not is_first(g):
                    dve.wait_ge(weightT_stored, 16 * g)
                for i in range(2):
                    last = dve.tensor_copy(weightT[:, i * 512:(i + 1) * 512], gu[0][i][0:ROUTED, :])
                last.then_inc(weightT_copied, 1)
                dve.wait_ge(weightT_hi, g + 1)
                dve.wait_ge(weightT_copied, g + 1)
                dve.tensor_tensor(weightT_split[1][0:ROUTED, :], weightT[:, :], weightT_split[0][0:ROUTED, :].bitcast(F32),
                                  ALU.subtract).then_inc(weightT_lo, 1)

                def experts(j):
                    for q in range(SLOTS):
                        e = SLOTS * j + q
                        for k in range(NB):
                            half_step(g, e + 1, k, bias_cols[1][:, bass.ds(e, 1)], spread[q % 2], g * ROUTED + e)

                experts(0)
                with dve.Fori(1, per_slot) as j:
                    experts(j)
                dve.wait_ge(acc_full, g + 1)
                if not is_first(g):
                    dve.wait_ge(turned, 4 * g)
                for c in range(DC):
                    last = dve.tensor_scalar(accT[:, c, BLK:], acc[:, c, 1, :], gate[:, 1:2], None, ALU.mult)
                last.then_inc(acc_read_dve, 1)
                if not is_last(g):
                    split_xT(g + 1)
                dve.wait_ge(x1_loaded, 16 * (g + 1))
                for i in range(4):
                    dve.wait_ge(turned, 4 * g + i + 1)
                    rows = x1[:, 2 * i:2 * i + 2, :]
                    dve.tensor_tensor(rows, banks[i][:, :].rearrange("p (t d) -> p t d", t=2), rows, ALU.add).then_inc(out_ready, 1)

            split_xT(0)
            over_groups(dve, group)

        @block.tensor
        def _(pe):
            pe.wait_ge(made, 2)
            pe.wait_ge(const_loaded, 16 * len(constants))
            for i in range(2):
                last = pe.transpose(gu[0][i][:, 0:ROUTED + 1], bias_rows[i][:, :], ident[0:ROUTED + 1, 0:ROUTED + 1])
            last.then_inc(bias_turned, 1)
            pe.wait_ge(bias_ready, 1)
            pe.wait_ge(const_lo, 1)

            def gate_up(g, e, k, slot):
                w = w_split[slot]
                for part, done in ((0, gate_full), (1, up_full)):
                    for c in range(DC):
                        col = (part * DC + c) * I
                        last = split_product(pe, gu[k][part][:, :], [t[:, col:col + I] for t in w],
                                             [t[:, c, k * BLK:(k + 1) * BLK] for t in xT], start=c == 0, stop=c == DC - 1)
                    last.then_inc(done, 1)

            def down(g, e, k, slot, start=False):
                n = step_index(g, e, k)
                pe.wait_ge(hid_lo, n + 1)
                for c in range(DC):
                    last = split_product(pe, acc[:, c, k, :], [t[:, 2 * DC * I + c * P:2 * DC * I + (c + 1) * P] for t in w_split[slot]],
                                         [t[:, :] for t in hid[k]], start=start, stop=False)
                last.then_inc(down_done, 1)

            def group(g):
                pe.wait_ge(xT_lo, g + 1)
                if not is_first(g):
                    pe.wait_ge(out_ready, 4 * g)
                for t in range(GTILES):
                    for c in range(DC):
                        last = split_product(pe, gu[1][0][:, t * ROUTED:(t + 1) * ROUTED], [x[:, c, t * P:(t + 1) * P] for x in xT],
                                             [w[:, c, :] for w in router_w], start=c == 0, stop=c == DC - 1)
                last.then_inc(logits_full, 1)
                gate_up(g, 0, 0, SLOTS)
                pe.wait_ge(logits_ready, g + 1)
                gate_up(g, 0, 1, SLOTS)
                pe.wait_ge(weight_ready, g + 1)
                pe.wait_ge(hidden_ready, step_index(g, 0, 0) + 1)
                for t in range(GTILES):
                    last = pe.transpose(gu[0][t // 4][0:ROUTED, (t % 4) * P:(t % 4 + 1) * P], weight[:, t, :], ident[:, :])
                last.then_inc(weightT_full, 1)
                if not is_first(g):
                    pe.wait_ge(acc_read_act, g)
                    pe.wait_ge(acc_read_dve, g)
                down(g, 0, 0, SLOTS, start=True)
                pe.wait_ge(weightT_hi, g + 1)

                def experts(j):
                    for q in range(SLOTS):
                        e = SLOTS * j + q
                        pe.wait_ge(w_lo, g * ROUTED + e + 1)
                        for k in range(NB):
                            if k == 1 or q or not isinstance(j, int):
                                pe.wait_ge(hidden_ready, step_index(g, e + 1, k) - 1)
                            gate_up(g, e + 1, k, q)
                            if k == 1:
                                down(g, e + 1, 0, q)
                            elif q == 0 and isinstance(j, int):
                                down(g, 0, 1, SLOTS, start=True)
                            else:
                                down(g, e, 1, (q - 1) % SLOTS)

                experts(0)
                with pe.Fori(1, per_slot) as j:
                    experts(j)
                down(g, ROUTED, 1, SLOTS - 1)
                pe.wait_ge(weightT_lo, g + 1)
                for k in range(NB):
                    for c in range(DC):
                        last = split_product(pe, acc[:, c, k, :], [t[:, c * P:(c + 1) * P] for t in down_bias],
                                             [t[:, k * BLK:(k + 1) * BLK] for t in weightT_split], start=False, stop=True)
                last.then_inc(acc_full, 1)
                pe.wait_ge(acc_read_act, g + 1)
                pe.wait_ge(acc_read_dve, g + 1)
                for i in range(4):
                    for t in range(2):
                        for c in range(DC):
                            last = pe.transpose(banks[i][:, t * D + c * P:t * D + (c + 1) * P],
                                                accT[:, c, (2 * i + t) * P:(2 * i + t + 1) * P], ident[:, :])
                    last.then_inc(turned, 1)

            over_groups(pe, group)


def layer(nc, dram):
    with ExitStack() as ctx:
        attention_phase(nc, ctx, dram)
    with ExitStack() as ctx:
        expert_phase(nc, ctx, dram)


INPUTS = {"x": "x", "ctx_2048": "ctx", "g_xattn": "g_xattn", "g_ffn": "g_ffn", "L0_xattn_Wq": "Wq", "L0_xattn_Wkv": "Wkv",
          "L0_xattn_null_kv": "null_kv", "L0_xattn_Wout": "Wout", "L0_xattn_ln_scale": "ln_scale", "L0_xattn_ln_bias": "ln_bias",
          **{f"L0_ffn_{n}": n for n in ("Wr", "br", "Wg_s", "bg_s", "Wu_s", "bu_s", "Wd_s", "bd_s", "Wg", "bg", "Wu", "bu", "Wd", "bd")}}


def kernel(**inputs):
    import numpy as np
    import concourse.bacc as bacc
    from concourse.bass_utils import run_bass_kernel_spmd

    nc = bacc.Bacc("TRN2", target_bir_lowering=False, num_devices=1)
    arrays, dram = {}, {}
    for given, name in INPUTS.items():
        arrays[f"in_{name}"] = np.ascontiguousarray(inputs[given])
        dram[name] = nc.dram_tensor(f"in_{name}", arrays[f"in_{name}"].shape, F32, kind="ExternalInput").ap()
    dram["out"] = nc.dram_tensor("out_dram", (B, N, D), F32, kind="ExternalOutput").ap()
    dram["x1"] = nc.dram_tensor("x1_dram", (T, D), F32, kind="Internal").ap()
    dram["x2T"] = nc.dram_tensor("x2T_dram", (DC, P, T), F32, kind="Internal").ap()
    dram["weightT"] = nc.dram_tensor("weightT_dram", (ROUTED, T), F32, kind="Internal").ap()
    layer(nc, dram)
    return run_bass_kernel_spmd(nc, [arrays], core_ids=[0]).results[0]["out_dram"]
```

```python
from contextlib import ExitStack

import concourse.bass as bass
from concourse import mybir

F32 = mybir.dt.float32
F32R = mybir.dt.float32r
ACT = mybir.ActivationFunctionType
ALU = mybir.AluOpType
AX = mybir.AxisListType

P = 128
B, N, D = 32, 256, 256
M, CTX = 77, 512
J = M + 1
HEADS, DH = 16, 64
INNER = HEADS * DH
PAIRS = HEADS // 2
HP = PAIRS // 2
TT = N // P
DC, CC = D // P, CTX // P
T = B * N
SCALE = DH ** -0.5
LN_EPS, OUT_EPS = 1e-5, 1e-6
ROUTED, TOPK = 32, 8
I = 128
GT = 1024
BLK = 512
NB = GT // BLK
GTILES = GT // P
SLOTS = 4
EW = 2 * DC * I + D
STEPS = NB * (ROUTED + 1)
SPLIT_AHEAD = 2
LOWEST = -3.0e38

CG, CBLOCKS = 8, 2
CGROUPS = B // CG
CROWS = CG * M
CBATCHES = CG // CBLOCKS
CCOLS = CROWS // CBLOCKS
CTILES = -(-CROWS // P)
CRING = ["K00", "K01", "C4"] + [f"K0{i}" for i in range(2, PAIRS)] + [f"K1{i}" for i in range(PAIRS)] + [
    "V00", "V01", "V10", "V11", "C0", "V20", "V21", "C1", "V30", "V31", "C2", "V40", "V41", "C3"]
CBANK = 8
CTURN = -(-len(CRING) // CBANK) * CBANK
C_ACT = [n for n in CRING if n[0] != "V"]
C_DVE = [n for n in CRING if n[0] != "K"]

RING = ["O", "X", "T0a", "T0b", "T1a", "T1b", "Q0", "Q1", "PV0a", "PV0b", "Q2",
        "T2a", "T2b", "T3a", "T3b", "Q3", "N2", "PV1a", "-", "PV1b"]
NBANK = 4
HI = [n for n in RING if n not in ("O", "-")]
LO = [n for n in RING if n not in ("O", "N2", "-")]


def runs(name, b):
    if name == "-":
        return False
    if not isinstance(b, int):
        return True
    if name in ("O", "N2"):
        return 1 <= b <= B
    return 0 <= b < B if name[0] in "TP" else -1 <= b < B - 1


def nth(names, name, b):
    return (b + 1) * len(names) + (names.index(name) + 1)


def split_product(eng, out, left, right, start=True, stop=True):
    eng.matmul(out, left[0], right[0], start=start, stop=False)
    eng.matmul(out, left[1], right[0], start=False, stop=False)
    return eng.matmul(out, left[0], right[1], start=False, stop=stop)


def iterations(eng, step):
    for b in (-2, -1, 0, 1):
        step(b)
    with eng.Fori(2, B - 2) as b:
        step(b)
    for b in (B - 2, B - 1, B):
        step(b)


def within(b, first, last):
    return first <= b <= last if isinstance(b, int) else True


def counted(names, semaphore):
    left_out = [0]

    def skip():
        left_out[0] += 1

    def signal(instruction):
        instruction.then_inc(semaphore, 1 + left_out[0])
        left_out[0] = 0
    return skip, signal


def context_phase(nc, ctx, dram, wq, wo):
    def sb(name, shape, dt=F32):
        return ctx.enter_context(nc.sbuf_tensor(name, shape, dt))

    def sem(name):
        return ctx.enter_context(nc.semaphore(name))

    ident = sb("ident0", [P, P])
    wkv = [sb(f"wkv_{s}", [P, CC, 2 * INNER], F32R) for s in "hl"]
    stage = [sb(f"stage{i}", [P, 2048]) for i in range(2)]
    rows = sb("ctx_rows", [P, CTILES, CTX])
    ctxT = [sb(f"ctxT_{s}", [P, CC, CROWS], F32R) for s in "hl"]
    keys = sb("keys", [P, CBLOCKS, CBATCHES, PAIRS * M])
    values = sb("values", [P, CTILES, INNER])
    banks = [ctx.enter_context(nc.psum_tensor(f"bank{i}", [P, 512], F32)) for i in range(CBANK)]

    w_loaded = [sem(f"w_loaded{i}") for i in range(2)]
    w_hi, w_lo, made = sem("w_hi"), sem("w_lo"), sem("made0")
    rows_loaded = [sem(f"ctx_rows_loaded{t}") for t in range(CTILES)]
    keys_stored = [sem(f"keys_stored{i}") for i in range(CBLOCKS)]
    values_stored = [sem(f"values_stored{t}") for t in range(CTILES)]
    full, act_read, dve_read = sem("full"), sem("act_read"), sem("dve_read")

    pieces = [(dram["Wkv"][c * P:(c + 1) * P, :], [w[:, c, :] for w in wkv], 1.0) for c in range(CC)]
    pieces.append((dram["Wq"].rearrange("(c p) n -> p c n", p=P), [w[:, :, :] for w in wq], SCALE))
    pieces.append((dram["Wout"].rearrange("(c p) n -> p c n", p=P), [w[:, :, :] for w in wo], 1.0))

    def staged(i):
        shape = pieces[i][1][0].shape
        s = stage[i % 2][:, :]
        return s.rearrange("p (c n) -> p c n", c=shape[1]) if len(shape) == 3 else s

    ctx_rows = dram["ctx"].rearrange("b m c -> (b m) c")
    keys_out = dram["keys"].rearrange("b p f -> p b f")

    def size(t):
        return min(P, CROWS - t * P)

    def bank(name):
        return banks[CRING.index(name) % CBANK]

    def made_in(name, g):
        if not isinstance(g, int):
            return True
        return g < CGROUPS - 1 if name in ("C0", "C1", "C2", "C3") else g >= 0

    def at(names, name, g):
        return (g + 1) * len(names) + names.index(name) + 1

    def steps(eng, step):
        step(-1)
        step(0)
        with eng.Fori(1, CGROUPS - 1) as g:
            step(g)
        step(CGROUPS - 1)

    with nc.Block() as block:
        @block.sync
        def _(sp):
            def load_rows(t, g):
                sp.dma_start(rows[0:size(t), t, :], ctx_rows[bass.ds(g * CROWS + t * P, size(t)), :]).then_inc(rows_loaded[t], 16)

            def load_piece(i):
                if i >= 2:
                    sp.wait_ge(w_lo, i - 1)
                sp.dma_start(staged(i), pieces[i][0]).then_inc(w_loaded[i % 2], 16)

            for t in range(CTILES):
                load_rows(t, 0)
            for i in range(CC):
                load_piece(i)

            def step(g):
                for name in CRING:
                    if not made_in(name, g):
                        continue
                    if name[0] == "K" and name[2] == str(PAIRS - 1):
                        i = int(name[1])
                        sp.wait_ge(act_read, at(C_ACT, name, g))
                        sp.dma_start(keys_out[:, bass.ds(g * CG + i * CBATCHES, CBATCHES), :], keys[:, i, :, :]).then_inc(keys_stored[i], 16)
                    elif name[0] == "V" and name[2] == "1":
                        t = int(name[1])
                        sp.wait_ge(dve_read, at(C_DVE, name, g))
                        sp.dma_start(dram["values"][bass.ds(g * CROWS + t * P, size(t)), :], values[0:size(t), t, :]).then_inc(values_stored[t], 16)
                    elif name[0] == "C":
                        t = int(name[1])
                        ahead = 1 if name == "C4" else 2
                        if not isinstance(g, int) or g + ahead < CGROUPS:
                            sp.wait_ge(full, at(CRING, name, g))
                            load_rows(t, g + ahead)

            step(-1)
            step(0)
            for i in range(CC, len(pieces)):
                load_piece(i)
            for g in range(1, CGROUPS):
                step(g)
            for t in range(CTILES):
                sp.wait_ge(values_stored[t], 16 * CGROUPS)
            for i in range(CBLOCKS):
                sp.wait_ge(keys_stored[i], 16 * CGROUPS)

        @block.gpsimd
        def _(pool):
            pool.memset(ident[:, :], 0.0).then_inc(made, 1)
            pool.wait_ge(made, 1)
            pool.affine_select(out=ident[:, :], in_=ident[:, :], compare_op=ALU.not_equal, fill=1.0, base=0,
                               pattern=[[-1, P]], channel_multiplier=1).then_inc(made, 1)

        @block.scalar
        def _(act):
            skip, signal = counted(C_ACT, act_read)

            def split_high(i):
                _, dst, factor = pieces[i]
                act.wait_ge(w_loaded[i % 2], 16 * (i // 2 + 1))
                act.activation(dst[0], staged(i), ACT.Copy, scale=factor).then_inc(w_hi, 1)

            def step(g):
                for name in C_ACT:
                    if not made_in(name, g):
                        skip()
                        continue
                    act.wait_ge(full, at(CRING, name, g))
                    ps = bank(name)
                    if name[0] == "K":
                        i, pair = int(name[1]), int(name[2])
                        if pair == 0 and not (isinstance(g, int) and g == 0):
                            act.wait_ge(keys_stored[i], 16 * g)
                        last = act.activation(keys[:, i, :, pair * M:(pair + 1) * M],
                                              ps[:, 0:CCOLS].rearrange("p (b m) -> p b m", m=M), ACT.Copy)
                    else:
                        t = int(name[1])
                        last = act.activation(ctxT[0][:, :, t * P:t * P + size(t)],
                                              ps[:, :].rearrange("p (c r) -> p c r", c=CC)[:, :, 0:size(t)], ACT.Copy)
                    signal(last)

            step(-1)
            for i in range(CC):
                split_high(i)
            step(0)
            for i in range(CC, len(pieces)):
                split_high(i)
            with act.Fori(1, CGROUPS - 1) as g:
                step(g)
            step(CGROUPS - 1)

        @block.vector
        def _(dve):
            skip, signal = counted(C_DVE, dve_read)

            def split_low(i):
                _, dst, factor = pieces[i]
                dve.wait_ge(w_hi, i + 1)
                dve.scalar_tensor_tensor(out=dst[1], in0=staged(i), scalar=factor, in1=dst[0].bitcast(F32),
                                         op0=ALU.mult, op1=ALU.subtract).then_inc(w_lo, 1)

            def step(g):
                for name in C_DVE:
                    if not made_in(name, g):
                        skip()
                        continue
                    ps, t = bank(name), int(name[1])
                    if name[0] == "C":
                        dve.wait_ge(act_read, at(C_ACT, name, g))
                        last = dve.tensor_tensor(ctxT[1][:, :, t * P:t * P + size(t)],
                                                 ps[:, :].rearrange("p (c r) -> p c r", c=CC)[:, :, 0:size(t)],
                                                 ctxT[0][:, :, t * P:t * P + size(t)].bitcast(F32), ALU.subtract)
                    else:
                        half = int(name[2])
                        dve.wait_ge(full, at(CRING, name, g))
                        if half == 0 and not (isinstance(g, int) and g == 0):
                            dve.wait_ge(values_stored[t], 16 * g)
                        last = dve.tensor_copy(values[0:size(t), t, half * 512:(half + 1) * 512], ps[0:size(t), :])
                    signal(last)

            step(-1)
            for i in range(CC):
                split_low(i)
            step(0)
            for i in range(CC, len(pieces)):
                split_low(i)
            with dve.Fori(1, CGROUPS - 1) as g:
                step(g)
            step(CGROUPS - 1)

        @block.tensor
        def _(pe):
            skip, signal = counted(CRING, full)

            def free(name, g):
                i, step = CRING.index(name) - CBANK, g
                while True:
                    if i < 0:
                        i, step = i + CTURN, step - 1
                    if isinstance(step, int) and step < -1:
                        return
                    if i < len(CRING) and made_in(CRING[i], step):
                        before = CRING[i]
                        if before[0] == "K":
                            pe.wait_ge(act_read, at(C_ACT, before, step))
                        else:
                            pe.wait_ge(dve_read, at(C_DVE, before, step))
                        return
                    i -= CBANK

            def step(g):
                for name in CRING:
                    if not made_in(name, g):
                        skip()
                        continue
                    free(name, g)
                    ps, i = bank(name), int(name[1])
                    if name[0] == "C":
                        ahead = 0 if name == "C4" else 1
                        pe.wait_ge(rows_loaded[i], 16 * (g + ahead + 1))
                        for c in range(CC):
                            last = pe.transpose(ps[:, c * P:c * P + size(i)], rows[0:size(i), i, c * P:(c + 1) * P],
                                                ident[0:size(i), 0:size(i)])
                    elif name[0] == "K":
                        if name[2] == "0":
                            pe.wait_ge(dve_read, at(C_DVE, "C4", g) if i else at(C_DVE, "C3", g - 1))
                        col = int(name[2]) * P
                        for c in range(CC):
                            last = split_product(pe, ps[:, 0:CCOLS], [w[:, c, col:col + P] for w in wkv],
                                                 [t[:, c, i * CCOLS:(i + 1) * CCOLS] for t in ctxT], c == 0, c == CC - 1)
                    else:
                        col = INNER + int(name[2]) * 512
                        for c in range(CC):
                            last = split_product(pe, ps[0:size(i), :], [t[:, c, i * P:i * P + size(i)] for t in ctxT],
                                                 [w[:, c, col:col + 512] for w in wkv], c == 0, c == CC - 1)
                    signal(last)

            pe.wait_ge(made, 2)
            step(-1)
            pe.wait_ge(w_lo, CC)
            step(0)
            with pe.Fori(1, CGROUPS - 1) as g:
                step(g)
            step(CGROUPS - 1)


def attention_phase(nc, ctx, dram, wq, wo):
    def sb(name, shape, dt=F32):
        return ctx.enter_context(nc.sbuf_tensor(name, shape, dt))

    def sem(name):
        return ctx.enter_context(nc.semaphore(name))

    ident = sb("ident", [P, P])
    scale_row = sb("scale_row", [P, D])
    bias_row = sb("bias_row", [P, D])
    gate = sb("gate", [P, 2])
    minus_half = sb("minus_half", [P, TT])
    eps_col = [sb(f"eps_col{i}", [P, TT]) for i in range(3)]
    null_k = sb("null_k", [P, 1])
    x_in = sb("x_in", [P, TT, D])
    x_res = sb("x_res", [P, TT, D])
    keys = sb("keys_raw", [P, PAIRS, 2 * J])
    values = sb("values_raw", [J, INNER])
    xn = sb("xn", [P, TT, D])
    xnT = [sb(f"xnT_{s}", [P, DC, N], F32R) for s in "hl"]
    kT = [sb(f"kT_{s}", [P, PAIRS, 2 * J], F32R) for s in "hl"]
    vv = [sb(f"v_{s}", [J, PAIRS, 3 * DH], F32R) for s in "hl"]
    qT = [sb(f"qT_{s}", [P, PAIRS, N], F32R) for s in "hl"]
    outT = [sb(f"outT_{s}", [P, PAIRS, N], F32R) for s in "hl"]
    probs = [sb(f"probs{i}", [P, PAIRS, J]) for i in range(2)]
    minus_max = [sb(f"minus_max{i}", [P, PAIRS]) for i in range(2)]
    row_sum = [sb(f"row_sum{i}", [P, PAIRS]) for i in range(2)]
    row_inv = [sb(f"row_inv{i}", [P, PAIRS]) for i in range(2)]
    stats = [sb(f"stats{i}", [P, TT, 6]) for i in range(3)]
    mean_var = [sb(f"mean_var{i}", [P, TT, 2]) for i in range(3)]
    var_eps = [sb(f"var_eps{i}", [P, TT]) for i in range(3)]
    rstd = [sb(f"rstd{i}", [P, TT]) for i in range(3)]
    z = sb("z", [P, TT, D])
    x1 = sb("x1", [P, TT, D])
    xn2 = sb("xn2", [P, TT, D])
    x2T = sb("x2T", [P, DC, N])
    pT = [sb(f"pT_{s}", [J, PAIRS, N], F32R) for s in "hl"]

    sim = [ctx.enter_context(nc.psum_tensor(f"sim{i}", [P, 2, 512], F32)) for i in range(2)]
    ring = [ctx.enter_context(nc.psum_tensor(f"ring{i}", [P, 512], F32)) for i in range(NBANK)]

    const_loaded, zeroed, made = sem("const_loaded"), sem("zeroed"), sem("made")
    null_key_placed, null_value_placed = sem("null_key_placed"), sem("null_value_placed")
    gate_ready, rows_ready = sem("gate_ready"), sem("rows_ready")
    x_loaded, res_loaded = sem("x_loaded"), sem("res_loaded")
    keys_loaded, keys_hi, keys_lo = sem("keys_loaded"), sem("keys_hi"), sem("keys_lo")
    values_loaded, values_hi, values_lo = sem("values_loaded"), sem("values_hi"), sem("values_lo")
    x1_stored, x2_stored = sem("x1_stored"), sem("x2_stored")
    ring_full, ring_hi, ring_lo = sem("ring_full"), sem("ring_hi"), sem("ring_lo")
    sim_full, max_done, exp_done = sem("sim_full"), sem("max_done"), sem("exp_done")
    inv_done, probs_ready = sem("inv_done"), sem("probs_ready")
    stats_done = [sem(f"stats_done{i}") for i in range(3)]
    var_done = [sem(f"var_done{i}") for i in range(3)]
    eps_done = [sem(f"eps_done{i}") for i in range(3)]
    rstd_done = [sem(f"rstd_done{i}") for i in range(3)]
    applied = [sem(f"applied{i}") for i in range(3)]
    scaled, shifted, summed = sem("scaled"), sem("shifted"), sem("summed")

    x_tiles = dram["x"].rearrange("b (t p) d -> b p t d", p=P)
    x1_tiles = dram["x1"].rearrange("(b t p) d -> b p t d", t=TT, p=P)
    x2_cols = dram["x2T"].rearrange("c p n -> p c n")

    def bank(name):
        return ring[RING.index(name) % NBANK]

    def scores(u):
        return sim[u % 2][:, :, 0:4 * J].rearrange("p a (h j) -> p a h j", j=J)

    def destinations(name):
        ps = bank(name)
        if name == "X":
            return [(ps[:, :].rearrange("p (c n) -> p c n", c=DC), [t[:, :, :] for t in xnT])]
        if name[0] == "T":
            tt, first = int(name[1]) % 2, 4 * "ab".index(name[2])
            return [(ps[0:J, :].rearrange("p (h n) -> p h n", h=4),
                     [t[:, first:first + 4, tt * P:(tt + 1) * P] for t in pT])]
        if name[0] == "Q":
            q = 2 * int(name[1])
            return [(ps[:, :].rearrange("p (h n) -> p h n", h=2), [t[:, q:q + 2, :] for t in qT])]
        q = HP * int(name[2]) + 2 * "ab".index(name[3])
        return [(ps[:, :].rearrange("p (h n) -> p h n", h=2), [t[:, q:q + 2, :] for t in outT])]

    def value_part(part):
        return vv[part][:, :, :].rearrange("p h (s d) -> p h s d", d=DH)[:, :, 0:3:2, :]

    values_by_head = values[:, :].rearrange("p (h s d) -> p h s d", s=2, d=DH)

    with nc.Block() as block:
        @block.sync
        def _(sp):
            sp.dma_start(x_in[:, :, :], x_tiles[0]).then_inc(x_loaded, 16)

            def load_keys(batch):
                for half, col in ((slice(0, DH), 0), (slice(DH, P), J)):
                    sp.dma_start(keys[half, :, col:col + M],
                                 dram["keys"].rearrange("b p (h m) -> b p h m", m=M)[batch, half]).then_inc(keys_loaded, 16)

            def load_values(batch):
                sp.dma_start(values[0:M, :], dram["values"][bass.ds(batch * M, M), :]).then_inc(values_loaded, 16)

            load_values(0)
            sp.dma_start(values[M:J, :].rearrange("p (h d) -> p h d", d=DH),
                         dram["null_kv"][1:2, :].unsqueeze(1).broadcast_to([1, HEADS, DH])).then_inc(null_value_placed, 16)
            sp.wait_ge(zeroed, 1)
            load_keys(0)
            def step(b):
                if within(b, -1, B - 3):
                    sp.wait_ge(applied[0], b + 2)
                    sp.dma_start(x_in[:, :, :], x_tiles[b + 2]).then_inc(x_loaded, 16)
                if within(b, 0, B - 2):
                    sp.wait_ge(values_lo, b + 1)
                    load_values(b + 1)
                if within(b, 1, B):
                    sp.wait_ge(summed, b)
                    sp.dma_start(x1_tiles[b - 1], x1[:, :, :]).then_inc(x1_stored, 16)
                if within(b, 0, B - 1):
                    sp.dma_start(x_res[:, :, :], x_tiles[b]).then_inc(res_loaded, 16)
                if within(b, 1, B):
                    sp.wait_ge(ring_hi, nth(HI, "N2", b))
                    sp.dma_start(x2_cols[:, :, bass.ds((b - 1) * N, N)], x2T[:, :, :]).then_inc(x2_stored, 16)
                if within(b, -1, B - 3):
                    sp.wait_ge(keys_lo, b + 2)
                    load_keys(b + 2)

            iterations(sp, step)
            sp.wait_ge(x1_stored, 16 * B)
            sp.wait_ge(x2_stored, 16 * B)

        @block.gpsimd
        def _(pool):
            pool.memset(ident[:, :], 0.0).then_inc(made, 1)
            pool.memset(minus_half[:, :], -0.5).then_inc(made, 1)
            for i, eps in enumerate((LN_EPS, OUT_EPS, LN_EPS)):
                pool.memset(eps_col[i][:, :], eps).then_inc(made, 1)
            pool.wait_ge(made, 5)
            pool.affine_select(out=ident[:, :], in_=ident[:, :], compare_op=ALU.not_equal, fill=1.0, base=0,
                               pattern=[[-1, P]], channel_multiplier=1).then_inc(made, 1)
            with nc.allow_non_contiguous_dma(reason="one column of 64 elements"):
                for half in (slice(0, DH), slice(DH, P)):
                    pool.dma_start(null_k[half, :], dram["null_kv"][0:1, :].rearrange("a d -> d a")).then_inc(const_loaded, 16)
            pool.dma_start(gate[:, 0:1], dram["g_xattn"].unsqueeze(0).broadcast_to([P, 1])).then_inc(const_loaded, 16)
            pool.dma_start(scale_row[:, :], dram["ln_scale"].unsqueeze(0).broadcast_to([P, D])).then_inc(const_loaded, 16)
            pool.dma_start(bias_row[:, :], dram["ln_bias"].unsqueeze(0).broadcast_to([P, D])).then_inc(const_loaded, 16)

            def make_rstd(i, batch):
                pool.wait_ge(var_done[i], batch + 1)
                pool.tensor_tensor(var_eps[i][:, :], mean_var[i][:, :, 1], eps_col[i][:, :], ALU.add).then_inc(eps_done[i], 1)
                pool.wait_ge(eps_done[i], batch + 1)
                pool.tensor_tensor(rstd[i][:, :], var_eps[i][:, :], minus_half[:, :], ALU.pow).then_inc(rstd_done[i], 1)

            def normalise(u, b):
                pool.wait_ge(inv_done, 4 * b + u + 1)
                e = probs[u % 2]
                pool.tensor_tensor(e[:, :, :], e[:, :, :], row_inv[u % 2][:, :].unsqueeze(2).broadcast_to([P, PAIRS, J]),
                                   ALU.mult).then_inc(probs_ready, 1)

            def step(b):
                if within(b, 0, B - 1):
                    pool.wait_ge(values_hi, b + 1)
                    pool.tensor_tensor(value_part(1), values_by_head, value_part(0).bitcast(F32), ALU.subtract).then_inc(values_lo, 1)
                    normalise(0, b)
                    normalise(1, b)
                if within(b, 1, B):
                    make_rstd(1, b - 1)
                    pool.wait_ge(res_loaded, 16 * b)
                    if isinstance(b, int) and b == 1:
                        pool.wait_ge(rows_ready, 2)
                    if within(b, 2, B):
                        pool.wait_ge(x1_stored, 16 * (b - 1))
                        pool.wait_ge(applied[2], b - 1)
                    pool.tensor_tensor(x1[:, :, :], x_res[:, :, :], bias_row[:, :].unsqueeze(1).broadcast_to([P, TT, D]),
                                       ALU.add).then_inc(shifted, 1)
                    pool.wait_ge(applied[1], b)
                    pool.tensor_tensor(z[:, :, :], z[:, :, :], scale_row[:, :].unsqueeze(1).broadcast_to([P, TT, D]),
                                       ALU.mult).then_inc(scaled, 1)
                    pool.wait_ge(scaled, b)
                    pool.wait_ge(shifted, b)
                    pool.tensor_tensor(x1[:, :, :], x1[:, :, :], z[:, :, :], ALU.add).then_inc(summed, 1)
                if within(b, 0, B - 1):
                    normalise(2, b)
                if within(b, 1, B):
                    make_rstd(2, b - 1)
                if within(b, 0, B - 1):
                    normalise(3, b)
                if within(b, -2, B - 3):
                    if within(b, -2, -2):
                        pool.wait_ge(made, 6)
                    make_rstd(0, b + 2)
                if within(b, -1, B - 2):
                    pool.wait_ge(keys_hi, b + 2)
                    pool.tensor_tensor(kT[1][:, :, :], keys[:, :, :], kT[0][:, :, :].bitcast(F32), ALU.subtract).then_inc(keys_lo, 1)

            iterations(pool, step)

        @block.scalar
        def _(act):
            skip, signal = counted(HI, ring_hi)

            act.wait_ge(const_loaded, 80)
            act.activation(gate[:, 1:2], gate[:, 0:1], ACT.Tanh).then_inc(gate_ready, 1)
            act.wait_ge(zeroed, 1)
            act.activation(keys[0:DH, :, M], null_k[0:DH, 0:1].broadcast_to([DH, PAIRS]), ACT.Copy).then_inc(null_key_placed, 1)
            act.activation(keys[DH:P, :, J + M], null_k[DH:P, 0:1].broadcast_to([DH, PAIRS]), ACT.Copy).then_inc(null_key_placed, 1)
            act.wait_ge(null_key_placed, 2)
            act.wait_ge(null_value_placed, 16)

            def exp(u, b):
                act.wait_ge(max_done, 4 * b + u + 1)
                if u >= 2:
                    act.wait_ge(ring_full, nth(RING, f"T{u - 2}b", b))
                elif within(b, 1, B):
                    act.wait_ge(ring_full, nth(RING, f"T{u + 2}b", b - 1))
                for h in range(PAIRS):
                    last = act.activation(probs[u % 2][:, h, :], scores(u)[:, h // 4, h % 4, :], ACT.Exp,
                                          bias=minus_max[u % 2][:, h:h + 1], accum_out=row_sum[u % 2][:, h:h + 1])
                last.then_inc(exp_done, 1)

            def high(name, b):
                if not runs(name, b):
                    return skip()
                act.wait_ge(ring_full, nth(RING, name, b))
                if name == "N2":
                    if within(b, 2, B):
                        act.wait_ge(x2_stored, 16 * (b - 1))
                    last = act.activation(x2T[:, :, :], bank(name)[:, :].rearrange("p (c n) -> p c n", c=DC), ACT.Copy)
                else:
                    for src, dst in destinations(name):
                        last = act.activation(dst[0], src, ACT.Copy)
                signal(last)

            def step(b):
                here = within(b, 0, B - 1)
                if here:
                    act.wait_ge(values_loaded, 16 * (b + 1))
                    if within(b, 1, B):
                        act.wait_ge(ring_full, nth(RING, "PV1b", b - 1))
                    act.activation(value_part(0), values_by_head, ACT.Copy).then_inc(values_hi, 1)
                    exp(0, b)
                    exp(1, b)
                for name in HI:
                    if within(b, -1, B):
                        high(name, b)
                    if name == "T1b" and here:
                        exp(2, b)
                    if name == "Q0" and here:
                        exp(3, b)
                    if name == "PV0b" and within(b, -1, B - 2):
                        act.wait_ge(keys_loaded, 32 * (b + 2))
                        if within(b, 0, B):
                            act.wait_ge(sim_full, 4 * b + 4)
                        act.activation(kT[0][:, :, :], keys[:, :, :], ACT.Copy).then_inc(keys_hi, 1)

            iterations(act, step)

        @block.vector
        def _(dve):
            skip, signal = counted(LO, ring_lo)

            for t in (keys[:, :, :], *(v[:, :, :].bitcast(F32) for v in vv)):
                last = dve.memset(t, 0.0)
            last.then_inc(zeroed, 1)
            dve.wait_ge(gate_ready, 1)
            for row in (scale_row, bias_row):
                dve.tensor_scalar(row[:, :], row[:, :], gate[:, 1:2], None, ALU.mult).then_inc(rows_ready, 1)

            def maximum(u, b):
                dve.wait_ge(sim_full, 4 * b + u + 1)
                dve.tensor_reduce(minus_max[u % 2][:, :].rearrange("p (a h) -> p a h", a=2), scores(u), AX.X,
                                  ALU.max, negate=True).then_inc(max_done, 1)

            def invert(u, b):
                n = 4 * b + u
                dve.wait_ge(exp_done, n + 1)
                if within(b, 1, B) or u >= 2:
                    dve.wait_ge(probs_ready, n - 1)
                dve.reciprocal(row_inv[u % 2][:, :], row_sum[u % 2][:, :]).then_inc(inv_done, 1)

            def statistics(i, src, batch, first):
                if not first:
                    dve.wait_ge(applied[i], batch)
                for t in range(TT):
                    last = dve.bn_stats(stats[i][:, t, :], src(t))
                last.then_inc(stats_done[i], 1)
                dve.wait_ge(zeroed, 1)
                dve.wait_ge(stats_done[i], batch + 1)
                for t in range(TT):
                    last = dve.bn_aggr(mean_var[i][:, t, :], stats[i][:, t, :])
                last.then_inc(var_done[i], 1)

            def apply(i, out, src, batch):
                dve.wait_ge(rstd_done[i], batch + 1)
                for t in range(TT):
                    last = dve.tensor_scalar(out[:, t, :], src(t), mean_var[i][:, t, 0:1], rstd[i][:, t:t + 1],
                                             ALU.subtract, ALU.mult)
                return last.then_inc(applied[i], 1)

            def from_o(t):
                return bank("O")[:, t * D:(t + 1) * D]

            def low(name, b):
                if not runs(name, b):
                    return skip()
                dve.wait_ge(ring_hi, nth(HI, name, b))
                for src, dst in destinations(name):
                    last = dve.tensor_tensor(dst[1], src, dst[0].bitcast(F32), ALU.subtract)
                signal(last)

            def step(b):
                here = within(b, 0, B - 1)
                if here:
                    maximum(0, b)
                    maximum(1, b)
                    invert(0, b)
                    invert(1, b)
                if within(b, 1, B):
                    dve.wait_ge(ring_full, nth(RING, "O", b))
                    statistics(1, from_o, b - 1, isinstance(b, int) and b == 1)
                for name in LO:
                    if within(b, -1, B):
                        low(name, b)
                    if name == "X" and within(b, 1, B):
                        if within(b, 2, B):
                            dve.wait_ge(summed, b - 1)
                        apply(1, z, from_o, b - 1)
                    if name == "T0b" and here:
                        maximum(2, b)
                    if name == "T1b" and here:
                        maximum(3, b)
                    if name == "Q0" and here:
                        invert(2, b)
                        invert(3, b)
                    if name == "PV0b" and within(b, 1, B):
                        dve.wait_ge(summed, b)
                        statistics(2, lambda t: x1[:, t, :], b - 1, isinstance(b, int) and b == 1)
                    if name == "Q2" and within(b, -2, B - 3):
                        dve.wait_ge(x_loaded, 16 * (b + 3))
                        statistics(0, lambda t: x_in[:, t, :], b + 2, isinstance(b, int) and b == -2)
                    if name == "T2b" and within(b, 1, B):
                        if within(b, 2, B):
                            dve.wait_ge(ring_full, nth(RING, "N2", b - 1))
                        apply(2, xn2, lambda t: x1[:, t, :], b - 1)
                if within(b, -2, B - 3):
                    if within(b, -1, B - 3):
                        dve.wait_ge(ring_full, nth(RING, "X", b))
                    apply(0, xn, lambda t: x_in[:, t, :], b + 2)

            iterations(dve, step)

        @block.tensor
        def _(pe):
            skip, signal = counted(RING, ring_full)

            def similarity(u, b):
                n = 4 * b + u
                pe.wait_ge(ring_lo, nth(LO, "Q3", b - 1))
                pe.wait_ge(keys_lo, b + 1)
                if within(b, 1, B) or u >= 2:
                    pe.wait_ge(exp_done, n - 1)
                tt, half = u % 2, u // 2
                for i in range(HP):
                    pair = half * HP + i
                    last = split_product(pe, sim[u % 2][:, i // 2, (i % 2) * 2 * J:(i % 2 + 1) * 2 * J],
                                         [t[:, pair, tt * P:(tt + 1) * P] for t in qT], [t[:, pair, :] for t in kT])
                last.then_inc(sim_full, 1)

            def accumulate(out, products):
                for k, (left, right) in enumerate(products):
                    last = split_product(pe, out, left, right, start=k == 0, stop=k == len(products) - 1)
                return last

            def output(name, b):
                if not runs(name, b):
                    return skip()
                i, at = RING.index(name) - NBANK, b
                while True:
                    if i < 0:
                        i, at = i + len(RING), at - 1
                    if runs(RING[i], at):
                        before = RING[i]
                        if before == "O":
                            pe.wait_ge(applied[1], at)
                        elif before == "N2":
                            pe.wait_ge(ring_hi, nth(HI, before, at))
                        else:
                            pe.wait_ge(ring_lo, nth(LO, before, at))
                        break
                    i -= NBANK
                    if isinstance(at, int) and at < -1:
                        break
                ps = bank(name)
                if name == "X":
                    pe.wait_ge(applied[0], b + 2)
                    for c in range(DC):
                        for t in range(TT):
                            last = pe.transpose(ps[:, c * N + t * P:c * N + (t + 1) * P], xn[:, t, c * P:(c + 1) * P], ident[:, :])
                elif name[0] == "T":
                    u, first = int(name[1]), 4 * "ab".index(name[2])
                    pe.wait_ge(probs_ready, 4 * b + u + 1)
                    for h in range(4):
                        last = pe.transpose(ps[0:J, h * P:(h + 1) * P], probs[u % 2][:, first + h, :], ident[:, :])
                elif name[0] == "Q":
                    pe.wait_ge(ring_lo, nth(LO, "X", b))
                    for i in range(2):
                        col = (2 * int(name[1]) + i) * P
                        last = accumulate(ps[:, i * N:(i + 1) * N],
                                          [([w[:, c, col:col + P] for w in wq], [t[:, c, :] for t in xnT]) for c in range(DC)])
                elif name[0] == "P":
                    half = int(name[2])
                    pe.wait_ge(values_lo, b + 1)
                    pe.wait_ge(ring_lo, nth(LO, f"T{2 * half + 1}b", b))
                    for i in range(2):
                        local = 2 * "ab".index(name[3]) + i
                        last = accumulate(ps[:, i * N:(i + 1) * N],
                                          [([t[:, half * HP + local, s * DH:s * DH + P] for t in vv],
                                            [t[:, 2 * local + s, :] for t in pT]) for s in range(2)])
                elif name == "O":
                    pe.wait_ge(ring_lo, nth(LO, "PV1b", b - 1))
                    for t in range(TT):
                        last = accumulate(ps[:, t * D:(t + 1) * D],
                                          [([o[:, q, t * P:(t + 1) * P] for o in outT], [w[:, q, :] for w in wo]) for q in range(PAIRS)])
                else:
                    pe.wait_ge(applied[2], b)
                    for c in range(DC):
                        for t in range(TT):
                            last = pe.transpose(ps[:, c * N + t * P:c * N + (t + 1) * P], xn2[:, t, c * P:(c + 1) * P], ident[:, :])
                signal(last)

            pe.wait_ge(made, 6)

            def step(b):
                here = within(b, 0, B - 1)
                if here:
                    similarity(0, b)
                    similarity(1, b)
                for name in RING:
                    if within(b, -1, B):
                        output(name, b)
                    if name == "T0b" and here:
                        similarity(2, b)
                    if name == "T1b" and here:
                        similarity(3, b)

            iterations(pe, step)


def expert_phase(nc, ctx, dram):
    def sb(name, shape, dt=F32):
        return ctx.enter_context(nc.sbuf_tensor(name, shape, dt))

    def sem(name):
        return ctx.enter_context(nc.semaphore(name))

    groups = T // GT
    ident = sb("ident2", [P, P])
    gate = sb("gate2", [P, 2])
    router = sb("router_raw", [P, DC, ROUTED])
    router_w = [sb(f"router_{s}", [P, DC, ROUTED], F32R) for s in "hl"]
    router_bias = sb("router_bias", [P, ROUTED])
    bias_rows = [sb(f"{n}_bias_rows", [ROUTED + 1, I]) for n in ("gate", "up")]
    bias_cols = [sb(f"{n}_bias_cols", [P, ROUTED + 1]) for n in ("gate", "up")]
    gate_bias = sb("gate_bias", [P, SLOTS])
    down_bias_raw = sb("down_bias_raw", [ROUTED + 1, D])
    down_bias = [sb(f"down_bias_{s}", [ROUTED + 1, D], F32R) for s in "hl"]
    w_raw = [sb(f"w_raw{i}", [P, EW]) for i in range(SLOTS + 1)]
    w_split = [[sb(f"w{i}_{s}", [P, EW], F32R) for s in "hl"] for i in range(SLOTS + 1)]
    xT_raw = sb("xT_raw", [P, DC, GT])
    xT = [sb(f"xT_{s}", [P, DC, GT], F32R) for s in "hl"]
    x1 = sb("x1_rows", [P, GTILES, D])
    logits = sb("logits", [P, GTILES, ROUTED])
    affinity = sb("affinity", [P, GTILES, ROUTED])
    top = sb("top", [P, GTILES, TOPK])
    without_top = sb("without_top", [P, GTILES, ROUTED])
    chosen = sb("chosen", [P, GTILES, ROUTED])
    weight = sb("weight", [P, GTILES, ROUTED])
    total = sb("total", [P, GTILES])
    total_inv = sb("total_inv", [P, GTILES])
    weightT = sb("weightT", [ROUTED, GT])
    weightT_split = [sb(f"weightT_{s}", [ROUTED + 1, GT], F32R) for s in "hl"]
    weight_rows = [sb(f"weight_rows{i}", [1, 2, GT]) for i in range(2)]
    spread = [sb(f"spread{i}", [P, GT]) for i in range(2)]
    act_gate = [sb(f"act_gate{i}", [P, BLK]) for i in range(2)]
    hidden = [sb(f"hidden{i}", [P, BLK]) for i in range(2)]
    hid = [[sb(f"hid{i}_{s}", [P, BLK], F32R) for s in "hl"] for i in range(2)]
    accT = sb("accT", [P, DC, GT])

    acc = ctx.enter_context(nc.psum_tensor("acc", [P, DC, NB, BLK], F32))
    gu = [[ctx.enter_context(nc.psum_tensor(f"{n}{i}", [P, BLK], F32)) for n in ("gate_ps", "up_ps")] for i in range(2)]
    banks = [gu[0][0], gu[0][1], gu[1][0], gu[1][1]]
    per_slot = ROUTED // SLOTS

    const_loaded, shared_loaded, made, gate_ready = sem("const2_loaded"), sem("shared_loaded"), sem("made2"), sem("gate2_ready")
    const_hi, const_lo, bias_turned, bias_ready, gate_bias_ready = sem("const_hi"), sem("const_lo"), sem("bias_turned"), sem("bias_ready"), sem("gate_bias_ready")
    w_loaded = [sem(f"w2_loaded{i}") for i in range(SLOTS)]
    w_hi, w_lo = sem("w2_hi"), sem("w2_lo")
    xT_loaded, xT_hi, xT_lo = sem("xT_loaded"), sem("xT_hi"), sem("xT_lo")
    x1_loaded = sem("x1_loaded")
    logits_full, logits_ready, affinity_ready, top_ready = sem("logits_full"), sem("logits_ready"), sem("affinity_ready"), sem("top_ready")
    removed, chosen_ready, picked, total_ready, total_safe, inv_ready, weight_ready = (
        sem(n) for n in ("removed", "chosen_ready", "picked", "total_ready", "total_safe", "inv_ready", "weight_ready"))
    weightT_full, weightT_copied, weightT_hi, weightT_lo = (sem(n) for n in ("weightT_full", "weightT_copied", "weightT_hi", "weightT_lo"))
    weightT_stored = sem("weightT_stored")
    rows_loaded = [sem(f"rows_loaded{i}") for i in range(2)]
    spread_ready = sem("spread_ready")
    gate_full, up_full, silu_done, weighted, hidden_ready, hid_hi, hid_lo, down_done = (
        sem(n) for n in ("gate_full", "up_full", "silu_done", "weighted", "hidden_ready", "hid_hi", "hid_lo", "down_done"))
    acc_full, acc_read_act, acc_read_dve = sem("acc_full"), sem("acc_read_act"), sem("acc_read_dve")
    turned, out_ready, out_stored = sem("turned"), sem("out_ready"), sem("out_stored")

    def weight_views(w):
        return (w[:, 0:DC * I].rearrange("p (c i) -> p c i", c=DC), w[:, DC * I:2 * DC * I].rearrange("p (c i) -> p c i", c=DC),
                w[:, 2 * DC * I:EW])

    def step_index(g, e, k):
        return g * STEPS + e * NB + k

    constants = [(gate[:, 0:1], dram["g_ffn"].unsqueeze(0).broadcast_to([P, 1])),
                 (router[:, :, :], dram["Wr"].rearrange("(c p) e -> p c e", p=P)),
                 (router_bias[:, :], dram["br"].unsqueeze(0).broadcast_to([P, ROUTED])),
                 (bias_rows[0][0:ROUTED, :], dram["bg"]), (bias_rows[0][ROUTED:, :], dram["bg_s"].unsqueeze(0)),
                 (bias_rows[1][0:ROUTED, :], dram["bu"]), (bias_rows[1][ROUTED:, :], dram["bu_s"].unsqueeze(0)),
                 (down_bias_raw[0:ROUTED, :], dram["bd"]), (down_bias_raw[ROUTED:, :], dram["bd_s"].unsqueeze(0))]
    x2_cols = dram["x2T"].rearrange("c p n -> p c n")
    x1_tiles = dram["x1"].rearrange("(g t p) d -> g p t d", t=GTILES, p=P)
    out_tiles = dram["out"].rearrange("b (s p) d -> p (b s) d", p=P)

    with nc.Block() as block:
        def over_groups(eng, group):
            group(0)
            with eng.Fori(1, groups - 1) as g:
                group(g)
            group(groups - 1)

        def is_first(g):
            return isinstance(g, int) and g == 0

        def is_last(g):
            return isinstance(g, int) and g == groups - 1

        @block.sync
        def _(sp):
            for dst, name in zip(weight_views(w_raw[SLOTS]), ("Wg_s", "Wu_s", "Wd_s")):
                src = dram[name] if name == "Wd_s" else dram[name].rearrange("(c p) i -> p c i", p=P)
                sp.dma_start(dst, src).then_inc(shared_loaded, 16)

            def load_expert(e, slot):
                for dst, name in zip(weight_views(w_raw[slot]), ("Wg", "Wu", "Wd")):
                    src = dram[name] if name == "Wd" else dram[name].rearrange("e (c p) i -> e p c i", p=P)
                    sp.dma_start(dst, src[e]).then_inc(w_loaded[slot], 16)

            def load_xT(g):
                sp.dma_start(xT_raw[:, :, :], x2_cols[:, :, bass.ds(g * GT, GT)]).then_inc(xT_loaded, 16)

            def group(g):
                if not is_first(g):
                    sp.wait_ge(out_stored, 64 * g)
                sp.dma_start(x1[:, :, :], x1_tiles[g]).then_inc(x1_loaded, 16)
                sp.wait_ge(weightT_copied, g + 1)
                sp.dma_start(dram["weightT"][:, bass.ds(g * GT, GT)], weightT[:, :]).then_inc(weightT_stored, 16)
                sp.wait_ge(weightT_stored, 16 * (g + 1))

                def load_rows(j):
                    for half in range(2):
                        if not (is_first(g) and isinstance(j, int)):
                            sp.wait_ge(spread_ready, g * ROUTED + SLOTS * j + 2 * half - 2)
                        sp.dma_start(weight_rows[half][:, :, :],
                                     dram["weightT"][bass.ds(SLOTS * j + 2 * half, 2), bass.ds(g * GT, GT)].unsqueeze(0)
                                     ).then_inc(rows_loaded[half], 16)

                def reload(j, e0):
                    for q in range(SLOTS):
                        sp.wait_ge(w_hi, g * ROUTED + SLOTS * j + q + 1)
                        sp.wait_ge(w_lo, g * ROUTED + SLOTS * j + q + 1)
                        load_expert(e0 + q, q)

                load_rows(0)
                with sp.Fori(1, per_slot) as j:
                    reload(j - 1, SLOTS * j)
                    load_rows(j)
                reload(per_slot - 1, 0)
                if not is_last(g):
                    load_xT(g + 1)
                for i in range(4):
                    sp.wait_ge(out_ready, 4 * g + i + 1)
                    sp.dma_start(out_tiles[:, bass.ds(g * GTILES + 2 * i, 2), :], x1[:, 2 * i:2 * i + 2, :]).then_inc(out_stored, 16)

            load_xT(0)
            for slot in range(SLOTS):
                load_expert(slot, slot)
            over_groups(sp, group)
            sp.wait_ge(out_stored, 64 * groups)
            for slot in range(SLOTS):
                sp.wait_ge(w_loaded[slot], 48 * (groups * per_slot + 1))

        @block.gpsimd
        def _(pool):
            pool.memset(ident[:, :], 0.0).then_inc(made, 1)
            pool.wait_ge(made, 1)
            pool.affine_select(out=ident[:, :], in_=ident[:, :], compare_op=ALU.not_equal, fill=1.0, base=0,
                               pattern=[[-1, P]], channel_multiplier=1).then_inc(made, 1)
            for dst, src in constants:
                pool.dma_start(dst, src).then_inc(const_loaded, 16)

            def split_low(slot, r):
                pool.wait_ge(w_hi, r + 1)
                pool.tensor_tensor(w_split[slot][1][:, :], w_raw[slot][:, :], w_split[slot][0][:, :].bitcast(F32),
                                   ALU.subtract).then_inc(w_lo, 1)

            split_low(0, 0)

            def group(g):
                def experts(j):
                    for q in range(SLOTS):
                        r = g * ROUTED + SLOTS * j + q
                        if q % 2 == 0:
                            pool.wait_ge(rows_loaded[q // 2], 16 * (g * per_slot + j + 1))
                        if not (is_first(g) and isinstance(j, int) and q < 2):
                            pool.wait_ge(weighted, NB * (r - 1))
                        split_low((q + 1) % SLOTS, r + 1)
                        pool.partition_broadcast(spread[q % 2][:, :], weight_rows[q // 2][:, q % 2, :], P).then_inc(spread_ready, 1)

                experts(0)
                with pool.Fori(1, per_slot) as j:
                    experts(j)

            over_groups(pool, group)

        @block.scalar
        def _(act):
            act.wait_ge(const_loaded, 16 * len(constants))
            act.activation(gate[:, 1:2], gate[:, 0:1], ACT.Tanh).then_inc(gate_ready, 1)
            act.activation(router_w[0][:, :, :], router[:, :, :], ACT.Copy).then_inc(const_hi, 1)
            act.activation(down_bias[0][:, :], down_bias_raw[:, :], ACT.Copy).then_inc(const_hi, 1)
            act.wait_ge(shared_loaded, 48)
            act.activation(w_split[SLOTS][0][:, :], w_raw[SLOTS][:, :], ACT.Copy).then_inc(const_hi, 1)

            def split_high(slot, r, loads, steps):
                act.wait_ge(w_loaded[slot], 48 * loads)
                if steps is not None:
                    act.wait_ge(down_done, steps)
                act.activation(w_split[slot][0][:, :], w_raw[slot][:, :], ACT.Copy).then_inc(w_hi, 1)

            for r in range(SPLIT_AHEAD):
                split_high(r, r, 1, None)
            act.wait_ge(bias_ready, 1)

            def half_step(g, e, k, bias):
                n = step_index(g, e, k)
                fresh = is_first(g) and isinstance(e, int) and e == 0
                act.wait_ge(gate_full, n + 1)
                if not fresh:
                    act.wait_ge(hidden_ready, n - 1)
                act.activation(act_gate[k][:, :], gu[k][0][:, :], ACT.Silu, bias=bias).then_inc(silu_done, 1)
                act.wait_ge(hidden_ready, n + 1)
                if not fresh:
                    act.wait_ge(down_done, n - 1)
                act.activation(hid[k][0][:, :], hidden[k][:, :], ACT.Copy).then_inc(hid_hi, 1)

            def split_xT(g):
                act.wait_ge(xT_loaded, 16 * (g + 1))
                if not is_first(g):
                    act.wait_ge(up_full, g * STEPS)
                act.activation(xT[0][:, :, :], xT_raw[:, :, :], ACT.Copy).then_inc(xT_hi, 1)

            def group(g):
                act.wait_ge(logits_ready, g + 1)
                act.activation(affinity[:, :, :], logits[:, :, :], ACT.Sigmoid).then_inc(affinity_ready, 1)
                for k in range(NB):
                    half_step(g, 0, k, bias_cols[0][:, ROUTED:])
                act.wait_ge(weightT_copied, g + 1)
                if not is_first(g):
                    act.wait_ge(acc_full, g)
                for i in range(2):
                    last = act.activation(weightT_split[0][0:ROUTED, i * 512:(i + 1) * 512], gu[0][i][0:ROUTED, :], ACT.Copy)
                last.then_inc(weightT_hi, 1)

                def experts(j):
                    act.wait_ge(silu_done, step_index(g, SLOTS * j + 1, 0))
                    act.activation(gate_bias[:, :], bias_cols[0][:, bass.ds(SLOTS * j, SLOTS)], ACT.Copy).then_inc(gate_bias_ready, 1)
                    act.wait_ge(gate_bias_ready, g * per_slot + j + 1)
                    for q in range(SLOTS):
                        e = SLOTS * j + q
                        half_step(g, e + 1, 0, gate_bias[:, q:q + 1])
                        ahead = q + SPLIT_AHEAD
                        if isinstance(j, int) and ahead < SLOTS:
                            steps = None if is_first(g) else g * STEPS
                        else:
                            steps = step_index(g, e, 0)
                        split_high(ahead % SLOTS, g * ROUTED + e + SPLIT_AHEAD, g * per_slot + j + ahead // SLOTS + 1, steps)
                        half_step(g, e + 1, 1, gate_bias[:, q:q + 1])

                experts(0)
                with act.Fori(1, per_slot) as j:
                    experts(j)
                if not is_last(g):
                    split_xT(g + 1)
                act.wait_ge(acc_full, g + 1)
                if not is_first(g):
                    act.wait_ge(turned, 4 * g)
                for c in range(DC):
                    last = act.activation(accT[:, c, 0:BLK], acc[:, c, 0, :], ACT.Copy, scale=gate[:, 1:2])
                last.then_inc(acc_read_act, 1)

            split_xT(0)
            over_groups(act, group)

        @block.vector
        def _(dve):
            dve.memset(weightT_split[0][ROUTED:, :].bitcast(F32), 1.0)
            dve.memset(weightT_split[1][ROUTED:, :].bitcast(F32), 0.0)
            dve.wait_ge(const_hi, 3)
            for dst, src in ((router_w, router), (down_bias, down_bias_raw), (w_split[SLOTS], w_raw[SLOTS])):
                whole = (slice(None),) * len(src.shape)
                last = dve.tensor_tensor(dst[1][whole], src[whole], dst[0][whole].bitcast(F32), ALU.subtract)
            last.then_inc(const_lo, 1)
            dve.wait_ge(bias_turned, 1)
            for i in range(2):
                last = dve.tensor_copy(bias_cols[i][:, :], gu[0][i][:, 0:ROUTED + 1])
            last.then_inc(bias_ready, 1)
            dve.wait_ge(bias_ready, 1)
            dve.wait_ge(gate_ready, 1)

            def half_step(g, e, k, bias, row=None, routed=None):
                n = step_index(g, e, k)
                dve.wait_ge(silu_done, n + 1)
                if row is not None:
                    if k == 0:
                        dve.wait_ge(spread_ready, routed + 1)
                    dve.tensor_tensor(act_gate[k][:, :], act_gate[k][:, :], row[:, k * BLK:(k + 1) * BLK],
                                      ALU.mult).then_inc(weighted, 1)
                    dve.wait_ge(weighted, NB * routed + k + 1)
                dve.wait_ge(up_full, n + 1)
                if not (is_first(g) and isinstance(e, int) and e == 0):
                    dve.wait_ge(hid_lo, n - 1)
                dve.scalar_tensor_tensor(out=hidden[k][:, :], in0=gu[k][1][:, :], scalar=bias, in1=act_gate[k][:, :],
                                         op0=ALU.add, op1=ALU.mult).then_inc(hidden_ready, 1)
                dve.wait_ge(hid_hi, n + 1)
                dve.tensor_tensor(hid[k][1][:, :], hidden[k][:, :], hid[k][0][:, :].bitcast(F32), ALU.subtract).then_inc(hid_lo, 1)

            def split_xT(g):
                dve.wait_ge(xT_hi, g + 1)
                dve.tensor_tensor(xT[1][:, :, :], xT_raw[:, :, :], xT[0][:, :, :].bitcast(F32), ALU.subtract).then_inc(xT_lo, 1)

            def route(g):
                dve.wait_ge(logits_full, g + 1)
                if not is_first(g):
                    dve.wait_ge(affinity_ready, g)
                dve.tensor_tensor(logits[:, :, :], gu[1][0][:, 0:GTILES * ROUTED].rearrange("p (t e) -> p t e", t=GTILES),
                                  router_bias[:, :].unsqueeze(1).broadcast_to([P, GTILES, ROUTED]), ALU.add).then_inc(logits_ready, 1)
                dve.wait_ge(gate_ready, 1)
                dve.wait_ge(logits_ready, g + 1)
                for t in range(GTILES):
                    last = dve.max(top[:, t, :], logits[:, t, :])
                last.then_inc(top_ready, 1)
                dve.wait_ge(gate_ready, 1)
                dve.wait_ge(top_ready, g + 1)
                for t in range(GTILES):
                    last = dve.match_replace(without_top[:, t, :], top[:, t, :], logits[:, t, :], LOWEST)
                last.then_inc(removed, 1)
                dve.wait_ge(removed, g + 1)
                dve.tensor_tensor(chosen[:, :, :], logits[:, :, :], without_top[:, :, :], ALU.not_equal).then_inc(chosen_ready, 1)
                dve.wait_ge(chosen_ready, g + 1)
                dve.wait_ge(affinity_ready, g + 1)
                dve.tensor_tensor(chosen[:, :, :], chosen[:, :, :], affinity[:, :, :], ALU.mult).then_inc(picked, 1)
                dve.wait_ge(picked, g + 1)
                dve.tensor_reduce(total[:, :], chosen[:, :, :], AX.X, ALU.add).then_inc(total_ready, 1)
                dve.wait_ge(total_ready, g + 1)
                dve.tensor_scalar(total[:, :], total[:, :], 1e-9, None, ALU.add).then_inc(total_safe, 1)
                dve.wait_ge(total_safe, g + 1)
                dve.reciprocal(total_inv[:, :], total[:, :]).then_inc(inv_ready, 1)
                dve.wait_ge(inv_ready, g + 1)
                if not is_first(g):
                    dve.wait_ge(weightT_full, g)
                dve.tensor_tensor(weight[:, :, :], chosen[:, :, :], total_inv[:, :].unsqueeze(2).broadcast_to([P, GTILES, ROUTED]),
                                  ALU.mult).then_inc(weight_ready, 1)

            def group(g):
                route(g)
                for k in range(NB):
                    half_step(g, 0, k, bias_cols[1][:, ROUTED:])
                dve.wait_ge(weightT_full, g + 1)
                if not is_first(g):
                    dve.wait_ge(weightT_stored, 16 * g)
                for i in range(2):
                    last = dve.tensor_copy(weightT[:, i * 512:(i + 1) * 512], gu[0][i][0:ROUTED, :])
                last.then_inc(weightT_copied, 1)
                dve.wait_ge(weightT_hi, g + 1)
                dve.wait_ge(weightT_copied, g + 1)
                dve.tensor_tensor(weightT_split[1][0:ROUTED, :], weightT[:, :], weightT_split[0][0:ROUTED, :].bitcast(F32),
                                  ALU.subtract).then_inc(weightT_lo, 1)

                def experts(j):
                    for q in range(SLOTS):
                        e = SLOTS * j + q
                        for k in range(NB):
                            half_step(g, e + 1, k, bias_cols[1][:, bass.ds(e, 1)], spread[q % 2], g * ROUTED + e)

                experts(0)
                with dve.Fori(1, per_slot) as j:
                    experts(j)
                dve.wait_ge(acc_full, g + 1)
                if not is_first(g):
                    dve.wait_ge(turned, 4 * g)
                for c in range(DC):
                    last = dve.tensor_scalar(accT[:, c, BLK:], acc[:, c, 1, :], gate[:, 1:2], None, ALU.mult)
                last.then_inc(acc_read_dve, 1)
                if not is_last(g):
                    split_xT(g + 1)
                dve.wait_ge(x1_loaded, 16 * (g + 1))
                for i in range(4):
                    dve.wait_ge(turned, 4 * g + i + 1)
                    rows = x1[:, 2 * i:2 * i + 2, :]
                    dve.tensor_tensor(rows, banks[i][:, :].rearrange("p (t d) -> p t d", t=2), rows, ALU.add).then_inc(out_ready, 1)

            split_xT(0)
            over_groups(dve, group)

        @block.tensor
        def _(pe):
            pe.wait_ge(made, 2)
            pe.wait_ge(const_loaded, 16 * len(constants))
            for i in range(2):
                last = pe.transpose(gu[0][i][:, 0:ROUTED + 1], bias_rows[i][:, :], ident[0:ROUTED + 1, 0:ROUTED + 1])
            last.then_inc(bias_turned, 1)
            pe.wait_ge(bias_ready, 1)
            pe.wait_ge(const_lo, 1)

            def gate_up(g, e, k, slot):
                w = w_split[slot]
                for part, done in ((0, gate_full), (1, up_full)):
                    for c in range(DC):
                        col = (part * DC + c) * I
                        last = split_product(pe, gu[k][part][:, :], [t[:, col:col + I] for t in w],
                                             [t[:, c, k * BLK:(k + 1) * BLK] for t in xT], start=c == 0, stop=c == DC - 1)
                    last.then_inc(done, 1)

            def down(g, e, k, slot, start=False):
                n = step_index(g, e, k)
                pe.wait_ge(hid_lo, n + 1)
                for c in range(DC):
                    last = split_product(pe, acc[:, c, k, :], [t[:, 2 * DC * I + c * P:2 * DC * I + (c + 1) * P] for t in w_split[slot]],
                                         [t[:, :] for t in hid[k]], start=start, stop=False)
                last.then_inc(down_done, 1)

            def group(g):
                pe.wait_ge(xT_lo, g + 1)
                if not is_first(g):
                    pe.wait_ge(out_ready, 4 * g)
                for t in range(GTILES):
                    for c in range(DC):
                        last = split_product(pe, gu[1][0][:, t * ROUTED:(t + 1) * ROUTED], [x[:, c, t * P:(t + 1) * P] for x in xT],
                                             [w[:, c, :] for w in router_w], start=c == 0, stop=c == DC - 1)
                last.then_inc(logits_full, 1)
                gate_up(g, 0, 0, SLOTS)
                pe.wait_ge(logits_ready, g + 1)
                gate_up(g, 0, 1, SLOTS)
                pe.wait_ge(weight_ready, g + 1)
                pe.wait_ge(hidden_ready, step_index(g, 0, 0) + 1)
                for t in range(GTILES):
                    last = pe.transpose(gu[0][t // 4][0:ROUTED, (t % 4) * P:(t % 4 + 1) * P], weight[:, t, :], ident[:, :])
                last.then_inc(weightT_full, 1)
                if not is_first(g):
                    pe.wait_ge(acc_read_act, g)
                    pe.wait_ge(acc_read_dve, g)
                down(g, 0, 0, SLOTS, start=True)
                pe.wait_ge(weightT_hi, g + 1)

                def experts(j):
                    for q in range(SLOTS):
                        e = SLOTS * j + q
                        pe.wait_ge(w_lo, g * ROUTED + e + 1)
                        for k in range(NB):
                            if k == 1 or q or not isinstance(j, int):
                                pe.wait_ge(hidden_ready, step_index(g, e + 1, k) - 1)
                            gate_up(g, e + 1, k, q)
                            if k == 1:
                                down(g, e + 1, 0, q)
                            elif q == 0 and isinstance(j, int):
                                down(g, 0, 1, SLOTS, start=True)
                            else:
                                down(g, e, 1, (q - 1) % SLOTS)

                experts(0)
                with pe.Fori(1, per_slot) as j:
                    experts(j)
                down(g, ROUTED, 1, SLOTS - 1)
                pe.wait_ge(weightT_lo, g + 1)
                for k in range(NB):
                    for c in range(DC):
                        last = split_product(pe, acc[:, c, k, :], [t[:, c * P:(c + 1) * P] for t in down_bias],
                                             [t[:, k * BLK:(k + 1) * BLK] for t in weightT_split], start=False, stop=True)
                last.then_inc(acc_full, 1)
                pe.wait_ge(acc_read_act, g + 1)
                pe.wait_ge(acc_read_dve, g + 1)
                for i in range(4):
                    for t in range(2):
                        for c in range(DC):
                            last = pe.transpose(banks[i][:, t * D + c * P:t * D + (c + 1) * P],
                                                accT[:, c, (2 * i + t) * P:(2 * i + t + 1) * P], ident[:, :])
                    last.then_inc(turned, 1)

            over_groups(pe, group)


def layer(nc, dram):
    with ExitStack() as held:
        wq = [held.enter_context(nc.sbuf_tensor(f"wq_{s}", [P, DC, INNER], F32R)) for s in "hl"]
        wo = [held.enter_context(nc.sbuf_tensor(f"wo_{s}", [P, PAIRS, D], F32R)) for s in "hl"]
        with ExitStack() as ctx:
            context_phase(nc, ctx, dram, wq, wo)
        with ExitStack() as ctx:
            attention_phase(nc, ctx, dram, wq, wo)
    with ExitStack() as ctx:
        expert_phase(nc, ctx, dram)


INPUTS = {"x": "x", "ctx_2048": "ctx", "g_xattn": "g_xattn", "g_ffn": "g_ffn", "L0_xattn_Wq": "Wq", "L0_xattn_Wkv": "Wkv",
          "L0_xattn_null_kv": "null_kv", "L0_xattn_Wout": "Wout", "L0_xattn_ln_scale": "ln_scale", "L0_xattn_ln_bias": "ln_bias",
          **{f"L0_ffn_{n}": n for n in ("Wr", "br", "Wg_s", "bg_s", "Wu_s", "bu_s", "Wd_s", "bd_s", "Wg", "bg", "Wu", "bu", "Wd", "bd")}}


def kernel(**inputs):
    import numpy as np
    import concourse.bacc as bacc
    from concourse.bass_utils import run_bass_kernel_spmd

    nc = bacc.Bacc("TRN2", target_bir_lowering=False, num_devices=1)
    arrays, dram = {}, {}
    for given, name in INPUTS.items():
        arrays[f"in_{name}"] = np.ascontiguousarray(inputs[given])
        dram[name] = nc.dram_tensor(f"in_{name}", arrays[f"in_{name}"].shape, F32, kind="ExternalInput").ap()
    dram["out"] = nc.dram_tensor("out_dram", (B, N, D), F32, kind="ExternalOutput").ap()
    dram["keys"] = nc.dram_tensor("keys_dram", (B, P, PAIRS * M), F32, kind="Internal").ap()
    dram["values"] = nc.dram_tensor("values_dram", (B * M, INNER), F32, kind="Internal").ap()
    dram["x1"] = nc.dram_tensor("x1_dram", (T, D), F32, kind="Internal").ap()
    dram["x2T"] = nc.dram_tensor("x2T_dram", (DC, P, T), F32, kind="Internal").ap()
    dram["weightT"] = nc.dram_tensor("weightT_dram", (ROUTED, T), F32, kind="Internal").ap()
    layer(nc, dram)
    return run_bass_kernel_spmd(nc, [arrays], core_ids=[0]).results[0]["out_dram"]
```

```python
from contextlib import ExitStack

import concourse.bass as bass
from concourse import mybir

F32 = mybir.dt.float32
F32R = mybir.dt.float32r
ACT = mybir.ActivationFunctionType
ALU = mybir.AluOpType
AX = mybir.AxisListType

P = 128
B, N, D = 32, 256, 256
M, CTX = 77, 512
J = M + 1
HEADS, DH = 16, 64
INNER = HEADS * DH
PAIRS = HEADS // 2
HP = PAIRS // 2
TT = N // P
DC, CC = D // P, CTX // P
T = B * N
SCALE = DH ** -0.5
LN_EPS, OUT_EPS = 1e-5, 1e-6
ROUTED, TOPK = 32, 8
I = 128
GT = 1024
BLK = 512
NB = GT // BLK
GTILES = GT // P
SLOTS = 4
EW = 2 * DC * I + D
STEPS = NB * (ROUTED + 1)
SPLIT_AHEAD = 2
LOWEST = -3.0e38

CG, CBLOCKS = 8, 2
CGROUPS = B // CG
CROWS = CG * M
CBATCHES = CG // CBLOCKS
CCOLS = CROWS // CBLOCKS
CTILES = -(-CROWS // P)
CRING = ["K00", "K01", "C4"] + [f"K0{i}" for i in range(2, PAIRS)] + [f"K1{i}" for i in range(PAIRS)] + [
    "V00", "V01", "V10", "V11", "C0", "V20", "V21", "C1", "V30", "V31", "C2", "V40", "V41", "C3"]
CBANK = 8
PIECE, STAGES = 1024, 4
CTURN = -(-len(CRING) // CBANK) * CBANK
C_ACT = [n for n in CRING if n[0] != "V"]
C_DVE = [n for n in CRING if n[0] != "K"]

RING = ["N2", "O", "X", "L", "T0a", "T0b", "T1a", "T1b", "Q0", "Q1", "PV0a", "PV0b", "Q2",
        "T2a", "T2b", "T3a", "T3b", "Q3", "PV1a", "PV1b"]
NBANK = 4
HI = [n for n in RING if n not in ("O", "L")]
LO = [n for n in RING if n != "O"]


def runs(name, b):
    if not isinstance(b, int):
        return True
    if name in ("N2", "L"):
        return 2 <= b <= B + 1
    if name == "O":
        return 1 <= b <= B
    return 0 <= b < B if name[0] in "TP" else -1 <= b < B - 1


def nth(names, name, b):
    return (b + 1) * len(names) + (names.index(name) + 1)


def split_product(eng, out, left, right, start=True, stop=True):
    eng.matmul(out, left[0], right[0], start=start, stop=False)
    eng.matmul(out, left[1], right[0], start=False, stop=False)
    return eng.matmul(out, left[0], right[1], start=False, stop=stop)


def iterations(eng, step, after_first=None):
    step(-2)
    if after_first:
        after_first()
    for b in (-1, 0, 1, 2):
        step(b)
    with eng.Fori(3, B - 2) as b:
        step(b)
    for b in (B - 2, B - 1, B, B + 1):
        step(b)


def within(b, first, last):
    return first <= b <= last if isinstance(b, int) else True


def counted(names, semaphore):
    left_out = [0]

    def skip():
        left_out[0] += 1

    def signal(instruction):
        instruction.then_inc(semaphore, 1 + left_out[0])
        left_out[0] = 0
    return skip, signal


def context_phase(nc, ctx, dram, wq, wo):
    def sb(name, shape, dt=F32):
        return ctx.enter_context(nc.sbuf_tensor(name, shape, dt))

    def sem(name):
        return ctx.enter_context(nc.semaphore(name))

    ident = sb("ident0", [P, P])
    wkv = [sb(f"wkv_{s}", [P, CC, 2 * INNER], F32R) for s in "hl"]
    stage = [sb(f"stage{i}", [P, PIECE]) for i in range(STAGES)]
    rows = sb("ctx_rows", [P, CTILES, CTX])
    ctxT = [sb(f"ctxT_{s}", [P, CC, CROWS], F32R) for s in "hl"]
    keys = sb("keys", [P, CBLOCKS, CBATCHES, PAIRS * M])
    values = sb("values", [P, CTILES, INNER])
    banks = [ctx.enter_context(nc.psum_tensor(f"bank{i}", [P, 512], F32)) for i in range(CBANK)]

    w_loaded = [sem(f"w_loaded{i}") for i in range(STAGES)]
    w_hi, w_lo, made = sem("w_hi"), sem("w_lo"), sem("made0")
    rows_loaded = [sem(f"ctx_rows_loaded{t}") for t in range(CTILES)]
    keys_stored = [sem(f"keys_stored{i}") for i in range(CBLOCKS)]
    values_stored = [sem(f"values_stored{t}") for t in range(CTILES)]
    full, act_read, dve_read = sem("full"), sem("act_read"), sem("dve_read")

    pieces = [(dram["Wkv"][c * P:(c + 1) * P, half * INNER:(half + 1) * INNER],
               [w[:, c, half * INNER:(half + 1) * INNER] for w in wkv], 1.0) for half in range(2) for c in range(CC)]
    pieces += [(dram["Wq"][c * P:(c + 1) * P, :], [w[:, c, :] for w in wq], SCALE) for c in range(DC)]
    of_piece = PIECE // D
    pieces += [(dram["Wout"].rearrange("(c p) n -> p c n", p=P)[:, q:q + of_piece, :], [w[:, q:q + of_piece, :] for w in wo], 1.0)
               for q in range(0, PAIRS, of_piece)]

    def staged(i):
        shape = pieces[i][1][0].shape
        s = stage[i % STAGES][:, :]
        return s.rearrange("p (c n) -> p c n", c=shape[1]) if len(shape) == 3 else s

    ctx_rows = dram["ctx"].rearrange("b m c -> (b m) c")
    keys_out = dram["keys"].rearrange("b p f -> p b f")

    def size(t):
        return min(P, CROWS - t * P)

    def bank(name):
        return banks[CRING.index(name) % CBANK]

    def made_in(name, g):
        if not isinstance(g, int):
            return True
        return g < CGROUPS - 1 if name in ("C0", "C1", "C2", "C3") else g >= 0

    def at(names, name, g):
        return (g + 1) * len(names) + names.index(name) + 1

    def steps(eng, step):
        step(-1)
        step(0)
        with eng.Fori(1, CGROUPS - 1) as g:
            step(g)
        step(CGROUPS - 1)

    with nc.Block() as block:
        @block.sync
        def _(sp):
            def load_rows(t, g):
                sp.dma_start(rows[0:size(t), t, :], ctx_rows[bass.ds(g * CROWS + t * P, size(t)), :]).then_inc(rows_loaded[t], 16)

            def load_piece(i):
                if i >= STAGES:
                    sp.wait_ge(w_lo, i - STAGES + 1)
                sp.dma_start(staged(i), pieces[i][0]).then_inc(w_loaded[i % STAGES], 16)

            for t in range(CTILES):
                load_rows(t, 0)
            for i in range(CC):
                load_piece(i)

            def step(g):
                for name in CRING:
                    if not made_in(name, g):
                        continue
                    if name[0] == "K" and name[2] == str(PAIRS - 1):
                        i = int(name[1])
                        sp.wait_ge(act_read, at(C_ACT, name, g))
                        sp.dma_start(keys_out[:, bass.ds(g * CG + i * CBATCHES, CBATCHES), :], keys[:, i, :, :]).then_inc(keys_stored[i], 16)
                    elif name[0] == "V" and name[2] == "1":
                        t = int(name[1])
                        sp.wait_ge(dve_read, at(C_DVE, name, g))
                        sp.dma_start(dram["values"][bass.ds(g * CROWS + t * P, size(t)), :], values[0:size(t), t, :]).then_inc(values_stored[t], 16)
                    elif name[0] == "C":
                        t = int(name[1])
                        ahead = 1 if name == "C4" else 2
                        if not isinstance(g, int) or g + ahead < CGROUPS:
                            sp.wait_ge(full, at(CRING, name, g))
                            load_rows(t, g + ahead)

            step(-1)
            for i in range(CC, len(pieces)):
                load_piece(i)
            for g in range(CGROUPS):
                step(g)
            for t in range(CTILES):
                sp.wait_ge(values_stored[t], 16 * CGROUPS)
            for i in range(CBLOCKS):
                sp.wait_ge(keys_stored[i], 16 * CGROUPS)

        @block.gpsimd
        def _(pool):
            pool.memset(ident[:, :], 0.0).then_inc(made, 1)
            pool.wait_ge(made, 1)
            pool.affine_select(out=ident[:, :], in_=ident[:, :], compare_op=ALU.not_equal, fill=1.0, base=0,
                               pattern=[[-1, P]], channel_multiplier=1).then_inc(made, 1)

        @block.scalar
        def _(act):
            skip, signal = counted(C_ACT, act_read)

            def split_high(i):
                _, dst, factor = pieces[i]
                act.wait_ge(w_loaded[i % STAGES], 16 * (i // STAGES + 1))
                act.activation(dst[0], staged(i), ACT.Copy, scale=factor).then_inc(w_hi, 1)

            def step(g):
                for name in C_ACT:
                    if not made_in(name, g):
                        skip()
                        continue
                    act.wait_ge(full, at(CRING, name, g))
                    ps = bank(name)
                    if name[0] == "K":
                        i, pair = int(name[1]), int(name[2])
                        if pair == 0 and not (isinstance(g, int) and g == 0):
                            act.wait_ge(keys_stored[i], 16 * g)
                        last = act.activation(keys[:, i, :, pair * M:(pair + 1) * M],
                                              ps[:, 0:CCOLS].rearrange("p (b m) -> p b m", m=M), ACT.Copy)
                    else:
                        t = int(name[1])
                        last = act.activation(ctxT[0][:, :, t * P:t * P + size(t)],
                                              ps[:, :].rearrange("p (c r) -> p c r", c=CC)[:, :, 0:size(t)], ACT.Copy)
                    signal(last)
                    if name == "C4" and isinstance(g, int) and g == 0:
                        for i in range(CC, 2 * CC):
                            split_high(i)

            step(-1)
            for i in range(CC):
                split_high(i)
            step(0)
            for i in range(2 * CC, len(pieces)):
                split_high(i)
            with act.Fori(1, CGROUPS - 1) as g:
                step(g)
            step(CGROUPS - 1)

        @block.vector
        def _(dve):
            skip, signal = counted(C_DVE, dve_read)

            def split_low(i):
                _, dst, factor = pieces[i]
                dve.wait_ge(w_hi, i + 1)
                dve.scalar_tensor_tensor(out=dst[1], in0=staged(i), scalar=factor, in1=dst[0].bitcast(F32),
                                         op0=ALU.mult, op1=ALU.subtract).then_inc(w_lo, 1)

            def step(g):
                for name in C_DVE:
                    if not made_in(name, g):
                        skip()
                        continue
                    ps, t = bank(name), int(name[1])
                    if name[0] == "C":
                        dve.wait_ge(act_read, at(C_ACT, name, g))
                        last = dve.tensor_tensor(ctxT[1][:, :, t * P:t * P + size(t)],
                                                 ps[:, :].rearrange("p (c r) -> p c r", c=CC)[:, :, 0:size(t)],
                                                 ctxT[0][:, :, t * P:t * P + size(t)].bitcast(F32), ALU.subtract)
                    else:
                        half = int(name[2])
                        dve.wait_ge(full, at(CRING, name, g))
                        if half == 0 and not (isinstance(g, int) and g == 0):
                            dve.wait_ge(values_stored[t], 16 * g)
                        last = dve.tensor_copy(values[0:size(t), t, half * 512:(half + 1) * 512], ps[0:size(t), :])
                    signal(last)
                    if name == "C4" and isinstance(g, int) and g == 0:
                        for i in range(CC, 2 * CC):
                            split_low(i)

            step(-1)
            for i in range(CC):
                split_low(i)
            step(0)
            for i in range(2 * CC, len(pieces)):
                split_low(i)
            with dve.Fori(1, CGROUPS - 1) as g:
                step(g)
            step(CGROUPS - 1)

        @block.tensor
        def _(pe):
            skip, signal = counted(CRING, full)

            def free(name, g):
                i, step = CRING.index(name) - CBANK, g
                while True:
                    if i < 0:
                        i, step = i + CTURN, step - 1
                    if isinstance(step, int) and step < -1:
                        return
                    if i < len(CRING) and made_in(CRING[i], step):
                        before = CRING[i]
                        if before[0] == "K":
                            pe.wait_ge(act_read, at(C_ACT, before, step))
                        else:
                            pe.wait_ge(dve_read, at(C_DVE, before, step))
                        return
                    i -= CBANK

            def step(g):
                for name in CRING:
                    if not made_in(name, g):
                        skip()
                        continue
                    free(name, g)
                    ps, i = bank(name), int(name[1])
                    if name[0] == "C":
                        ahead = 0 if name == "C4" else 1
                        pe.wait_ge(rows_loaded[i], 16 * (g + ahead + 1))
                        for c in range(CC):
                            last = pe.transpose(ps[:, c * P:c * P + size(i)], rows[0:size(i), i, c * P:(c + 1) * P],
                                                ident[0:size(i), 0:size(i)])
                    elif name[0] == "K":
                        if name[2] == "0":
                            pe.wait_ge(dve_read, at(C_DVE, "C4", g) if i else at(C_DVE, "C3", g - 1))
                        col = int(name[2]) * P
                        for c in range(CC):
                            last = split_product(pe, ps[:, 0:CCOLS], [w[:, c, col:col + P] for w in wkv],
                                                 [t[:, c, i * CCOLS:(i + 1) * CCOLS] for t in ctxT], c == 0, c == CC - 1)
                    else:
                        if name == "V00" and isinstance(g, int) and g == 0:
                            pe.wait_ge(w_lo, 2 * CC)
                        col = INNER + int(name[2]) * 512
                        for c in range(CC):
                            last = split_product(pe, ps[0:size(i), :], [t[:, c, i * P:i * P + size(i)] for t in ctxT],
                                                 [w[:, c, col:col + 512] for w in wkv], c == 0, c == CC - 1)
                    signal(last)

            pe.wait_ge(made, 2)
            step(-1)
            pe.wait_ge(w_lo, CC)
            step(0)
            with pe.Fori(1, CGROUPS - 1) as g:
                step(g)
            step(CGROUPS - 1)


def weight_views(w):
    return (w[:, 0:DC * I].rearrange("p (c i) -> p c i", c=DC), w[:, DC * I:2 * DC * I].rearrange("p (c i) -> p c i", c=DC),
            w[:, 2 * DC * I:EW])


def attention_phase(nc, ctx, dram, wq, wo, ahead):
    def sb(name, shape, dt=F32):
        return ctx.enter_context(nc.sbuf_tensor(name, shape, dt))

    def sem(name):
        return ctx.enter_context(nc.semaphore(name))

    ident = sb("ident", [P, P])
    scale_row = sb("scale_row", [P, D])
    bias_row = sb("bias_row", [P, D])
    gate = sb("gate", [P, 2])
    minus_half = sb("minus_half", [P, TT])
    eps_col = [sb(f"eps_col{i}", [P, TT]) for i in range(3)]
    null_k = sb("null_k", [P, 1])
    x_in = sb("x_in", [P, TT, D])
    x_res = sb("x_res", [P, TT, D])
    keys = sb("keys_raw", [P, PAIRS, 2 * J])
    values = sb("values_raw", [J, INNER])
    xn = sb("xn", [P, TT, D])
    xnT = [sb(f"xnT_{s}", [P, DC, N], F32R) for s in "hl"]
    kT = [sb(f"kT_{s}", [P, PAIRS, 2 * J], F32R) for s in "hl"]
    vv = [sb(f"v_{s}", [J, PAIRS, 3 * DH], F32R) for s in "hl"]
    qT = [sb(f"qT_{s}", [P, PAIRS, N], F32R) for s in "hl"]
    outT = [sb(f"outT_{s}", [P, PAIRS, N], F32R) for s in "hl"]
    probs = [sb(f"probs{i}", [P, PAIRS, J]) for i in range(2)]
    minus_max = [sb(f"minus_max{i}", [P, PAIRS]) for i in range(2)]
    row_sum = [sb(f"row_sum{i}", [P, PAIRS]) for i in range(2)]
    row_inv = [sb(f"row_inv{i}", [P, PAIRS]) for i in range(2)]
    stats = [sb(f"stats{i}", [P, TT, 6]) for i in range(3)]
    mean_var = [sb(f"mean_var{i}", [P, TT, 2]) for i in range(3)]
    var_eps = [sb(f"var_eps{i}", [P, TT]) for i in range(3)]
    rstd = [sb(f"rstd{i}", [P, TT]) for i in range(3)]
    minus_mean = sb("minus_mean", [P, TT])
    shift = sb("shift", [P, TT])
    z = sb("z", [P, TT, D])
    x1 = sb("x1", [P, TT, D])
    xn2 = sb("xn2", [P, TT, D])
    x2T = [sb(f"x2T_{s}", [P, DC, N], F32R) for s in "hl"]
    router = sb("router_raw", [P, DC, ROUTED])
    router_w = sb("router_split", [P, DC, 2, ROUTED], F32R)
    router_bias = sb("router_bias", [P, ROUTED])
    routing = sb("routing", [P, TT, 2, ROUTED])
    pT = [sb(f"pT_{s}", [J, PAIRS, N], F32R) for s in "hl"]

    sim = [ctx.enter_context(nc.psum_tensor(f"sim{i}", [P, 2, 512], F32)) for i in range(2)]
    ring = [ctx.enter_context(nc.psum_tensor(f"ring{i}", [P, 512], F32)) for i in range(NBANK)]

    const_loaded, null_k_loaded, zeroed, made = sem("const_loaded"), sem("null_k_loaded"), sem("zeroed"), sem("made")
    null_key_placed, null_value_placed = sem("null_key_placed"), sem("null_value_placed")
    gate_ready, rows_ready = sem("gate_ready"), sem("rows_ready")
    x_loaded, res_loaded = sem("x_loaded"), sem("res_loaded")
    keys_loaded, keys_hi, keys_lo = sem("keys_loaded"), sem("keys_hi"), sem("keys_lo")
    values_loaded, values_hi, values_lo = sem("values_loaded"), sem("values_hi"), sem("values_lo")
    x1_stored, x2_stored, routing_stored = sem("x1_stored"), sem("x2_stored"), sem("routing_stored")
    biased, minus_mean_done, shift_done = sem("biased"), sem("minus_mean_done"), sem("shift_done")
    ahead_loaded, shared_hi = sem("ahead_loaded"), sem("shared_hi")
    router_hi, router_lo, routing_ready = sem("router_hi"), sem("router_lo"), sem("routing_ready")
    ring_full, ring_hi, ring_lo = sem("ring_full"), sem("ring_hi"), sem("ring_lo")
    sim_full, max_done, exp_done = sem("sim_full"), sem("max_done"), sem("exp_done")
    sum_done, inv_done, probs_ready = sem("sum_done"), sem("inv_done"), sem("probs_ready")
    stats_done = [sem(f"stats_done{i}") for i in range(3)]
    var_done = [sem(f"var_done{i}") for i in range(3)]
    eps_done = [sem(f"eps_done{i}") for i in range(3)]
    rstd_done = [sem(f"rstd_done{i}") for i in range(3)]
    applied = [sem(f"applied{i}") for i in range(3)]
    scaled, shifted, summed = sem("scaled"), sem("shifted"), sem("summed")

    x_tiles = dram["x"].rearrange("b (t p) d -> b p t d", p=P)
    x1_tiles = dram["x1"].rearrange("(b t p) d -> b p t d", t=TT, p=P)
    x2_cols = [dram[f"x2T_{s}"].rearrange("c p n -> p c n") for s in "hl"]
    routing_tiles = dram["routing"].rearrange("(b t p) e -> b p t e", t=TT, p=P)

    def bank(name):
        return ring[RING.index(name) % NBANK]

    def scores(u):
        return sim[u % 2][:, :, 0:4 * J].rearrange("p a (h j) -> p a h j", j=J)

    def destinations(name):
        ps = bank(name)
        if name == "X":
            return [(ps[:, :].rearrange("p (c n) -> p c n", c=DC), [t[:, :, :] for t in xnT])]
        if name == "N2":
            return [(ps[:, :].rearrange("p (c n) -> p c n", c=DC), [t[:, :, :] for t in x2T])]
        if name[0] == "T":
            tt, first = int(name[1]) % 2, 4 * "ab".index(name[2])
            return [(ps[0:J, :].rearrange("p (h n) -> p h n", h=4),
                     [t[:, first:first + 4, tt * P:(tt + 1) * P] for t in pT])]
        if name[0] == "Q":
            q = 2 * int(name[1])
            return [(ps[:, :].rearrange("p (h n) -> p h n", h=2), [t[:, q:q + 2, :] for t in qT])]
        q = HP * int(name[2]) + 2 * "ab".index(name[3])
        return [(ps[:, :].rearrange("p (h n) -> p h n", h=2), [t[:, q:q + 2, :] for t in outT])]

    def value_part(part):
        return vv[part][:, :, :].rearrange("p h (s d) -> p h s d", d=DH)[:, :, 0:3:2, :]

    values_by_head = values[:, :].rearrange("p (h s d) -> p h s d", s=2, d=DH)

    with nc.Block() as block:
        @block.sync
        def _(sp):
            sp.dma_start(x_in[:, :, :], x_tiles[0]).then_inc(x_loaded, 16)

            def load_keys(batch):
                for half, col in ((slice(0, DH), 0), (slice(DH, P), J)):
                    sp.dma_start(keys[half, :, col:col + M],
                                 dram["keys"].rearrange("b p (h m) -> b p h m", m=M)[batch, half]).then_inc(keys_loaded, 16)

            def load_values(batch):
                sp.dma_start(values[0:M, :], dram["values"][bass.ds(batch * M, M), :]).then_inc(values_loaded, 16)

            with nc.allow_non_contiguous_dma(reason="one column of 64 elements"):
                for half in (slice(0, DH), slice(DH, P)):
                    sp.dma_start(null_k[half, :], dram["null_kv"][0:1, :].rearrange("a d -> d a")).then_inc(null_k_loaded, 16)
            load_values(0)
            sp.dma_start(values[M:J, :].rearrange("p (h d) -> p h d", d=DH),
                         dram["null_kv"][1:2, :].unsqueeze(1).broadcast_to([1, HEADS, DH])).then_inc(null_value_placed, 16)
            sp.wait_ge(zeroed, 1)
            load_keys(0)
            sp.dma_start(gate[:, 0:1], dram["g_xattn"].unsqueeze(0).broadcast_to([P, 1])).then_inc(const_loaded, 16)
            sp.dma_start(scale_row[:, :], dram["ln_scale"].unsqueeze(0).broadcast_to([P, D])).then_inc(const_loaded, 16)
            sp.dma_start(bias_row[:, :], dram["ln_bias"].unsqueeze(0).broadcast_to([P, D])).then_inc(const_loaded, 16)
            sp.dma_start(router[:, :, :], dram["Wr"].rearrange("(c p) e -> p c e", p=P)).then_inc(const_loaded, 16)
            sp.dma_start(router_bias[:, :], dram["br"].unsqueeze(0).broadcast_to([P, ROUTED])).then_inc(const_loaded, 16)

            def load_ahead():
                sp.wait_ge(x2_stored, 32 * (GT // N))
                for cols, part in zip(x2_cols, ahead["xT"]):
                    sp.dma_start(part[:, :, :].bitcast(F32), cols[:, :, 0:GT]).then_inc(ahead_loaded, 16)
                sp.wait_ge(routing_stored, 16 * (GT // N))
                sp.dma_start(ahead["routing"][:, :, :, :],
                             dram["routing"][0:GT].rearrange("(t p) (a e) -> p t a e", p=P, a=2)).then_inc(ahead_loaded, 16)
                for dst, name in zip(weight_views(ahead["shared"]), ("Wg_s", "Wu_s", "Wd_s")):
                    src = dram[name] if name == "Wd_s" else dram[name].rearrange("(c p) i -> p c i", p=P)
                    sp.dma_start(dst, src).then_inc(ahead_loaded, 16)
                sp.dma_start(ahead["gate"][:, 0:1], dram["g_ffn"].unsqueeze(0).broadcast_to([P, 1])).then_inc(ahead_loaded, 16)
                for rows, routed, shared in (("gate_bias_rows", "bg", "bg_s"), ("up_bias_rows", "bu", "bu_s"), ("down_bias_rows", "bd", "bd_s")):
                    sp.dma_start(ahead[rows][0:ROUTED, :], dram[routed]).then_inc(ahead_loaded, 16)
                    sp.dma_start(ahead[rows][ROUTED:, :], dram[shared].unsqueeze(0)).then_inc(ahead_loaded, 16)

            def step(b):
                if isinstance(b, int) and b == B - 2:
                    load_ahead()
                if within(b, -1, B - 3):
                    sp.wait_ge(applied[0], b + 2)
                    sp.dma_start(x_in[:, :, :], x_tiles[b + 2]).then_inc(x_loaded, 16)
                if within(b, 0, B - 2):
                    sp.wait_ge(values_lo, b + 1)
                    load_values(b + 1)
                if within(b, 2, B + 1):
                    sp.wait_ge(ring_lo, nth(LO, "N2", b))
                    for cols, part in zip(x2_cols, x2T):
                        sp.dma_start(cols[:, :, bass.ds((b - 2) * N, N)], part[:, :, :].bitcast(F32)).then_inc(x2_stored, 16)
                if within(b, 1, B):
                    sp.wait_ge(summed, b)
                    sp.dma_start(x1_tiles[b - 1], x1[:, :, :]).then_inc(x1_stored, 16)
                if within(b, 0, B - 1):
                    sp.dma_start(x_res[:, :, :], x_tiles[b]).then_inc(res_loaded, 16)
                if within(b, -1, B - 3):
                    sp.wait_ge(keys_lo, b + 2)
                    load_keys(b + 2)
                if within(b, 2, B + 1):
                    sp.wait_ge(routing_ready, b - 1)
                    sp.dma_start(routing_tiles[b - 2], routing[:, :, :, :].rearrange("p t a e -> p t (a e)")).then_inc(routing_stored, 16)

            iterations(sp, step)
            sp.wait_ge(x1_stored, 16 * B)
            sp.wait_ge(x2_stored, 32 * B)
            sp.wait_ge(routing_stored, 16 * B)
            sp.wait_ge(ahead_loaded, 208)

        @block.gpsimd
        def _(pool):
            pool.memset(ident[:, :], 0.0).then_inc(made, 1)
            pool.memset(minus_half[:, :], -0.5).then_inc(made, 1)
            for i, eps in enumerate((LN_EPS, OUT_EPS, LN_EPS)):
                pool.memset(eps_col[i][:, :], eps).then_inc(made, 1)
            pool.wait_ge(made, 5)
            pool.affine_select(out=ident[:, :], in_=ident[:, :], compare_op=ALU.not_equal, fill=1.0, base=0,
                               pattern=[[-1, P]], channel_multiplier=1).then_inc(made, 1)
            def prepare():
                for t in (keys[:, :, :], *(v[:, :, :].bitcast(F32) for v in vv)):
                    last = pool.memset(t, 0.0)
                last.then_inc(zeroed, 1)

            def make_rstd(i, batch):
                pool.wait_ge(var_done[i], batch + 1)
                pool.tensor_tensor(var_eps[i][:, :], mean_var[i][:, :, 1], eps_col[i][:, :], ALU.add).then_inc(eps_done[i], 1)
                pool.wait_ge(eps_done[i], batch + 1)
                pool.tensor_tensor(rstd[i][:, :], var_eps[i][:, :], minus_half[:, :], ALU.pow).then_inc(rstd_done[i], 1)

            def normalise(u, b):
                pool.wait_ge(inv_done, 4 * b + u + 1)
                e = probs[u % 2]
                pool.tensor_tensor(e[:, :, :], e[:, :, :], row_inv[u % 2][:, :].unsqueeze(2).broadcast_to([P, PAIRS, J]),
                                   ALU.mult).then_inc(probs_ready, 1)

            def step(b):
                if within(b, 0, B - 1):
                    pool.wait_ge(values_hi, b + 1)
                    pool.tensor_tensor(value_part(1), values_by_head, value_part(0).bitcast(F32), ALU.subtract).then_inc(values_lo, 1)
                    normalise(0, b)
                    normalise(1, b)
                if within(b, 1, B):
                    make_rstd(1, b - 1)
                    pool.wait_ge(minus_mean_done, b)
                    pool.wait_ge(rstd_done[1], b)
                    pool.tensor_tensor(shift[:, :], minus_mean[:, :], rstd[1][:, :], ALU.mult).then_inc(shift_done, 1)
                    pool.wait_ge(res_loaded, 16 * b)
                    if isinstance(b, int) and b == 1:
                        pool.wait_ge(rows_ready, 2)
                    if within(b, 2, B):
                        pool.wait_ge(x1_stored, 16 * (b - 1))
                        pool.wait_ge(applied[2], b - 1)
                    pool.tensor_tensor(x1[:, :, :], x_res[:, :, :], bias_row[:, :].unsqueeze(1).broadcast_to([P, TT, D]),
                                       ALU.add).then_inc(shifted, 1)
                    pool.wait_ge(applied[1], b)
                    pool.tensor_tensor(z[:, :, :], z[:, :, :], scale_row[:, :].unsqueeze(1).broadcast_to([P, TT, D]),
                                       ALU.mult).then_inc(scaled, 1)
                    pool.wait_ge(scaled, b)
                    pool.wait_ge(shifted, b)
                    pool.tensor_tensor(x1[:, :, :], x1[:, :, :], z[:, :, :], ALU.add).then_inc(summed, 1)
                if within(b, 0, B - 1):
                    normalise(2, b)
                    normalise(3, b)
                if within(b, -1, B - 2):
                    pool.wait_ge(keys_hi, b + 2)
                    pool.tensor_tensor(kT[1][:, :, :], keys[:, :, :], kT[0][:, :, :].bitcast(F32), ALU.subtract).then_inc(keys_lo, 1)
                if within(b, 1, B):
                    make_rstd(2, b - 1)
                if within(b, -2, B - 3):
                    if within(b, -2, -2):
                        pool.wait_ge(made, 6)
                    make_rstd(0, b + 2)

            iterations(pool, step, prepare)

        @block.scalar
        def _(act):
            skip, signal = counted(HI, ring_hi)

            def place_null_key():
                act.wait_ge(null_k_loaded, 32)
                act.wait_ge(zeroed, 1)
                act.activation(keys[0:DH, :, M], null_k[0:DH, 0:1].broadcast_to([DH, PAIRS]), ACT.Copy).then_inc(null_key_placed, 1)
                act.activation(keys[DH:P, :, J + M], null_k[DH:P, 0:1].broadcast_to([DH, PAIRS]), ACT.Copy).then_inc(null_key_placed, 1)
                act.wait_ge(null_key_placed, 2)
                act.wait_ge(null_value_placed, 16)

            def prepare():
                act.wait_ge(const_loaded, 80)
                act.activation(gate[:, 1:2], gate[:, 0:1], ACT.Tanh).then_inc(gate_ready, 1)
                act.activation(router_w[:, :, 0, :], router[:, :, :], ACT.Copy).then_inc(router_hi, 1)

            def exp(u, b):
                act.wait_ge(max_done, 4 * b + u + 1)
                if u >= 2:
                    act.wait_ge(ring_full, nth(RING, f"T{u - 2}b", b))
                elif within(b, 1, B):
                    act.wait_ge(ring_full, nth(RING, f"T{u + 2}b", b - 1))
                for h in range(PAIRS):
                    last = act.activation(probs[u % 2][:, h, :], scores(u)[:, h // 4, h % 4, :], ACT.Exp,
                                          bias=minus_max[u % 2][:, h:h + 1])
                last.then_inc(exp_done, 1)

            def high(name, b):
                if not runs(name, b):
                    return skip()
                act.wait_ge(ring_full, nth(RING, name, b))
                if name == "N2" and within(b, 3, B + 1):
                    act.wait_ge(x2_stored, 32 * (b - 2))
                for src, dst in destinations(name):
                    last = act.activation(dst[0], src, ACT.Copy)
                signal(last)

            def step(b):
                here = within(b, 0, B - 1)
                if isinstance(b, int) and b == 0:
                    prepare()
                if isinstance(b, int) and b == B + 1:
                    act.wait_ge(ahead_loaded, 208)
                    act.activation(ahead["shared_split"][0][:, :], ahead["shared"][:, :], ACT.Copy).then_inc(shared_hi, 1)
                if here:
                    act.wait_ge(values_loaded, 16 * (b + 1))
                    if within(b, 1, B):
                        act.wait_ge(ring_full, nth(RING, "PV1b", b - 1))
                    act.activation(value_part(0), values_by_head, ACT.Copy).then_inc(values_hi, 1)
                    exp(0, b)
                    exp(1, b)
                for name in HI:
                    if within(b, -1, B + 1):
                        high(name, b)
                    if name == "X" and within(b, 1, B):
                        act.wait_ge(shift_done, b)
                        if within(b, 2, B):
                            act.wait_ge(summed, b - 1)
                        for t in range(TT):
                            last = act.activation(z[:, t, :], bank("O")[:, t * D:(t + 1) * D], ACT.Identity,
                                                  bias=shift[:, t:t + 1], scale=rstd[1][:, t:t + 1])
                        last.then_inc(applied[1], 1)
                    if name == "T1b" and here:
                        exp(2, b)
                    if name == "Q0" and here:
                        exp(3, b)
                    if name == "PV0b" and within(b, -1, B - 2):
                        if within(b, -1, -1) and isinstance(b, int):
                            place_null_key()
                        act.wait_ge(keys_loaded, 32 * (b + 2))
                        if within(b, 0, B):
                            act.wait_ge(sim_full, 4 * b + 4)
                        act.activation(kT[0][:, :, :], keys[:, :, :], ACT.Copy).then_inc(keys_hi, 1)
                    if name == "Q1" and within(b, 2, B + 1):
                        act.wait_ge(ring_lo, nth(LO, "L", b))
                        act.activation(routing[:, :, 1, :], routing[:, :, 0, :], ACT.Exp, scale=-1.0).then_inc(routing_ready, 1)

            iterations(act, step)

        @block.vector
        def _(dve):
            skip, signal = counted(LO, ring_lo)

            def prepare():
                dve.wait_ge(gate_ready, 1)
                for row in (scale_row, bias_row):
                    dve.tensor_scalar(row[:, :], row[:, :], gate[:, 1:2], None, ALU.mult).then_inc(rows_ready, 1)
                dve.wait_ge(router_hi, 1)
                dve.tensor_tensor(router_w[:, :, 1, :], router[:, :, :], router_w[:, :, 0, :].bitcast(F32), ALU.subtract).then_inc(router_lo, 1)

            def maximum(u, b):
                dve.wait_ge(sim_full, 4 * b + u + 1)
                dve.tensor_reduce(minus_max[u % 2][:, :].rearrange("p (a h) -> p a h", a=2), scores(u), AX.X,
                                  ALU.max, negate=True).then_inc(max_done, 1)

            def invert(u, b):
                n = 4 * b + u
                dve.wait_ge(exp_done, n + 1)
                dve.tensor_reduce(row_sum[u % 2][:, :], probs[u % 2][:, :, :], AX.X, ALU.add).then_inc(sum_done, 1)
                dve.wait_ge(sum_done, n + 1)
                if within(b, 1, B) or u >= 2:
                    dve.wait_ge(probs_ready, n - 1)
                dve.reciprocal(row_inv[u % 2][:, :], row_sum[u % 2][:, :]).then_inc(inv_done, 1)

            def statistics(i, src, batch, first):
                if not first:
                    dve.wait_ge(applied[i], batch)
                for t in range(TT):
                    last = dve.bn_stats(stats[i][:, t, :], src(t))
                last.then_inc(stats_done[i], 1)
                dve.wait_ge(made, 6)
                dve.wait_ge(stats_done[i], batch + 1)
                for t in range(TT):
                    last = dve.bn_aggr(mean_var[i][:, t, :], stats[i][:, t, :])
                last.then_inc(var_done[i], 1)

            def apply(i, out, src, batch):
                dve.wait_ge(rstd_done[i], batch + 1)
                for t in range(TT):
                    last = dve.tensor_scalar(out[:, t, :], src(t), mean_var[i][:, t, 0:1], rstd[i][:, t:t + 1],
                                             ALU.subtract, ALU.mult)
                return last.then_inc(applied[i], 1)

            def from_o(t):
                return bank("O")[:, t * D:(t + 1) * D]

            def low(name, b):
                if not runs(name, b):
                    return skip()
                if name == "L":
                    dve.wait_ge(ring_full, nth(RING, name, b))
                    if within(b, 3, B + 1):
                        dve.wait_ge(routing_stored, 16 * (b - 2))
                    parts = bank(name)[:, 0:2 * TT * ROUTED].rearrange("p (t a e) -> p a t e", t=TT, a=2)
                    dve.tensor_tensor(routing[:, :, 0, :], parts[:, 0], router_bias[:, :].unsqueeze(1).broadcast_to([P, TT, ROUTED]),
                                      ALU.add).then_inc(biased, 1)
                    dve.wait_ge(biased, b - 1)
                    return signal(dve.tensor_tensor(routing[:, :, 0, :], parts[:, 1], routing[:, :, 0, :], ALU.add))
                dve.wait_ge(ring_hi, nth(HI, name, b))
                for src, dst in destinations(name):
                    last = dve.tensor_tensor(dst[1], src, dst[0].bitcast(F32), ALU.subtract)
                signal(last)

            def step(b):
                here = within(b, 0, B - 1)
                if isinstance(b, int) and b == 0:
                    prepare()
                if isinstance(b, int) and b == B + 1:
                    dve.wait_ge(shared_hi, 1)
                    dve.tensor_tensor(ahead["shared_split"][1][:, :], ahead["shared"][:, :],
                                      ahead["shared_split"][0][:, :].bitcast(F32), ALU.subtract)
                if here:
                    maximum(0, b)
                    maximum(1, b)
                if within(b, -1, B - 2):
                    if within(b, 0, B - 2):
                        dve.wait_ge(ring_full, nth(RING, "X", b - 1))
                    apply(0, xn, lambda t: x_in[:, t, :], b + 1)
                if here:
                    invert(0, b)
                    invert(1, b)
                if within(b, -1, B + 1):
                    low("N2", b)
                if within(b, 1, B):
                    dve.wait_ge(ring_full, nth(RING, "O", b))
                    statistics(1, from_o, b - 1, isinstance(b, int) and b == 1)
                    dve.wait_ge(var_done[1], b)
                    dve.tensor_scalar(minus_mean[:, :], mean_var[1][:, :, 0], -1.0, None, ALU.mult).then_inc(minus_mean_done, 1)
                for name in LO[1:]:
                    if within(b, -1, B + 1):
                        low(name, b)
                    if name == "T0a" and here:
                        maximum(2, b)
                    if name == "T0b" and here:
                        maximum(3, b)
                    if name == "Q0" and here:
                        invert(2, b)
                    if name == "Q1" and here:
                        invert(3, b)
                    if name == "T3b" and within(b, 1, B):
                        dve.wait_ge(summed, b)
                        statistics(2, lambda t: x1[:, t, :], b - 1, isinstance(b, int) and b == 1)
                    if name == "PV1a" and within(b, -2, B - 3):
                        dve.wait_ge(x_loaded, 16 * (b + 3))
                        statistics(0, lambda t: x_in[:, t, :], b + 2, isinstance(b, int) and b == -2)
                    if name == "PV1b" and within(b, 1, B):
                        if within(b, 2, B):
                            dve.wait_ge(ring_full, nth(RING, "N2", b))
                        apply(2, xn2, lambda t: x1[:, t, :], b - 1)

            iterations(dve, step)

        @block.tensor
        def _(pe):
            skip, signal = counted(RING, ring_full)

            def similarity(u, b):
                n = 4 * b + u
                pe.wait_ge(ring_lo, nth(LO, "Q3", b - 1))
                pe.wait_ge(keys_lo, b + 1)
                if within(b, 1, B) or u >= 2:
                    pe.wait_ge(exp_done, n - 1)
                tt, half = u % 2, u // 2
                for i in range(HP):
                    pair = half * HP + i
                    last = split_product(pe, sim[u % 2][:, i // 2, (i % 2) * 2 * J:(i % 2 + 1) * 2 * J],
                                         [t[:, pair, tt * P:(tt + 1) * P] for t in qT], [t[:, pair, :] for t in kT])
                last.then_inc(sim_full, 1)

            def accumulate(out, products):
                for k, (left, right) in enumerate(products):
                    last = split_product(pe, out, left, right, start=k == 0, stop=k == len(products) - 1)
                return last

            def output(name, b):
                if not runs(name, b):
                    return skip()
                i, at = RING.index(name) - NBANK, b
                while True:
                    if i < 0:
                        i, at = i + len(RING), at - 1
                    if runs(RING[i], at):
                        before = RING[i]
                        if before == "O":
                            pe.wait_ge(applied[1], at)
                        else:
                            pe.wait_ge(ring_lo, nth(LO, before, at))
                        break
                    i -= NBANK
                    if isinstance(at, int) and at < -1:
                        break
                ps = bank(name)
                if name == "X":
                    pe.wait_ge(applied[0], b + 2)
                    for c in range(DC):
                        for t in range(TT):
                            last = pe.transpose(ps[:, c * N + t * P:c * N + (t + 1) * P], xn[:, t, c * P:(c + 1) * P], ident[:, :])
                elif name[0] == "T":
                    u, first = int(name[1]), 4 * "ab".index(name[2])
                    pe.wait_ge(probs_ready, 4 * b + u + 1)
                    for h in range(4):
                        last = pe.transpose(ps[0:J, h * P:(h + 1) * P], probs[u % 2][:, first + h, :], ident[:, :])
                elif name[0] == "Q":
                    pe.wait_ge(ring_lo, nth(LO, "X", b))
                    for i in range(2):
                        col = (2 * int(name[1]) + i) * P
                        last = accumulate(ps[:, i * N:(i + 1) * N],
                                          [([w[:, c, col:col + P] for w in wq], [t[:, c, :] for t in xnT]) for c in range(DC)])
                elif name[0] == "P":
                    half = int(name[2])
                    pe.wait_ge(values_lo, b + 1)
                    pe.wait_ge(ring_lo, nth(LO, f"T{2 * half + 1}b", b))
                    for i in range(2):
                        local = 2 * "ab".index(name[3]) + i
                        last = accumulate(ps[:, i * N:(i + 1) * N],
                                          [([t[:, half * HP + local, s * DH:s * DH + P] for t in vv],
                                            [t[:, 2 * local + s, :] for t in pT]) for s in range(2)])
                elif name == "O":
                    pe.wait_ge(ring_lo, nth(LO, "PV1b", b - 1))
                    for t in range(TT):
                        last = accumulate(ps[:, t * D:(t + 1) * D],
                                          [([o[:, q, t * P:(t + 1) * P] for o in outT], [w[:, q, :] for w in wo]) for q in range(PAIRS)])
                elif name == "L":
                    if isinstance(b, int) and b == 2:
                        pe.wait_ge(router_lo, 1)
                    pe.wait_ge(ring_lo, nth(LO, "N2", b))
                    for t in range(TT):
                        out = ps[:, 2 * t * ROUTED:2 * (t + 1) * ROUTED]
                        for c in range(DC):
                            pe.matmul(out, x2T[0][:, c, t * P:(t + 1) * P], router_w[:, c, :, :].rearrange("p a e -> p (a e)"),
                                      start=c == 0, stop=False)
                        for c in range(DC):
                            last = pe.matmul(out[:, 0:ROUTED], x2T[1][:, c, t * P:(t + 1) * P], router_w[:, c, 0, :],
                                             start=False, stop=c == DC - 1)
                else:
                    pe.wait_ge(applied[2], b - 1)
                    for c in range(DC):
                        for t in range(TT):
                            last = pe.transpose(ps[:, c * N + t * P:c * N + (t + 1) * P], xn2[:, t, c * P:(c + 1) * P], ident[:, :])
                signal(last)

            pe.wait_ge(made, 6)

            def step(b):
                here = within(b, 0, B - 1)
                if here:
                    similarity(0, b)
                    similarity(1, b)
                for name in RING:
                    if within(b, -1, B + 1):
                        output(name, b)
                    if name == "T0a" and here:
                        similarity(2, b)
                        similarity(3, b)

            iterations(pe, step)


def expert_phase(nc, ctx, dram, ahead):
    def sb(name, shape, dt=F32):
        return ctx.enter_context(nc.sbuf_tensor(name, shape, dt))

    def sem(name):
        return ctx.enter_context(nc.semaphore(name))

    groups = T // GT
    ident = sb("ident2", [ROUTED + 1, ROUTED + 1])
    gate = ahead["gate"]
    bias_rows = [ahead["gate_bias_rows"], ahead["up_bias_rows"]]
    bias_cols = [sb(f"{n}_bias_cols", [P, ROUTED + 1]) for n in ("gate", "up")]
    gate_bias = sb("gate_bias", [P, SLOTS])
    down_bias_raw = ahead["down_bias_rows"]
    down_bias = [sb(f"down_bias_{s}", [ROUTED + 1, D], F32R) for s in "hl"]
    w_raw = [sb(f"w_raw{i}", [P, EW]) for i in range(SLOTS)]
    w_split = [[sb(f"w{i}_{s}", [P, EW], F32R) for s in "hl"] for i in range(SLOTS)] + [ahead["shared_split"]]
    xT = ahead["xT"]
    x1 = sb("x1_rows", [P, GTILES, D])
    routing = ahead["routing"]
    divisor = sb("divisor", [P, GTILES, ROUTED])
    affinity = sb("affinity", [P, GTILES, ROUTED])
    top = sb("top", [P, GTILES, TOPK])
    without_top = sb("without_top", [P, GTILES, ROUTED])
    chosen = sb("chosen", [P, GTILES, ROUTED])
    weight = sb("weight", [P, GTILES, ROUTED])
    total = sb("total", [P, GTILES])
    total_inv = sb("total_inv", [P, GTILES])
    weight_blocks = sb("weight_blocks", [P, GTILES, ROUTED])
    weightT = sb("weightT", [ROUTED, GT])
    weightT_split = [sb(f"weightT_{s}", [ROUTED + 1, GT], F32R) for s in "hl"]
    zeros = sb("zeros", [1, 2 * D], F32R)
    weight_rows = [sb(f"weight_rows{i}", [1, 2, GT]) for i in range(2)]
    spread = [sb(f"spread{i}", [P, GT]) for i in range(2)]
    act_gate = [sb(f"act_gate{i}", [P, BLK]) for i in range(2)]
    hidden = [sb(f"hidden{i}", [P, BLK]) for i in range(2)]
    hid = [[sb(f"hid{i}_{s}", [P, BLK], F32R) for s in "hl"] for i in range(2)]

    acc = ctx.enter_context(nc.psum_tensor("acc", [P, 4, 2, D], F32))
    gu = [[ctx.enter_context(nc.psum_tensor(f"{n}{i}", [P, BLK], F32)) for n in ("gate_ps", "up_ps")] for i in range(2)]
    per_slot = ROUTED // SLOTS

    made, gate_ready = sem("made2"), sem("gate2_ready")
    const_hi, const_lo, bias_turned, bias_ready, gate_bias_ready = (
        sem(n) for n in ("const_hi", "const_lo", "bias_turned", "bias_ready", "gate_bias_ready"))
    w_loaded = [sem(f"w2_loaded{i}") for i in range(SLOTS)]
    w_hi, w_lo = sem("w2_hi"), sem("w2_lo")
    xT_loaded = [sem(f"xT_loaded{k}") for k in range(NB)]
    x1_loaded = sem("x1_loaded")
    routing_loaded, top_ready, divisor_ready, affinity_ready = (
        sem(n) for n in ("routing_loaded", "top_ready", "divisor_ready", "affinity_ready"))
    removed, chosen_ready, picked, total_ready, total_safe, inv_ready, weight_ready = (
        sem(n) for n in ("removed", "chosen_ready", "picked", "total_ready", "total_safe", "inv_ready", "weight_ready"))
    blocks_turned, weightT_stored, weightT_loaded, weightT_hi, weightT_lo = (
        sem(n) for n in ("blocks_turned", "weightT_stored", "weightT_loaded", "weightT_hi", "weightT_lo"))
    rows_loaded = [sem(f"rows_loaded{i}") for i in range(2)]
    spread_ready = sem("spread_ready")
    gate_full, up_full, silu_done, weighted, hidden_ready, hid_hi, hid_lo, down_done = (
        sem(n) for n in ("gate_full", "up_full", "silu_done", "weighted", "hidden_ready", "hid_hi", "hid_lo", "down_done"))
    acc_full, out_ready, out_stored = sem("acc_full"), sem("out_ready"), sem("out_stored")

    def step_index(g, e, k):
        return g * STEPS + e * NB + k

    x2_cols = [dram[f"x2T_{s}"].rearrange("c p n -> p c n") for s in "hl"]
    routing_tiles = dram["routing"].rearrange("(g t p) (a e) -> g p t a e", t=GTILES, p=P, a=2)
    x1_tiles = dram["x1"].rearrange("(g t p) d -> g p t d", t=GTILES, p=P)
    out_tiles = dram["out"].rearrange("b (s p) d -> p (b s) d", p=P)

    with nc.Block() as block:
        def over_groups(eng, group):
            group(0)
            with eng.Fori(1, groups - 1) as g:
                group(g)
            group(groups - 1)

        def is_first(g):
            return isinstance(g, int) and g == 0

        def is_last(g):
            return isinstance(g, int) and g == groups - 1

        @block.sync
        def _(sp):
            def load_expert(e, slot):
                for dst, name in zip(weight_views(w_raw[slot]), ("Wg", "Wu", "Wd")):
                    src = dram[name] if name == "Wd" else dram[name].rearrange("e (c p) i -> e p c i", p=P)
                    sp.dma_start(dst, src[e]).then_inc(w_loaded[slot], 16)

            def load_xT(g, k):
                for cols, part in zip(x2_cols, xT):
                    sp.dma_start(part[:, :, k * BLK:(k + 1) * BLK].bitcast(F32),
                                 cols[:, :, bass.ds(g * GT + k * BLK, BLK)]).then_inc(xT_loaded[k], 16)

            def load_routing(g):
                sp.dma_start(routing[:, :, :, :], routing_tiles[g]).then_inc(routing_loaded, 16)

            def turn_weights(g):
                sp.wait_ge(blocks_turned, g + 1)
                columns = dram["weightT"][:, bass.ds(g * GT, GT)].rearrange("e (t q n) -> q e t n", t=GTILES, n=ROUTED)
                for q in range(P // ROUTED):
                    sp.dma_start(columns[q], weight_blocks[q * ROUTED:(q + 1) * ROUTED, :, :]).then_inc(weightT_stored, 16)
                sp.wait_ge(weightT_stored, 64 * (g + 1))
                if not is_first(g):
                    sp.wait_ge(weightT_lo, g)
                sp.dma_start(weightT[:, :], dram["weightT"][:, bass.ds(g * GT, GT)]).then_inc(weightT_loaded, 16)

            def load_rows(g, j):
                for half in range(2):
                    if not (is_first(g) and isinstance(j, int)):
                        sp.wait_ge(spread_ready, g * ROUTED + SLOTS * j + 2 * half - 2)
                    sp.dma_start(weight_rows[half][:, :, :],
                                 dram["weightT"][bass.ds(SLOTS * j + 2 * half, 2), bass.ds(g * GT, GT)].unsqueeze(0)
                                 ).then_inc(rows_loaded[half], 16)

            def reload(g, j, e0):
                for q in range(SLOTS):
                    sp.wait_ge(w_hi, g * ROUTED + SLOTS * j + q + 1)
                    sp.wait_ge(w_lo, g * ROUTED + SLOTS * j + q + 1)
                    load_expert(e0 + q, q)

            def group(g):
                if not is_first(g):
                    sp.wait_ge(out_stored, 64 * g)
                sp.dma_start(x1[:, :, :], x1_tiles[g]).then_inc(x1_loaded, 16)
                if not is_last(g):
                    sp.wait_ge(weight_ready, g + 1)
                    load_routing(g + 1)
                with sp.Fori(1, per_slot) as j:
                    reload(g, j - 1, SLOTS * j)
                    load_rows(g, j)
                if not is_last(g):
                    turn_weights(g + 1)
                reload(g, per_slot - 1, 0)
                if not is_last(g):
                    load_rows(g + 1, 0)
                    for k in range(NB):
                        sp.wait_ge(up_full, step_index(g, ROUTED, k) + 1)
                        load_xT(g + 1, k)
                for i in range(4):
                    sp.wait_ge(out_ready, 4 * g + i + 1)
                    sp.dma_start(out_tiles[:, bass.ds(g * GTILES + 2 * i, 2), :], x1[:, 2 * i:2 * i + 2, :]).then_inc(out_stored, 16)

            load_expert(0, 0)
            load_expert(1, 1)
            turn_weights(0)
            load_rows(0, 0)
            load_expert(2, 2)
            load_expert(3, 3)
            over_groups(sp, group)
            sp.wait_ge(out_stored, 64 * groups)
            for slot in range(SLOTS):
                sp.wait_ge(w_loaded[slot], 48 * (groups * per_slot + 1))

        @block.gpsimd
        def _(pool):
            pool.memset(ident[:, :], 0.0).then_inc(made, 1)
            pool.wait_ge(made, 1)
            pool.affine_select(out=ident[:, :], in_=ident[:, :], compare_op=ALU.not_equal, fill=1.0, base=0,
                               pattern=[[-1, ROUTED + 1]], channel_multiplier=1).then_inc(made, 1)
            pool.wait_ge(made, 2)
            pool.memset(zeros[:, :].bitcast(F32), 0.0).then_inc(made, 1)

            def split_low(slot, r):
                pool.wait_ge(w_hi, r + 1)
                pool.tensor_tensor(w_split[slot][1][:, :], w_raw[slot][:, :], w_split[slot][0][:, :].bitcast(F32),
                                   ALU.subtract).then_inc(w_lo, 1)

            split_low(0, 0)

            def group(g):
                def experts(j):
                    for q in range(SLOTS):
                        r = g * ROUTED + SLOTS * j + q
                        if q % 2 == 0:
                            pool.wait_ge(rows_loaded[q // 2], 16 * (g * per_slot + j + 1))
                        if not (is_first(g) and isinstance(j, int) and q < 2):
                            pool.wait_ge(weighted, NB * (r - 1))
                        split_low((q + 1) % SLOTS, r + 1)
                        pool.partition_broadcast(spread[q % 2][:, :], weight_rows[q // 2][:, q % 2, :], P).then_inc(spread_ready, 1)

                experts(0)
                with pool.Fori(1, per_slot) as j:
                    experts(j)

            over_groups(pool, group)

        @block.scalar
        def _(act):
            def split_high(slot, r, loads, steps):
                act.wait_ge(w_loaded[slot], 48 * loads)
                if steps is not None:
                    act.wait_ge(down_done, steps)
                act.activation(w_split[slot][0][:, :], w_raw[slot][:, :], ACT.Copy).then_inc(w_hi, 1)

            for r in range(SPLIT_AHEAD):
                split_high(r, r, 1, None)
            act.activation(gate[:, 1:2], gate[:, 0:1], ACT.Tanh).then_inc(gate_ready, 1)
            act.activation(down_bias[0][:, :], down_bias_raw[:, :], ACT.Copy).then_inc(const_hi, 1)
            act.wait_ge(bias_ready, 1)

            def half_step(g, e, k, bias):
                n = step_index(g, e, k)
                fresh = is_first(g) and isinstance(e, int) and e == 0
                act.wait_ge(gate_full, n + 1)
                if not fresh:
                    act.wait_ge(hidden_ready, n - 1)
                act.activation(act_gate[k][:, :], gu[k][0][:, :], ACT.Silu, bias=bias).then_inc(silu_done, 1)
                act.wait_ge(hidden_ready, n + 1)
                if not fresh:
                    act.wait_ge(down_done, n - 1)
                act.activation(hid[k][0][:, :], hidden[k][:, :], ACT.Copy).then_inc(hid_hi, 1)

            def group(g):
                for k in range(NB):
                    half_step(g, 0, k, bias_cols[0][:, ROUTED:])

                def experts(j):
                    act.wait_ge(silu_done, step_index(g, SLOTS * j + 1, 0))
                    act.activation(gate_bias[:, :], bias_cols[0][:, bass.ds(SLOTS * j, SLOTS)], ACT.Copy).then_inc(gate_bias_ready, 1)
                    act.wait_ge(gate_bias_ready, g * per_slot + j + 1)
                    for q in range(SLOTS):
                        e = SLOTS * j + q
                        half_step(g, e + 1, 0, gate_bias[:, q:q + 1])
                        ahead = q + SPLIT_AHEAD
                        if isinstance(j, int) and ahead < SLOTS:
                            steps = None if is_first(g) else g * STEPS
                        else:
                            steps = step_index(g, e, 0)
                        split_high(ahead % SLOTS, g * ROUTED + e + SPLIT_AHEAD, g * per_slot + j + ahead // SLOTS + 1, steps)
                        half_step(g, e + 1, 1, gate_bias[:, q:q + 1])
                        if isinstance(j, int) and q == 0:
                            act.wait_ge(weightT_loaded, 16 * (g + 1))
                            if not is_first(g):
                                act.wait_ge(acc_full, g)
                            act.activation(weightT_split[0][0:ROUTED, :], weightT[:, :], ACT.Copy).then_inc(weightT_hi, 1)

                experts(0)
                with act.Fori(1, per_slot) as j:
                    experts(j)

            over_groups(act, group)

        @block.vector
        def _(dve):
            def route(g, part):
                logits = routing[:, :, 0, :]
                if part == 0:
                    if not (isinstance(g, int) and g == 0):
                        dve.wait_ge(routing_loaded, 16 * g)
                    dve.tensor_scalar(divisor[:, :, :], routing[:, :, 1, :], 1.0, None, ALU.add).then_inc(divisor_ready, 1)
                    for t in range(GTILES):
                        last = dve.max(top[:, t, :], logits[:, t, :])
                    last.then_inc(top_ready, 1)
                elif part == 1:
                    dve.wait_ge(top_ready, g + 1)
                    dve.wait_ge(divisor_ready, g + 1)
                    dve.reciprocal(affinity[:, :, :], divisor[:, :, :]).then_inc(affinity_ready, 1)
                    for t in range(GTILES):
                        last = dve.match_replace(without_top[:, t, :], top[:, t, :], logits[:, t, :], LOWEST)
                    last.then_inc(removed, 1)
                elif part == 2:
                    dve.wait_ge(removed, g + 1)
                    dve.tensor_tensor(chosen[:, :, :], logits, without_top[:, :, :], ALU.not_equal).then_inc(chosen_ready, 1)
                elif part == 3:
                    dve.wait_ge(chosen_ready, g + 1)
                    dve.wait_ge(affinity_ready, g + 1)
                    dve.tensor_tensor(chosen[:, :, :], chosen[:, :, :], affinity[:, :, :], ALU.mult).then_inc(picked, 1)
                elif part == 4:
                    dve.wait_ge(picked, g + 1)
                    dve.tensor_reduce(total[:, :], chosen[:, :, :], AX.X, ALU.add).then_inc(total_ready, 1)
                elif part == 5:
                    dve.wait_ge(total_ready, g + 1)
                    dve.tensor_scalar(total[:, :], total[:, :], 1e-9, None, ALU.add).then_inc(total_safe, 1)
                    dve.wait_ge(total_safe, g + 1)
                    dve.reciprocal(total_inv[:, :], total[:, :]).then_inc(inv_ready, 1)
                elif part == 6:
                    dve.wait_ge(inv_ready, g + 1)
                    dve.tensor_tensor(weight[:, :, :], chosen[:, :, :], total_inv[:, :].unsqueeze(2).broadcast_to([P, GTILES, ROUTED]),
                                      ALU.mult).then_inc(weight_ready, 1)
                else:
                    dve.wait_ge(weight_ready, g + 1)
                    if not (isinstance(g, int) and g == 0):
                        dve.wait_ge(weightT_stored, 64 * g)
                    dve.transpose(weight_blocks[:, :, :].rearrange("p t e -> p (t e)"),
                                  weight[:, :, :].rearrange("p t e -> p (t e)")).then_inc(blocks_turned, 1)

            for part in range(2):
                route(0, part)
            dve.wait_ge(bias_turned, 1)
            for i in range(2):
                last = dve.tensor_copy(bias_cols[i][:, :], gu[1][i][:, 0:ROUTED + 1])
            last.then_inc(bias_ready, 1)
            for part in range(2, 8):
                route(0, part)
            dve.wait_ge(bias_ready, 1)
            dve.wait_ge(gate_ready, 1)

            def half_step(g, e, k, bias, row=None, routed=None):
                n = step_index(g, e, k)
                dve.wait_ge(silu_done, n + 1)
                if row is not None:
                    if k == 0:
                        dve.wait_ge(spread_ready, routed + 1)
                    dve.tensor_tensor(act_gate[k][:, :], act_gate[k][:, :], row[:, k * BLK:(k + 1) * BLK],
                                      ALU.mult).then_inc(weighted, 1)
                    dve.wait_ge(weighted, NB * routed + k + 1)
                dve.wait_ge(up_full, n + 1)
                if not (is_first(g) and isinstance(e, int) and e == 0):
                    dve.wait_ge(hid_lo, n - 1)
                dve.scalar_tensor_tensor(out=hidden[k][:, :], in0=gu[k][1][:, :], scalar=bias, in1=act_gate[k][:, :],
                                         op0=ALU.add, op1=ALU.mult).then_inc(hidden_ready, 1)
                dve.wait_ge(hid_hi, n + 1)
                dve.tensor_tensor(hid[k][1][:, :], hidden[k][:, :], hid[k][0][:, :].bitcast(F32), ALU.subtract).then_inc(hid_lo, 1)

            def group(g):
                for k in range(NB):
                    half_step(g, 0, k, bias_cols[1][:, ROUTED:])
                if isinstance(g, int) and g == 0:
                    dve.memset(weightT_split[0][ROUTED:, :].bitcast(F32), 1.0)
                    dve.memset(weightT_split[1][ROUTED:, :].bitcast(F32), 0.0)
                    dve.wait_ge(const_hi, 1)
                    dve.tensor_tensor(down_bias[1][:, :], down_bias_raw[:, :], down_bias[0][:, :].bitcast(F32), ALU.subtract).then_inc(const_lo, 1)

                def experts(j):
                    for q in range(SLOTS):
                        e = SLOTS * j + q
                        for k in range(NB):
                            half_step(g, e + 1, k, bias_cols[1][:, bass.ds(e, 1)], spread[q % 2], g * ROUTED + e)
                            if isinstance(j, int) and not is_last(g):
                                route(g + 1, NB * q + k)
                            if isinstance(j, int) and q == 1 and k == 0:
                                dve.wait_ge(weightT_hi, g + 1)
                                dve.tensor_tensor(weightT_split[1][0:ROUTED, :], weightT[:, :], weightT_split[0][0:ROUTED, :].bitcast(F32),
                                                  ALU.subtract).then_inc(weightT_lo, 1)

                experts(0)
                with dve.Fori(1, per_slot) as j:
                    experts(j)
                dve.wait_ge(acc_full, g + 1)
                dve.wait_ge(x1_loaded, 16 * (g + 1))
                for i in range(4):
                    rows = x1[:, 2 * i:2 * i + 2, :]
                    dve.scalar_tensor_tensor(out=rows, in0=acc[:, i, :, :], scalar=gate[:, 1:2], in1=rows,
                                             op0=ALU.mult, op1=ALU.add).then_inc(out_ready, 1)

            over_groups(dve, group)

        @block.tensor
        def _(pe):
            pe.wait_ge(made, 2)
            for i in range(2):
                last = pe.transpose(gu[1][i][:, 0:ROUTED + 1], bias_rows[i][:, :], ident[:, :])
            last.then_inc(bias_turned, 1)

            def gate_up(g, e, k, slot):
                w = w_split[slot]
                for part, done in ((0, gate_full), (1, up_full)):
                    for c in range(DC):
                        col = (part * DC + c) * I
                        last = split_product(pe, gu[k][part][:, :], [t[:, col:col + I] for t in w],
                                             [t[:, c, k * BLK:(k + 1) * BLK] for t in xT], start=c == 0, stop=c == DC - 1)
                    last.then_inc(done, 1)

            def down(g, e, k, slot, start=False):
                n = step_index(g, e, k)
                pe.wait_ge(hid_lo, n + 1)
                for t in range(BLK // P):
                    bank = acc[:, 2 * k + t // 2, :, :]
                    if start and t % 2 == 0:
                        pe.matmul(bank.rearrange("p t d -> p (t d)"), zeros[:, 0:P], zeros[:, :], start=True, stop=False)
                    last = split_product(pe, bank[:, t % 2, :], [h[:, t * P:(t + 1) * P] for h in hid[k]],
                                         [w[:, 2 * DC * I:] for w in w_split[slot]], start=False, stop=False)
                last.then_inc(down_done, 1)

            def group(g):
                for k in range(NB):
                    if not is_first(g):
                        pe.wait_ge(xT_loaded[k], 32 * g)
                        pe.wait_ge(hidden_ready, step_index(g, 0, k) - 1)
                    elif k == 1:
                        pe.wait_ge(bias_ready, 1)
                    gate_up(g, 0, k, SLOTS)
                if not is_first(g):
                    pe.wait_ge(out_ready, 4 * g)
                else:
                    pe.wait_ge(made, 3)
                down(g, 0, 0, SLOTS, start=True)

                def experts(j):
                    for q in range(SLOTS):
                        e = SLOTS * j + q
                        pe.wait_ge(w_lo, g * ROUTED + e + 1)
                        for k in range(NB):
                            pe.wait_ge(hidden_ready, step_index(g, e + 1, k) - 1)
                            gate_up(g, e + 1, k, q)
                            if k == 1:
                                down(g, e + 1, 0, q)
                            elif q == 0 and isinstance(j, int):
                                down(g, 0, 1, SLOTS, start=True)
                            else:
                                down(g, e, 1, (q - 1) % SLOTS)

                experts(0)
                with pe.Fori(1, per_slot) as j:
                    experts(j)
                down(g, ROUTED, 1, SLOTS - 1)
                if is_first(g):
                    pe.wait_ge(const_lo, 1)
                pe.wait_ge(weightT_lo, g + 1)
                for t in range(GTILES):
                    last = split_product(pe, acc[:, t // 2, t % 2, :], [w[:, t * P:(t + 1) * P] for w in weightT_split],
                                         [b[:, :] for b in down_bias], start=False, stop=t % 2 == 1)
                last.then_inc(acc_full, 1)

            over_groups(pe, group)


def layer(nc, dram):
    with ExitStack() as across:
        def sb(name, shape, dt=F32):
            return across.enter_context(nc.sbuf_tensor(name, shape, dt))

        wq = [sb(f"wq_{s}", [P, DC, INNER], F32R) for s in "hl"]
        wo = [sb(f"wo_{s}", [P, PAIRS, D], F32R) for s in "hl"]
        with ExitStack() as ctx:
            context_phase(nc, ctx, dram, wq, wo)
        ahead = {"xT": [sb(f"xT_{s}", [P, DC, GT], F32R) for s in "hl"],
                 "routing": sb("routing_in", [P, GTILES, 2, ROUTED]),
                 "shared": sb("shared", [P, EW]),
                 "gate": sb("gate_ffn", [P, 2]),
                 "gate_bias_rows": sb("gate_bias_rows", [ROUTED + 1, I]),
                 "up_bias_rows": sb("up_bias_rows", [ROUTED + 1, I]),
                 "down_bias_rows": sb("down_bias_rows", [ROUTED + 1, D]),
                 "shared_split": [sb(f"shared_{s}", [P, EW], F32R) for s in "hl"]}
        with ExitStack() as ctx:
            attention_phase(nc, ctx, dram, wq, wo, ahead)
        with ExitStack() as ctx:
            expert_phase(nc, ctx, dram, ahead)


INPUTS = {"x": "x", "ctx_2048": "ctx", "g_xattn": "g_xattn", "g_ffn": "g_ffn", "L0_xattn_Wq": "Wq", "L0_xattn_Wkv": "Wkv",
          "L0_xattn_null_kv": "null_kv", "L0_xattn_Wout": "Wout", "L0_xattn_ln_scale": "ln_scale", "L0_xattn_ln_bias": "ln_bias",
          **{f"L0_ffn_{n}": n for n in ("Wr", "br", "Wg_s", "bg_s", "Wu_s", "bu_s", "Wd_s", "bd_s", "Wg", "bg", "Wu", "bu", "Wd", "bd")}}


def kernel(**inputs):
    import numpy as np
    import concourse.bacc as bacc
    from concourse.bass_utils import run_bass_kernel_spmd

    nc = bacc.Bacc("TRN2", target_bir_lowering=False, num_devices=1)
    arrays, dram = {}, {}
    for given, name in INPUTS.items():
        arrays[f"in_{name}"] = np.ascontiguousarray(inputs[given])
        dram[name] = nc.dram_tensor(f"in_{name}", arrays[f"in_{name}"].shape, F32, kind="ExternalInput").ap()
    dram["out"] = nc.dram_tensor("out_dram", (B, N, D), F32, kind="ExternalOutput").ap()
    dram["keys"] = nc.dram_tensor("keys_dram", (B, P, PAIRS * M), F32, kind="Internal").ap()
    dram["values"] = nc.dram_tensor("values_dram", (B * M, INNER), F32, kind="Internal").ap()
    dram["x1"] = nc.dram_tensor("x1_dram", (T, D), F32, kind="Internal").ap()
    for part in "hl":
        dram[f"x2T_{part}"] = nc.dram_tensor(f"x2T_{part}_dram", (DC, P, T), F32, kind="Internal").ap()
    dram["routing"] = nc.dram_tensor("routing_dram", (T, 2 * ROUTED), F32, kind="Internal").ap()
    dram["weightT"] = nc.dram_tensor("weightT_dram", (ROUTED, T), F32, kind="Internal").ap()
    layer(nc, dram)
    return run_bass_kernel_spmd(nc, [arrays], core_ids=[0]).results[0]["out_dram"]
```
